# Optimizing a Trainium2 kernel written in Bass

```python
import numpy as np
import jax
import jax.numpy as jnp

def _softmax(x, axis=-1):
    return jax.nn.softmax(x, axis=axis)

def _gelu(x):
    return jax.nn.gelu(x, approximate=True)

def _silu(x):
    return jax.nn.silu(x)

def _sigmoid(x):
    return jax.nn.sigmoid(x)

def _layernorm(x, axis=-1, eps=1e-05):
    m = jnp.mean(x, axis=axis, keepdims=True)
    v = jnp.var(x, axis=axis, keepdims=True)
    return (x - m) / jnp.sqrt(v + eps)

def _scatter_add(tgt, idx, src, axis=0):
    return tgt.at[idx].add(src)

def _segment_sum(src, seg, n):
    return jax.ops.segment_sum(src, seg, n)
kernel_name = 'mk_decoder_postln_d1_seqx_r4_dd1956'

def setup_inputs(seed: int=0):
    np.random.seed(seed)
    _w = jnp.asarray

    def _rec_inputs():
        import jax
        import jax.numpy as jnp
        _rk = jax.random.key(seed)
        x = -0.0002928 + 1 * jax.random.normal(jax.random.fold_in(_rk, 1), (32, 100, 256), jnp.float32)
        _lenS = 100 - jax.random.randint(jax.random.fold_in(_rk, 7), (32,), 0, max(1, 100 // 4) + 1, jnp.int32)
        _lenS2 = 361 - jax.random.randint(jax.random.fold_in(_rk, 8), (32,), 0, max(1, 361 // 4) + 1, jnp.int32)
        _ctx_1024P = jax.random.normal(jax.random.fold_in(_rk, 11), (32, 16, 256), jnp.float32)
        _ctx_1024c = jax.random.dirichlet(jax.random.fold_in(_rk, 511), 0.3 * jnp.ones((16,), jnp.float32), (32, 361))
        _ctx_1024t = jnp.einsum('bsk,bkd->bsd', _ctx_1024c, _ctx_1024P)
        _ctx_1024t = _ctx_1024t * jax.lax.rsqrt(jnp.mean(jnp.square(_ctx_1024t)) + 1e-12) * 0.953939
        ctx_1024 = 4.13588e-05 + 0.999923 * (_ctx_1024t + 0.3 * jax.random.normal(jax.random.fold_in(_rk, 611), (32, 361, 256), jnp.float32))
        return (x, ctx_1024)
    x, ctx_1024 = _rec_inputs()

    def _L0_attn_setup():
        import jax, jax.numpy as jnp
        import numpy as np
        D_MODEL = 256
        N_HEADS = 16
        HEAD_DIM = D_MODEL // N_HEADS
        WINDOW = 128
        LOCAL_BLOCK = 64
        LATENT_TOKENS = 64
        LATENT_D = 64
        LATENT_HEADS = 4
        LATENT_HD = LATENT_D // LATENT_HEADS
        NEG = -1000000000.0

        def _local_attention(q, k, v):
            B, H, S, hd = q.shape
            bs = min(S, max(WINDOW, LOCAL_BLOCK))
            nb = S // bs
            w = WINDOW
            L = bs + w - 1
            k_pad = jnp.pad(k, ((0, 0), (0, 0), (w - 1, 0), (0, 0)))
            v_pad = jnp.pad(v, ((0, 0), (0, 0), (w - 1, 0), (0, 0)))
            starts = jnp.arange(nb) * bs
            idx = starts[:, None] + jnp.arange(L)[None, :]
            kb = k_pad[:, :, idx]
            vb = v_pad[:, :, idx]
            qb = q.reshape(B, H, nb, bs, hd)
            q_pos = starts[:, None] + jnp.arange(bs)[None, :]
            k_gpos = starts[:, None] + jnp.arange(L)[None, :] - (w - 1)
            dist = q_pos[:, :, None] - k_gpos[:, None, :]
            allowed = (dist > 0) & (dist <= w) & (k_gpos[:, None, :] >= 0)
            scale = 1.0 / np.sqrt(hd)
            scores = jnp.einsum('bhnqd,bhnkd->bhnqk', qb, kb) * scale
            scores = jnp.where(allowed, scores, NEG)
            attn = jax.nn.softmax(scores, axis=-1)
            attn = jnp.where(allowed.any(-1)[None, None, :, :, None], attn, 0.0)
            out = jnp.einsum('bhnqk,bhnkd->bhnqd', attn, vb)
            return out.reshape(B, H, S, hd)
        key = jax.random.key(seed)
        ks = jax.random.split(key, 14)
        B, S = (2, 1024)
        s = 0.02
        f32 = jnp.float32
        return {'x': jax.random.normal(ks[0], (B, S, D_MODEL), f32), 'qkv_w': jax.random.normal(ks[1], (D_MODEL, 3 * D_MODEL), f32) * s, 'qkv_b': jnp.zeros((3 * D_MODEL,), f32), 'rq_w': jax.random.normal(ks[2], (D_MODEL, LATENT_D), f32) * s, 'rq_b': jnp.zeros((LATENT_D,), f32), 'rkv_w': jax.random.normal(ks[3], (D_MODEL, 2 * LATENT_D), f32) * s, 'rkv_b': jnp.zeros((2 * LATENT_D,), f32), 'rout_w': jax.random.normal(ks[4], (LATENT_D, D_MODEL), f32) * s, 'rout_b': jnp.zeros((D_MODEL,), f32), 'out_w': jax.random.normal(ks[5], (D_MODEL, D_MODEL), f32) * s, 'out_b': jnp.zeros((D_MODEL,), f32), 'gl_w': jax.random.normal(ks[6], (HEAD_DIM, 1), f32) * s, 'gr_w': jax.random.normal(ks[7], (HEAD_DIM, 1), f32) * s}
    _L0_attn_all = _L0_attn_setup()
    _L0_attn_in = {k: v for k, v in _L0_attn_all.items() if k in ('qkv_w', 'qkv_b', 'rq_w', 'rq_b', 'rkv_w', 'rkv_b', 'rout_w', 'rout_b', 'out_w', 'out_b', 'gl_w', 'gr_w')}
    del _L0_attn_all

    def _L0_xattn_setup():
        import jax, jax.numpy as jnp
        import numpy as np
        E = 256
        KD = 256
        H = 16
        DH = E // H
        EPS = 1e-05

        def layernorm(x, gamma, beta):
            mu = jnp.mean(x, axis=-1, keepdims=True)
            var = jnp.mean(jnp.square(x - mu), axis=-1, keepdims=True)
            return (x - mu) * jax.lax.rsqrt(var + EPS) * gamma + beta
        key = jax.random.key(seed)
        ks = jax.random.split(key, 16)
        B, QN, KN = (4, 256, 512)
        s_q = 1.0 / np.sqrt(E)
        s_k = 1.0 / np.sqrt(KD)
        return {'q': jax.random.normal(ks[0], (B, QN, E), jnp.float32), 'k': jax.random.normal(ks[1], (B, KN, KD), jnp.float32), 'v': jax.random.normal(ks[2], (B, KN, KD), jnp.float32), 'Wq': jax.random.uniform(ks[3], (E, E), jnp.float32, -s_q, s_q), 'bq': jax.random.uniform(ks[4], (E,), jnp.float32, -s_q, s_q), 'Wk': jax.random.uniform(ks[5], (E, KD), jnp.float32, -s_k, s_k), 'bk': jax.random.uniform(ks[6], (E,), jnp.float32, -s_k, s_k), 'Wv': jax.random.uniform(ks[7], (E, KD), jnp.float32, -s_k, s_k), 'bv': jax.random.uniform(ks[8], (E,), jnp.float32, -s_k, s_k), 'Wp': jax.random.uniform(ks[9], (E, E), jnp.float32, -s_q, s_q), 'bp': jax.random.uniform(ks[10], (E,), jnp.float32, -s_q, s_q), 'q_gamma': jnp.ones((DH,), jnp.float32), 'q_beta': jnp.zeros((DH,), jnp.float32), 'k_gamma': jnp.ones((DH,), jnp.float32), 'k_beta': jnp.zeros((DH,), jnp.float32)}
    _L0_xattn_all = _L0_xattn_setup()
    _L0_xattn_in = {k: v for k, v in _L0_xattn_all.items() if k in ('Wq', 'bq', 'Wk', 'bk', 'Wv', 'bv', 'Wp', 'bp', 'q_gamma', 'q_beta', 'k_gamma', 'k_beta')}
    del _L0_xattn_all

    def _L0_ffn_setup():
        import jax, jax.numpy as jnp
        import numpy as np
        D_MODEL = 256
        EXPERT_DIM = 1024
        N_EXPERTS = 8
        CAP_FACTOR = 0.5
        key = jax.random.key(seed)
        ks = jax.random.split(key, 7)
        inp = {'input': jax.random.normal(ks[0], (4, 1024, D_MODEL), dtype=jnp.float32), 'w_switch': jax.random.normal(ks[1], (D_MODEL, N_EXPERTS), dtype=jnp.float32) * 0.02, 'b_switch': jnp.zeros((N_EXPERTS,), jnp.float32), 'w1': jax.random.normal(ks[2], (N_EXPERTS, D_MODEL, EXPERT_DIM), dtype=jnp.float32) * 0.02, 'b1': jnp.zeros((N_EXPERTS, EXPERT_DIM), jnp.float32), 'w2': jax.random.normal(ks[3], (N_EXPERTS, EXPERT_DIM, D_MODEL), dtype=jnp.float32) * 0.02, 'b2': jnp.zeros((N_EXPERTS, D_MODEL), jnp.float32)}
        return inp
    _L0_ffn_all = _L0_ffn_setup()
    _L0_ffn_in = {k: v for k, v in _L0_ffn_all.items() if k in ('w_switch', 'b_switch', 'w1', 'b1', 'w2', 'b2')}
    del _L0_ffn_all
    return {'x': x, 'ctx_1024': ctx_1024, 'L0_attn_qkv_w': _L0_attn_in['qkv_w'], 'L0_attn_qkv_b': _L0_attn_in['qkv_b'], 'L0_attn_rq_w': _L0_attn_in['rq_w'], 'L0_attn_rq_b': _L0_attn_in['rq_b'], 'L0_attn_rkv_w': _L0_attn_in['rkv_w'], 'L0_attn_rkv_b': _L0_attn_in['rkv_b'], 'L0_attn_rout_w': _L0_attn_in['rout_w'], 'L0_attn_rout_b': _L0_attn_in['rout_b'], 'L0_attn_out_w': _L0_attn_in['out_w'], 'L0_attn_out_b': _L0_attn_in['out_b'], 'L0_attn_gl_w': _L0_attn_in['gl_w'], 'L0_attn_gr_w': _L0_attn_in['gr_w'], 'L0_xattn_Wq': _L0_xattn_in['Wq'], 'L0_xattn_bq': _L0_xattn_in['bq'], 'L0_xattn_Wk': _L0_xattn_in['Wk'], 'L0_xattn_bk': _L0_xattn_in['bk'], 'L0_xattn_Wv': _L0_xattn_in['Wv'], 'L0_xattn_bv': _L0_xattn_in['bv'], 'L0_xattn_Wp': _L0_xattn_in['Wp'], 'L0_xattn_bp': _L0_xattn_in['bp'], 'L0_xattn_q_gamma': _L0_xattn_in['q_gamma'], 'L0_xattn_q_beta': _L0_xattn_in['q_beta'], 'L0_xattn_k_gamma': _L0_xattn_in['k_gamma'], 'L0_xattn_k_beta': _L0_xattn_in['k_beta'], 'L0_ffn_w_switch': _L0_ffn_in['w_switch'], 'L0_ffn_b_switch': _L0_ffn_in['b_switch'], 'L0_ffn_w1': _L0_ffn_in['w1'], 'L0_ffn_b1': _L0_ffn_in['b1'], 'L0_ffn_w2': _L0_ffn_in['w2'], 'L0_ffn_b2': _L0_ffn_in['b2']}

def reference(x, ctx_1024, L0_attn_qkv_w, L0_attn_qkv_b, L0_attn_rq_w, L0_attn_rq_b, L0_attn_rkv_w, L0_attn_rkv_b, L0_attn_rout_w, L0_attn_rout_b, L0_attn_out_w, L0_attn_out_b, L0_attn_gl_w, L0_attn_gr_w, L0_xattn_Wq, L0_xattn_bq, L0_xattn_Wk, L0_xattn_bk, L0_xattn_Wv, L0_xattn_bv, L0_xattn_Wp, L0_xattn_bp, L0_xattn_q_gamma, L0_xattn_q_beta, L0_xattn_k_gamma, L0_xattn_k_beta, L0_ffn_w_switch, L0_ffn_b_switch, L0_ffn_w1, L0_ffn_b1, L0_ffn_w2, L0_ffn_b2):
    import jax
    import jax.numpy as jnp

    def _L0_attn_ref(x, qkv_w, qkv_b, rq_w, rq_b, rkv_w, rkv_b, rout_w, rout_b, out_w, out_b, gl_w, gr_w):
        import jax, jax.numpy as jnp
        import numpy as np
        D_MODEL = 256
        N_HEADS = 16
        HEAD_DIM = D_MODEL // N_HEADS
        WINDOW = 128
        LOCAL_BLOCK = 64
        LATENT_TOKENS = 64
        LATENT_D = 64
        LATENT_HEADS = 4
        LATENT_HD = LATENT_D // LATENT_HEADS
        NEG = -1000000000.0

        def _local_attention(q, k, v):
            B, H, S, hd = q.shape
            bs = min(S, max(WINDOW, LOCAL_BLOCK))
            nb = S // bs
            w = WINDOW
            L = bs + w - 1
            k_pad = jnp.pad(k, ((0, 0), (0, 0), (w - 1, 0), (0, 0)))
            v_pad = jnp.pad(v, ((0, 0), (0, 0), (w - 1, 0), (0, 0)))
            starts = jnp.arange(nb) * bs
            idx = starts[:, None] + jnp.arange(L)[None, :]
            kb = k_pad[:, :, idx]
            vb = v_pad[:, :, idx]
            qb = q.reshape(B, H, nb, bs, hd)
            q_pos = starts[:, None] + jnp.arange(bs)[None, :]
            k_gpos = starts[:, None] + jnp.arange(L)[None, :] - (w - 1)
            dist = q_pos[:, :, None] - k_gpos[:, None, :]
            allowed = (dist > 0) & (dist <= w) & (k_gpos[:, None, :] >= 0)
            scale = 1.0 / np.sqrt(hd)
            scores = jnp.einsum('bhnqd,bhnkd->bhnqk', qb, kb) * scale
            scores = jnp.where(allowed, scores, NEG)
            attn = jax.nn.softmax(scores, axis=-1)
            attn = jnp.where(allowed.any(-1)[None, None, :, :, None], attn, 0.0)
            out = jnp.einsum('bhnqk,bhnkd->bhnqd', attn, vb)
            return out.reshape(B, H, S, hd)
        B, S, D = x.shape
        qkv = x @ qkv_w + qkv_b
        q, k, v = jnp.split(qkv, 3, axis=-1)

        def heads(t):
            return t.reshape(B, S, N_HEADS, HEAD_DIM).transpose(0, 2, 1, 3)
        local = _local_attention(heads(q), heads(k), heads(v))
        chunk = -(-S // min(LATENT_TOKENS, S))
        nlat = S // chunk
        pooled = x.reshape(B, nlat, chunk, D).mean(axis=2)
        chunk_ids = jnp.arange(S) // chunk
        rq = (x @ rq_w + rq_b).reshape(B, S, LATENT_HEADS, LATENT_HD).transpose(0, 2, 1, 3)
        rkv = pooled @ rkv_w + rkv_b
        rk, rv = jnp.split(rkv, 2, axis=-1)
        rk = rk.reshape(B, nlat, LATENT_HEADS, LATENT_HD).transpose(0, 2, 1, 3)
        rv = rv.reshape(B, nlat, LATENT_HEADS, LATENT_HD).transpose(0, 2, 1, 3)
        lscale = 1.0 / np.sqrt(LATENT_HD)
        lscores = jnp.einsum('bhsd,bhld->bhsl', rq, rk) * lscale
        lat_allowed = jnp.arange(nlat)[None, :] < chunk_ids[:, None]
        lscores = jnp.where(lat_allowed[None, None], lscores, NEG)
        lattn = jax.nn.softmax(lscores, axis=-1)
        lattn = jnp.where(lat_allowed.any(-1)[None, None, :, None], lattn, 0.0)
        lat_out = jnp.einsum('bhsl,bhld->bhsd', lattn, rv)
        lat_out = lat_out.transpose(0, 2, 1, 3).reshape(B, S, LATENT_D)
        remote = lat_out @ rout_w + rout_b
        remote_h = remote.reshape(B, S, N_HEADS, HEAD_DIM).transpose(0, 2, 1, 3)
        gate = jax.nn.sigmoid(local @ gl_w + remote_h @ gr_w)
        mixed = gate * local + (1.0 - gate) * remote_h
        mixed = mixed.transpose(0, 2, 1, 3).reshape(B, S, D)
        return mixed @ out_w + out_b

    def _L0_xattn_ref(q, k, v, Wq, bq, Wk, bk, Wv, bv, Wp, bp, q_gamma, q_beta, k_gamma, k_beta):
        import jax, jax.numpy as jnp
        import numpy as np
        E = 256
        KD = 256
        H = 16
        DH = E // H
        EPS = 1e-05

        def layernorm(x, gamma, beta):
            mu = jnp.mean(x, axis=-1, keepdims=True)
            var = jnp.mean(jnp.square(x - mu), axis=-1, keepdims=True)
            return (x - mu) * jax.lax.rsqrt(var + EPS) * gamma + beta
        B, QN, _ = q.shape
        KN = k.shape[1]
        scale = DH ** (-0.5)
        qh = (q @ Wq.T + bq).reshape(B, QN, H, DH).transpose(0, 2, 1, 3)
        kh = (k @ Wk.T + bk).reshape(B, KN, H, DH).transpose(0, 2, 1, 3)
        vh = (v @ Wv.T + bv).reshape(B, KN, H, DH).transpose(0, 2, 1, 3)
        qh = layernorm(qh, q_gamma, q_beta) * scale
        kh = layernorm(kh, k_gamma, k_beta)
        attn = jax.nn.softmax(jnp.einsum('bhqd,bhkd->bhqk', qh, kh), axis=-1)
        x = jnp.einsum('bhqk,bhkd->bhqd', attn, vh)
        x = x.transpose(0, 2, 1, 3).reshape(B, QN, E)
        return x @ Wp.T + bp

    def _L0_ffn_ref(input, w_switch, b_switch, w1, b1, w2, b2):
        import jax, jax.numpy as jnp
        import numpy as np
        D_MODEL = 256
        EXPERT_DIM = 1024
        N_EXPERTS = 8
        CAP_FACTOR = 0.5
        B, S, D = input.shape
        T = B * S
        E = b_switch.shape[0]
        capacity = int(CAP_FACTOR * T / E)
        x = input.reshape(T, D)
        logits = x @ w_switch + b_switch
        probs = jax.nn.softmax(logits, axis=-1)
        pmax = probs.max(axis=-1)
        routes = probs.argmax(axis=-1)
        oh = (routes[:, None] == jnp.arange(E)[None, :]).astype(jnp.int32)
        pos = (jnp.cumsum(oh, axis=0) * oh).sum(-1) - 1
        keep = pos < capacity
        slot = jnp.where(keep, routes * capacity + pos, E * capacity)
        buf = jnp.zeros((E * capacity + 1, D), x.dtype).at[slot].set(x)
        buf_e = buf[:E * capacity].reshape(E, capacity, D)
        h = jax.nn.relu(jnp.einsum('ecd,edh->ech', buf_e, w1) + b1[:, None, :])
        y = jnp.einsum('ech,ehd->ecd', h, w2) + b2[:, None, :]
        y_flat = jnp.concatenate([y.reshape(E * capacity, D), jnp.zeros((1, D), x.dtype)], axis=0)
        out = jnp.where(keep[:, None], y_flat[slot], x)
        scale = pmax / jax.lax.stop_gradient(pmax)
        out = out * scale[:, None]
        return out.reshape(B, S, D)
    x = _layernorm(x + _L0_attn_ref(x, L0_attn_qkv_w, L0_attn_qkv_b, L0_attn_rq_w, L0_attn_rq_b, L0_attn_rkv_w, L0_attn_rkv_b, L0_attn_rout_w, L0_attn_rout_b, L0_attn_out_w, L0_attn_out_b, L0_attn_gl_w, L0_attn_gr_w), axis=-1)
    x = _layernorm(x + _L0_xattn_ref(x, ctx_1024, ctx_1024, L0_xattn_Wq, L0_xattn_bq, L0_xattn_Wk, L0_xattn_bk, L0_xattn_Wv, L0_xattn_bv, L0_xattn_Wp, L0_xattn_bp, L0_xattn_q_gamma, L0_xattn_q_beta, L0_xattn_k_gamma, L0_xattn_k_beta), axis=-1)
    x = _layernorm(x + _L0_ffn_ref(x, L0_ffn_w_switch, L0_ffn_b_switch, L0_ffn_w1, L0_ffn_b1, L0_ffn_w2, L0_ffn_b2), axis=-1)
    return x

_drawn_inputs = setup_inputs


def setup_inputs(seed=0):
    import zlib

    import numpy as np

    out = dict(_drawn_inputs(seed))
    spreads = {'L0_attn_qkv_b': (0.0, 0.342),
     'L0_attn_rq_b': (0.0, 0.8),
     'L0_attn_rkv_b': (0.0, 0.8),
     'L0_attn_rout_b': (0.0, 0.1),
     'L0_attn_out_b': (0.0, 0.1),
     'L0_xattn_q_gamma': (1.0, 0.6),
     'L0_xattn_q_beta': (0.0, 0.488),
     'L0_xattn_k_gamma': (1.0, 0.6),
     'L0_xattn_k_beta': (0.0, 0.8),
     'L0_ffn_b_switch': (0.0, 0.1),
     'L0_ffn_b1': (0.0, 0.1),
     'L0_ffn_b2': (0.0, 0.1)}
    factors = {'L0_attn_qkv_w': 3.179,
     'L0_attn_rq_w': 8.0,
     'L0_attn_rkv_w': 8.0,
     'L0_attn_rout_w': 7.402,
     'L0_attn_gl_w': 8.0,
     'L0_attn_gr_w': 8.0,
     'L0_xattn_bq': 3.929,
     'L0_xattn_bk': 8.0}
    for name, (base, spread) in spreads.items():
        noise = np.random.default_rng([zlib.crc32(name.encode()), seed]).standard_normal(out[name].shape)
        drawn = base * np.exp(spread * noise) if base else spread * noise
        out[name] = jnp.asarray(drawn.astype(out[name].dtype))
    for name, factor in factors.items():
        out[name] = (out[name] * factor).astype(out[name].dtype)
    return out
```

```python
from contextlib import ExitStack

import numpy as np

import concourse.bass as bass
from concourse import mybir

ALU = mybir.AluOpType
ACT = mybir.ActivationFunctionType
X = mybir.AxisListType.X
F32, BF16, F16, U32 = mybir.dt.float32, mybir.dt.bfloat16, mybir.dt.float16, mybir.dt.uint32

B, S, D = 32, 100, 256
M = 361
H, HD = 16, 16
NL, LH = 50, 4
E, F, CAP = 8, 1024, 200
KN = [121, 121, 119]
KO = [0, 121, 242]
NEG = -1.0e30
EPS = 1e-5
SCALE = HD ** -0.5
SP1 = HD + 1

FIRST, LAST = -1, B
OFFSET = {"T": -1, "X": 0, "K": 1, "A": 1, "B": 1}

MISC = ["T1", "A1", "K1", "A2", "K2", "T2", "K3", "A4", "K4", "T3", "K5", "A6", "K6", "T4", "X1",
        "B1", "B2", "T5", "B3", "T6", "B4", "B5", "B6", "B7"]
MAXIMA = ["X0", "X1", "X2", "X3", "X4", "X5", "As0", "As1"] + [f"X{n}" for n in range(6, 16)]
SCORES = ["As0", "As1", "As2"] + [f"X{n}" for n in range(8)]


class It:

    def __init__(self, n, j=None):
        self.n, self.j = n, j

    def value(self, here, per_iteration):
        return max(here, 0) if self.j is None else self.j * (2 * per_iteration) + here

    def has(self, stage):
        return 0 <= self.n + OFFSET[stage] < B

    def of(self, stage):
        return Seq(self.n + OFFSET[stage], self.j)


class Seq:

    def __init__(self, n, j=None):
        self.n, self.j, self.parity = n, j, n % 2

    def done(self, per=1, k=None, back=0):
        here = (self.n - back) * per + (per if k is None else k)
        return max(here, 0) if self.j is None else self.j * (2 * per) + here

    def pairs(self, per, k=None, back=0):
        here = (self.n // 2 - back) * per + (per if k is None else k)
        return max(here, 0) if self.j is None else self.j * per + here

    def index(self):
        return self.n if self.j is None else self.j * 2 + self.n


def held(eng, value):
    return value if isinstance(value, int) else eng.to_reg(value)


def count(units, name, it):
    before = sum(OFFSET[u[0]] + i in range(B) for i in range(FIRST, it.n) for u in units)
    here = [u for u in units if it.has(u[0])]
    return before + here.index(name) + 1


def iterations(eng, body):
    for n in range(FIRST, 3):
        body(It(n))
    with eng.Fori(0, (B - 4) // 2) as j:
        body(It(3, j))
        body(It(4, j))
    body(It(B - 1))
    body(It(B))


def rounds(eng, body):
    body(0)
    with eng.Fori(1, B // 4) as j:
        body(j)


def decoder_kernel(nc, io):
    ctx = ExitStack()
    with ctx:
        def sb(name, shape, dt=F32):
            return ctx.enter_context(nc.sbuf_tensor(name, shape, dt))

        def sem(name):
            return ctx.enter_context(nc.semaphore(name))

        MI = [ctx.enter_context(nc.psum_tensor(f"MI{n}", [128, 512], F32)) for n in range(2)]
        MX = ctx.enter_context(nc.psum_tensor("MX", [128, 2, 512], F32))
        ST = ctx.enter_context(nc.psum_tensor("ST", [128, 4, 512], F32))

        early = sb("early", [128, 5 * 2 * M])
        wide = sb("wide", [128, 4800])

        def part(region, at, shape):
            n = int(np.prod(shape[1:]))
            ap = region[0:shape[0], at:at + n]
            names = "abcde"[:len(shape) - 1]
            sizes = dict(zip(names, shape[1:]))
            return ap.rearrange(f"p ({' '.join(names)}) -> p {' '.join(names)}", **sizes)

        ident = sb("ident", [128, 128])
        identb = sb("identb", [128, 128], BF16)
        center = sb("center", [128, 128])
        average = sb("average", [128, 128])
        upto = sb("upto", [S, S])
        ones = sb("ones", [S, S])
        select_f = part(early, 0, [128, 6, 128])
        select = sb("select", [128, 6, 128], BF16)
        mask_q_f = part(early, 768, [S, 500])
        mask_q = sb("mask_q", [S, 500], BF16)
        mask_k_f = part(early, 1268, [S, 400])
        mask_k = sb("mask_k", [S, 400], BF16)
        mask_l_f = part(early, 1668, [NL, 200])
        mask_l = sb("mask_l", [NL, 200], BF16)
        some_key = sb("some_key", [S, H + LH])
        expert_id = sb("expert_id", [S, E])
        own_row = sb("own_row", [S, B])
        parity = sb("parity", [128, 2])
        eps = sb("eps", [128, 1])
        zero1 = sb("zero1", [128, 1])

        wqkv = sb("wqkv", [128, 2, 3 * D])
        bqk = sb("bqk", [128, 4])
        bv_self = sb("bv_self", [S, D])
        rqw = sb("rqw", [128, 2, 64])
        rqb = sb("rqb", [64, 1])
        rkvw = sb("rkvw", [128, 2, 128])
        rkvh = sb("rkvh", [128, 2, 128])
        rkb = sb("rkb", [64, 1])
        rvb = sb("rvb", [NL, 64])
        routw = sb("routw", [64, D])
        routb = sb("routb", [S, D])
        outw = sb("outw", [128, 2, D])
        outb = sb("outb", [S, D])
        glb = sb("glb", [S, D])
        grb = sb("grb", [S, D])
        Wq = part(early, 1868, [128, 2, D])
        Wk = part(early, 2380, [128, 2, D])
        WqC = sb("WqC", [128, 2, D])
        WkC = sb("WkC", [128, 2, D])
        bq2 = sb("bq2", [128, 2])
        bk2 = sb("bk2", [128, 2])
        bqC = sb("bqC", [128, 2])
        bkC = sb("bkC", [128, 2])
        WvT = sb("WvT", [128, 2, D])
        WpT = sb("WpT", [128, 2, D])
        bv_cross = sb("bv_cross", [S, D])
        bp = sb("bp", [S, D])
        norm4 = sb("norm4", [128, 4])
        parity_s = sb("parity_s", [128, 2])
        gq2 = sb("gq2", [128, 2])
        bq2n = sb("bq2n", [128, 2])
        wsw = sb("wsw", [128, 2, E])
        bsw = sb("bsw", [S, E])

        xT = [sb(f"xT{p}", [128, 2, S]) for p in range(2)]
        xn = [sb(f"xn{p}", [S, D]) for p in range(2)]
        pairsum = sb("pairsum", [128, 2, NL])
        Qs = sb("Qs", [128, 2, 2, S])
        Qsb = sb("Qsb", [128, 2, 2, S], BF16)
        Ks = sb("Ks", [128, 2, S])
        Ksb = sb("Ksb", [128, 2, S], BF16)
        Vs = sb("Vs", [S, H, SP1])
        Ql = sb("Ql", [64, 2, S])
        Qlb = sb("Qlb", [64, 2, S], BF16)
        Kl = sb("Kl", [64, NL])
        Klb = sb("Klb", [64, NL], BF16)
        Vl = sb("Vl", [NL, LH, SP1])
        negmax_s = sb("negmax_s", [S, 128], BF16)
        shift_s = sb("shift_s", [128, S], BF16)
        Ps = sb("Ps", [S, 4, 2, 2, S])
        Pl = sb("Pl", [NL, 2, 2, S])
        recip_s = sb("recip_s", [S, H + LH])
        recip_m = sb("recip_m", [S, H + LH])
        Os = sb("Os", [S, H + LH, HD])

        latT = sb("latT", [64, S])
        rem = sb("rem", [S, D])
        gate_l = sb("gate_l", [S, D])
        gate_r = sb("gate_r", [S, D])
        gate_t = sb("gate_t", [S, D])
        differ = sb("differ", [S, D])
        gate_z = sb("gate_z", [S, H])
        gate_e = sb("gate_e", [S, H])
        gate_d = sb("gate_d", [S, H])
        gate = sb("gate", [S, H])
        gated = sb("gated", [S, D])
        mixed = sb("mixed", [S, D])
        mixT = sb("mixT", [128, 2, S])
        xob = sb("xob", [S, D])
        res1 = sb("res1", [S, D])
        bn1 = sb("bn1", [S, 6])
        mv1 = sb("mv1", [S, 2])
        ln1 = sb("ln1", [S, 1])
        rs1 = sb("rs1", [S, 1])
        x1 = sb("x1", [S, D])
        x1bp = [sb(f"x1bp{p}", [S, D]) for p in range(2)]
        x1T = sb("x1T", [128, 2, S])
        qc = sb("qc", [128, 2, S])
        sqq = sb("sqq", [128, 2, S])
        lnq = sb("lnq", [128, 2, S])
        rsq = sb("rsq", [128, 2, S])
        qn = sb("qn", [128, 2, S])
        Qx = sb("Qx", [128, 2, 2, S])
        Qh = [sb(f"Qh{p}", [128, 2, 2, S], F16) for p in range(2)]
        Qlo = [sb(f"Qlo{p}", [128, 2, 2, S], F16) for p in range(2)]

        cT = [sb(f"cT{p}", [128, 2, M]) for p in range(2)]
        kc = part(early, 0 * 2 * M, [128, 2, M])
        sqk = part(early, 1 * 2 * M, [128, 2, M])
        lnk = part(early, 2 * 2 * M, [128, 2, M])
        rsk = part(early, 3 * 2 * M, [128, 2, M])
        kn = part(early, 4 * 2 * M, [128, 2, M])
        Kh = [sb(f"Kh{p}", [128, 2, M], F16) for p in range(2)]
        Klo = [sb(f"Klo{p}", [128, 2, M], F16) for p in range(2)]
        Vx = [sb(f"Vx{p}", [KN[0], 3, H, SP1]) for p in range(2)]

        negmax_x = sb("negmax_x", [S, 128], BF16)
        shift_x = sb("shift_x", [128, S], BF16)
        Px = part(wide, 0, [KN[0], 4, 2, 3, 2, S])
        recip_x = sb("recip_x", [S, H])
        Ox = sb("Ox", [S, H, HD])
        Oxb = sb("Oxb", [S, D])
        OxT = sb("OxT", [128, 2, S])
        res2 = sb("res2", [S, D])
        bn2 = sb("bn2", [S, 6])
        mv2 = sb("mv2", [S, 2])
        ln2 = sb("ln2", [S, 1])
        rs2 = sb("rs2", [S, 1])
        x2 = [sb(f"x2{p}", [S, D]) for p in range(2)]
        x2T = sb("x2T", [128, 2, S])
        x2_all = sb("x2_all", [S, B, D])
        logits = sb("logits", [S, E])
        top8 = sb("top8", [S, 8])
        negtop = sb("negtop", [S, 1])
        index8 = sb("index8", [S, 8], U32)
        route = sb("route", [S, 1])
        onehot = sb("onehot", [S, E])
        exps8 = sb("exps8", [S, E])
        sum8 = sb("sum8", [S, B])
        carry = [sb(f"carry{p}", [S, E]) for p in range(2)]
        place = sb("place", [S, E])
        place1 = sb("place1", [S, E])
        pos = sb("pos", [S, 1])
        keep = sb("keep", [S, 1])
        slot0 = sb("slot0", [S, 1])
        slot1 = sb("slot1", [S, 1])
        slot2 = sb("slot2", [S, 1])
        slot = [sb(f"slot{p}u", [S, 1], U32) for p in range(2)]
        slot_all = sb("slot_all", [S, B], U32)

        W1 = [sb(f"W1{p}", [128, 2, F]) for p in range(2)]
        W2 = [sb(f"W2{p}", [128, 8, D]) for p in range(2)]
        b1 = [sb(f"b1{p}", [128, 8]) for p in range(2)]
        b2 = [sb(f"b2{p}", [S, D]) for p in range(2)]
        Xe = [part(wide, 2000 + 512 * p, [S, 2, D]) for p in range(2)]
        XeT = part(wide, 1600, [128, 2, CAP])
        hT = part(wide, 0, [128, 8, CAP])
        Y = [part(wide, 3024 + 512 * p, [S, 2, D]) for p in range(2)]
        pmax = sb("pmax", [S, B])
        pinv = sb("pinv", [S, B])
        pone = sb("pone", [S, B])
        slot_g = [sb(f"slot_g{c}", [S, 1], U32) for c in range(4)]
        G = [part(early, (0 + c) * D, [S, D]) for c in range(4)]
        R = [part(early, (4 + c) * D, [S, D]) for c in range(4)]
        bn3 = sb("bn3", [S, 4, 6])
        mv3 = sb("mv3", [S, 4, 2])
        ln3 = sb("ln3", [S, 4])
        rs3 = sb("rs3", [S, 4])
        O3 = [part(early, (8 + c) * D, [S, D]) for c in range(4)]

        slots = nc.dram_tensor("slots", (E * CAP + B * S, D), F32, kind="Internal").ap()

        loaded_const = sem("loaded_const")
        cast_const = sem("cast_const")
        started = sem("started")
        zeroed = sem("zeroed")
        weights_mm = sem("weights_mm")
        weights_ok = sem("weights_ok")
        loaded_x = [sem(f"loaded_x{p}") for p in range(2)]
        loaded_c = [sem(f"loaded_c{p}") for p in range(2)]
        filled = {s: sem(f"filled_{s}") for s in MISC}
        emptied = [sem(f"emptied_MI{n}") for n in range(2)]
        max_full = sem("max_full")
        max_read = sem("max_read")
        st_full = sem("st_full")
        st_exp = sem("st_exp")
        a_pool = sem("a_pool")
        a_cast = sem("a_cast")
        a_dve = sem("a_dve")
        b_pool = sem("b_pool")
        b_mixed = sem("b_mixed")
        b_z = sem("b_z")
        b_e = sem("b_e")
        b_ln = sem("b_ln")
        b_rs = sem("b_rs")
        b_x1bp = sem("b_x1bp")
        b_sq = sem("b_sq")
        b_rsq = sem("b_rsq")
        b_q = sem("b_q")
        b_qh = sem("b_qh")
        k_sq = sem("k_sq")
        k_rs = sem("k_rs")
        k_n = sem("k_n")
        k_hi = sem("k_hi")
        k_lo = sem("k_lo")
        t_dve = sem("t_dve")
        t_pool = sem("t_pool")
        t_ln = sem("t_ln")
        t_rs = sem("t_rs")
        t_keep = sem("t_keep")
        t_top = sem("t_top")
        t_exp = sem("t_exp")
        t_pos = sem("t_pos")
        scattered = sem("scattered")
        w_in = [sem(f"w_in{p}") for p in range(2)]
        xe_in = [sem(f"xe_in{p}") for p in range(2)]
        xe_mm = sem("xe_mm")
        xe_ok = sem("xe_ok")
        h_mm = sem("h_mm")
        h_act = sem("h_act")
        h_dve = sem("h_dve")
        y_mm = sem("y_mm")
        y_ok = sem("y_ok")
        y_out = [sem(f"y_out{p}") for p in range(2)]
        e_one = sem("e_one")
        g_idx = sem("g_idx")
        g_in = [sem(f"g_in{c}") for c in range(4)]
        e_sum = sem("e_sum")
        e_bn = sem("e_bn")
        e_mv = sem("e_mv")
        e_rs = sem("e_rs")
        e_out = sem("e_out")
        stored = [sem(f"stored{c}") for c in range(4)]

        block = ctx.enter_context(nc.Block())


        def bank(step, it):
            return (count(MISC, step, it) - 1) % 2

        def uses(step, it):
            return it.value((count(MISC, step, it) - 1) // 2 + 1, len(MISC) // 2)

        def uses_before(step, it):
            return it.value((count(MISC, step, it) - 1) // 2, len(MISC) // 2)

        def left(step, it):
            return emptied[bank(step, it)], uses(step, it)

        def in_order(units, name, it, back=0):
            return it.value(count(units, name, it) - back, len(units))

        def pair_of(name, it):
            return 2 * (count(SCORES, name, it) % 2)

        constants = [
            (ident, "ident"), (center, "center"), (average, "average"), (upto, "upto"),
            (select_f, "select"), (mask_q_f, "mask_q"), (mask_k_f, "mask_k"), (mask_l_f, "mask_l"),
            (some_key, "some_key"), (expert_id, "expert_id"), (own_row, "own_row"), (parity, "parity"),
            (wqkv, "qkv_w"), (bqk, "qk_b"), (rqw, "rq_w"), (rqb, "rq_b"), (rkvw, "rkv_w"),
            (rkb, "rk_b"), (routw, "rout_w"), (outw, "out_w"), (Wq, "Wq"), (Wk, "Wk"), (bq2, "bq"),
            (bk2, "bk"), (WvT, "WvT"), (WpT, "WpT"), (norm4, "norm4"), (wsw, "w_switch"),
        ]
        rows = [
            (bv_self, "v_b"), (rvb, "rv_b"), (routb, "rout_b"), (outb, "out_b"), (glb, "gl"),
            (grb, "gr"), (bv_cross, "bv"), (bp, "bp"), (bsw, "b_switch"),
        ]
        N_CONST = 16 * (len(constants) + len(rows))

        @block.sync
        def _(sp):
            for tile, name in constants:
                sp.dma_start(tile[:], io[name]).then_inc(loaded_const, 16)
            for tile, name in rows:
                n = tile.shape[0]
                sp.dma_start(tile[:], io[name].partition_broadcast(n)).then_inc(loaded_const, 16)

            def load(b):
                p, n = b.parity, b.index()
                after = held(sp, b.done(back=2))
                sp.wait_ge(started, 1)
                sp.wait_ge(filled["K6"], after)
                sp.dma_start(cT[p][:], io["cT"][:, :, bass.ds(n * M, M)]).then_inc(loaded_c[p], 16)
                after1 = held(sp, b.done(back=2))
                after2 = held(sp, b.done(per=5, back=2))
                sp.wait_ge(started, 1)
                sp.wait_ge(filled["A2"], after1)
                sp.wait_ge(b_pool, after2)
                sp.dma_start(xT[p][:], io["xT"][:, :, bass.ds(n * S, S)]).then_inc(loaded_x[p], 16)
                sp.dma_start(xn[p][:], io["x"][bass.ds(n * S, S), :]).then_inc(loaded_x[p], 16)

            load(Seq(0))
            load(Seq(1))
            with sp.Fori(0, (B - 2) // 2) as j:
                load(Seq(2, j))
                load(Seq(3, j))

            def load_weights(e):
                p, n = e.parity, e.index()
                after = held(sp, e.done(per=2, back=2))
                sp.wait_ge(started, 1)
                sp.wait_ge(y_ok, after)
                sp.dma_start(W1[p][:], io["w1"][bass.ds(n, 1)].rearrange("a (k p) f -> p (a k) f", p=128)).then_inc(w_in[p], 16)
                sp.dma_start(W2[p][:], io["w2"][bass.ds(n, 1)].rearrange("a (k p) f -> p (a k) f", p=128)).then_inc(w_in[p], 16)
                sp.dma_start(b1[p][:], io["b1"][bass.ds(n, 1)].rearrange("a p f -> p (a f)")).then_inc(w_in[p], 16)
                sp.dma_start(b2[p][:], io["b2"][bass.ds(n, 1)].rearrange("a f -> (a f)").partition_broadcast(S)).then_inc(w_in[p], 16)

            def load_rows(e):
                p, n = e.parity, e.index()
                after = held(sp, e.done(back=2))
                sp.wait_ge(started, 1)
                sp.wait_ge(xe_mm, after)
                sp.dma_start(Xe[p][:], slots[bass.ds(n * CAP, CAP), :].rearrange("(s p) d -> p s d", p=S)).then_inc(xe_in[p], 16)

            load_weights(Seq(0))
            load_weights(Seq(1))
            sp.wait_ge(scattered, 16 * B)
            load_rows(Seq(0))
            load_rows(Seq(1))
            with sp.Fori(0, (E - 2) // 2) as j:
                for n in (2, 3):
                    load_rows(Seq(n, j))
                    load_weights(Seq(n, j))

            def store(j):
                for c in range(4):
                    after = held(sp, j * 4 + (c + 1))
                    sp.wait_ge(started, 1)
                    sp.wait_ge(e_out, after)
                    sp.dma_start(io["out"][bass.ds((j * 4 + c) * S, S), :], O3[c][:]).then_inc(stored[c], 16)

            rounds(sp, store)
            for c in range(4):
                sp.wait_ge(stored[c], 16 * (B // 4))

        @block.gpsimd
        def _(pool):
            pool.memset(wide[:], 0.0).then_inc(cast_const, 1)
            pool.memset(eps[:], EPS).then_inc(cast_const, 1)
            pool.memset(zero1[:], 0.0).then_inc(started, 1)
            pool.memset(negmax_s[:], 0.0).then_inc(cast_const, 1)
            pool.memset(negmax_x[:], 0.0).then_inc(cast_const, 1)
            pool.memset(Vs[:], 1.0).then_inc(cast_const, 1)
            pool.memset(Vl[:], 1.0).then_inc(cast_const, 1)
            pool.memset(Vx[0][:], 1.0).then_inc(cast_const, 1)
            pool.memset(Vx[1][:], 1.0).then_inc(cast_const, 1)
            pool.memset(ones[:], 1.0).then_inc(cast_const, 1)
            pool.memset(carry[1][:], -1.0).then_inc(cast_const, 1)
            pool.wait_ge(cast_const, 1)
            for n in range(0, E * CAP + B * S, E * CAP):
                pool.dma_start(slots[n:n + E * CAP, :].rearrange("(p n) d -> p (n d)", p=S),
                               wide[0:S, 0:16 * D]).then_inc(zeroed, 16)
            pool.wait_ge(loaded_const, N_CONST)
            pool.tensor_copy(identb[:], ident[:]).then_inc(cast_const, 1)
            pool.tensor_copy(select[:], select_f[:]).then_inc(cast_const, 1)
            pool.tensor_copy(mask_q[:], mask_q_f[:]).then_inc(cast_const, 1)
            pool.tensor_copy(mask_k[:], mask_k_f[:]).then_inc(cast_const, 1)
            pool.tensor_copy(mask_l[:], mask_l_f[:]).then_inc(cast_const, 1)
            pool.tensor_scalar(rkvh[:], rkvw[:], 0.5, None, ALU.mult).then_inc(cast_const, 1)
            pool.tensor_scalar(parity_s[:], parity[:], SCALE, None, ALU.mult).then_inc(cast_const, 1)
            pool.wait_ge(cast_const, POOL_CONST - 2)
            pool.tensor_scalar(gq2[:], parity_s[:], norm4[:, 0:1], None, ALU.mult).then_inc(cast_const, 1)
            pool.tensor_scalar(bq2n[:], parity_s[:], norm4[:, 1:2], None, ALU.mult).then_inc(cast_const, 1)
            pool.wait_ge(zeroed, 48)

            def pair_sums(b):
                pool.wait_ge(loaded_x[b.parity], b.pairs(32))
                pool.wait_ge(filled["A2"], b.done(back=1))
                x = xT[b.parity][:].rearrange("p t (n a) -> p t n a", a=2)
                pool.tensor_tensor(pairsum[:], x[:, :, :, 0], x[:, :, :, 1], ALU.add).then_inc(a_pool, 1)

            def cast_self(b, it):
                after1 = held(pool, uses("A1", it))
                after2 = held(pool, in_order(MAXIMA, "As1", it, back=len(MAXIMA)) if it.n > -1 else 0)
                pool.wait_ge(started, 1)
                pool.wait_ge(emptied[bank("A1", it)], after1)
                pool.wait_ge(max_full, after2)
                pool.tensor_copy(Qsb[:], Qs[:]).then_inc(a_cast, 1)
                pool.tensor_copy(Ksb[:], Ks[:]).then_inc(a_cast, 1)

            def cast_latent(b, it):
                after = held(pool, uses("A2", it))
                pool.wait_ge(started, 1)
                pool.wait_ge(emptied[bank("A2", it)], after)
                pool.tensor_copy(Qlb[:], Ql[:]).then_inc(a_cast, 1)
                pool.tensor_copy(Klb[:], Kl[:]).then_inc(a_cast, 1)

            def square_k(b, it, t):
                pool.wait_ge(*left(f"K{t + 1}", it))
                pool.wait_ge(filled[f"K{t + 3}"], b.done(back=1))
                pool.tensor_tensor(sqk[:, t], kc[:, t], kc[:, t], ALU.mult).then_inc(k_sq, 1)

            def high_k(b, t):
                p = b.parity
                after1 = held(pool, b.done(per=2, k=t + 1))
                after2 = held(pool, b.done(back=2))
                pool.wait_ge(started, 1)
                pool.wait_ge(k_n, after1)
                pool.wait_ge(filled["T1"], after2)
                pool.tensor_scalar(Kh[p][:, t], kn[:, t], norm4[:, 3:4], None, ALU.add).then_inc(k_hi, 1)

            def gate_local(b, it):
                pool.wait_ge(*left("A6", it))
                pool.tensor_tensor(gate_l[:], Os[:, 0:H].rearrange("p h d -> p (h d)"), glb[:], ALU.mult).then_inc(b_pool, 1)
                pool.wait_ge(loaded_x[b.parity], b.pairs(32))
                pool.wait_ge(b_ln, b.done(per=3, back=1))
                pool.tensor_tensor(xob[:], xn[b.parity][:], outb[:], ALU.add).then_inc(b_pool, 1)

            def gate_remote(b, it):
                pool.wait_ge(*left("B2", it))
                pool.tensor_tensor(gate_r[:], rem[:], grb[:], ALU.mult).then_inc(b_pool, 1)
                pool.wait_ge(b_pool, b.done(per=5, k=3))
                pool.tensor_tensor(gate_t[:], gate_l[:], gate_r[:], ALU.add).then_inc(b_pool, 1)
                pool.tensor_tensor(differ[:], Os[:, 0:H].rearrange("p h d -> p (h d)"), rem[:], ALU.subtract).then_inc(b_pool, 1)

            def mix(b):
                pool.wait_ge(b_z, b.done(per=4))
                pool.wait_ge(filled["B3"], b.done(back=1))
                pool.tensor_tensor(mixed[:], gated[:], rem[:], ALU.add).then_inc(b_mixed, 1)

            def x1_bias(b):
                pool.wait_ge(b_ln, b.done(per=3))
                pool.wait_ge(t_ln, b.done(per=3, k=1, back=2))
                pool.tensor_tensor(x1bp[b.parity][:], x1[:], bp[:], ALU.add).then_inc(b_x1bp, 1)

            def square_q(b, it):
                pool.wait_ge(*left("B6", it))
                pool.tensor_tensor(sqq[:], qc[:], qc[:], ALU.mult).then_inc(b_sq, 1)

            def high_q(b):
                after = held(pool, b.done(per=3, k=2))
                pool.wait_ge(started, 1)
                pool.wait_ge(b_q, after)
                pool.tensor_copy(Qh[b.parity][:], Qx[:]).then_inc(b_qh, 1)

            def value_bias(b, it):
                pool.wait_ge(*left("T1", it))
                pool.wait_ge(filled["T2"], b.done(back=1))
                pool.tensor_tensor(Oxb[:], Ox[:].rearrange("p h d -> p (h d)"), bv_cross[:], ALU.add).then_inc(t_pool, 1)

            def keep_x2(b):
                after = held(pool, b.done(per=3))
                pool.wait_ge(started, 1)
                pool.wait_ge(t_ln, after)
                pool.tensor_copy(x2_all[:, bass.ds(b.index(), 1), :].rearrange("p a d -> p (a d)"), x2[b.parity][:]).then_inc(t_keep, 1)

            def scatter(b):
                p = b.parity
                after1 = held(pool, b.done(per=7))
                after2 = held(pool, b.done(per=16, back=1))
                pool.wait_ge(started, 1)
                pool.wait_ge(t_pos, after1)
                pool.wait_ge(scattered, after2)
                pool.indirect_dma_start(
                    out=slots[:, :], out_offset=bass.IndirectOffsetOnAxis(ap=slot[p][:, 0:1], axis=0),
                    in_=x2[p][:], in_offset=None).then_inc(scattered, 16)

            def body(it):
                K, A, Bs, T = it.of("K"), it.of("A"), it.of("B"), it.of("T")
                if it.has("T"):
                    value_bias(T, it)
                if it.has("A"):
                    pair_sums(A)
                    cast_self(A, it)
                    square_k(K, it, 0)
                    cast_latent(A, it)
                    square_k(K, it, 1)
                    high_k(K, 0)
                    high_k(K, 1)
                if it.has("T"):
                    keep_x2(T)
                if it.has("A"):
                    gate_local(Bs, it)
                    gate_remote(Bs, it)
                    mix(Bs)
                if it.has("T"):
                    scatter(T)
                if it.has("A"):
                    x1_bias(Bs)
                    square_q(Bs, it)
                    high_q(Bs)

            iterations(pool, body)

            def gather(j, c):
                pool.tensor_copy(slot_g[c][:], slot_all[:, bass.ds(j * 4 + c, 1)]).then_inc(g_idx, 1)
                after = held(pool, j * 4 + (c + 1))
                pool.wait_ge(started, 1)
                pool.wait_ge(g_idx, after)
                pool.indirect_dma_start(
                    out=G[c][:], out_offset=None, in_=slots[:, :],
                    in_offset=bass.IndirectOffsetOnAxis(ap=slot_g[c][:, 0:1], axis=0)).then_inc(g_in[c], 16)

            for p in range(2):
                pool.wait_ge(y_out[p], 16 * (E // 2))
            pool.wait_ge(t_pos, 7 * B)

            def gather_round(j):
                used, arrived = held(pool, j * 4), held(pool, j * 16)
                pool.wait_ge(started, 1)
                pool.wait_ge(e_sum, used)
                for c in range(4):
                    pool.wait_ge(g_in[c], arrived)
                for c in range(4):
                    gather(j, c)

            rounds(pool, gather_round)

        @block.tensor
        def _(pe):
            pe.wait_ge(loaded_const, N_CONST)
            for n, w in enumerate((Wk, Wq)):
                for k in range(2):
                    for t in range(2):
                        mm = pe.matmul(MX[:, n, (2 * k + t) * 128:(2 * k + t + 1) * 128],
                                       w[:, t, k * 128:(k + 1) * 128], center[:], start=True, stop=True)
            mm.then_inc(weights_mm, 1)
            pe.matmul(MI[0][:, 0:2], center[:], bk2[:], start=True, stop=True)
            pe.matmul(MI[0][:, 2:4], center[:], bq2[:], start=True, stop=True).then_inc(weights_mm, 1)
            pe.wait_ge(weights_ok, 4)
            pe.wait_ge(cast_const, POOL_CONST)

            def enter(step, it, source=None):
                pe.wait_ge(emptied[bank(step, it)], uses_before(step, it))
                if source and bank(source, it) != bank(step, it):
                    pe.wait_ge(*left(source, it))
                return MI[bank(step, it)]

            def two(out, lhs, rhs):
                pe.matmul(out, lhs(0), rhs(0), start=True, stop=False)
                return pe.matmul(out, lhs(1), rhs(1), start=False, stop=True)

            def A1(it):
                b = it.of("A")
                p, ps = b.parity, enter("A1", it)
                pe.wait_ge(loaded_x[p], b.pairs(32))
                for m in range(4):
                    mm = two(ps[:, m * S:(m + 1) * S], lambda k: wqkv[:, k, m * 128:(m + 1) * 128],
                             lambda k: xT[p][:, k])
                mm.then_inc(filled["A1"], 1)

            def A2(it):
                b = it.of("A")
                p, ps = b.parity, enter("A2", it)
                pe.wait_ge(a_pool, b.done())
                two(ps[0:S, 0:D], lambda k: xT[p][:, k], lambda k: wqkv[:, k, 2 * D:3 * D])
                two(ps[0:64, 256:356], lambda k: rqw[:, k], lambda k: xT[p][:, k])
                two(ps[0:64, 356:406], lambda k: rkvh[:, k, 0:64], lambda k: pairsum[:, k])
                two(ps[0:NL, 406:470], lambda k: pairsum[:, k], lambda k: rkvh[:, k, 64:128]).then_inc(filled["A2"], 1)

            def self_maxima(it, g):
                b = it.of("A")
                pe.wait_ge(max_read, in_order(MAXIMA, f"As{g}", it, back=1))
                pe.wait_ge(a_cast, b.done(per=4))
                n = 500 if g == 0 else 400
                for i in range(2):
                    pe.matmul(MX[0:S, i, 0:n], identb[0:S, 0:S], mask_q[:, 0:n], start=True, stop=True)
                for t in range(2):
                    for e in range(2):
                        for i in range(2):
                            r = 32 * (2 * g + i)
                            c = (2 * t + e) * S
                            mm = pe.matmul(MX[0:S, i, c:c + S], Qsb[r:r + 32, t, e], Ksb[r:r + 32, t],
                                           start=False, stop=True, skip_group_check=True)
                if g == 0:
                    for e in range(2):
                        for i in range(2):
                            c = 400 + e * NL
                            mm = pe.matmul(MX[0:S, i, c:c + NL], Qlb[32 * i:32 * i + 32, e], Klb[32 * i:32 * i + 32],
                                           start=False, stop=True, skip_group_check=True)
                mm.then_inc(max_full, 1)

            def A4(it):
                ps = enter("A4", it)
                pe.wait_ge(max_read, in_order(MAXIMA, "As1", it))
                pe.transpose(ps[:, 0:S // 2].bitcast(BF16), negmax_s[:], identb[0:S, 0:S]).then_inc(filled["A4"], 1)

            def self_scores(it, u):
                first = pair_of(f"As{u}", it)
                after1 = held(pe, in_order(SCORES, f"As{u}", it, back=2))
                after2 = held(pe, uses("A4", it))
                pe.wait_ge(started, 1)
                pe.wait_ge(st_exp, after1)
                pe.wait_ge(emptied[bank("A4", it)], after2)
                nk, width = (S, 400) if u < 2 else (NL, 200)
                for i in range(2):
                    pe.matmul(ST[0:nk, first + i, 0:width], identb[0:nk, 0:nk], (mask_k if u < 2 else mask_l)[:],
                              start=True, stop=True)
                for t in range(2 if u < 2 else 1):
                    for i in range(2):
                        r = 32 * (2 * u + i) if u < 2 else 32 * i
                        out = ST[0:nk, first + i, t * 200:t * 200 + 200]
                        lhs = Ks[r:r + 32, t] if u < 2 else Kl[r:r + 32]
                        rhs = (Qs[r:r + 32, t] if u < 2 else Ql[r:r + 32]).rearrange("p e q -> p (e q)")
                        pe.matmul(out, lhs, rhs, start=False, stop=True, skip_group_check=True)
                    for e in range(2):
                        for i in range(2):
                            r = 32 * (2 * u + i) if u < 2 else 32 * i
                            c = t * 200 + e * S
                            row = 2 * t + e if u < 2 else 4 + e
                            mm = pe.matmul(ST[0:nk, first + i, c:c + S], select[r:r + 32, row, 0:nk], shift_s[r:r + 32],
                                           start=False, stop=True, skip_group_check=True)
                mm.then_inc(st_full, 1)

            def A6(it):
                ps = enter("A6", it)
                pe.wait_ge(st_exp, in_order(SCORES, "As2", it))
                for h in range(H):
                    t, r, e = h // 8, h % 8 // 2, h % 2
                    pe.matmul(ps[0:S, h * SP1:(h + 1) * SP1], Ps[:, r, t, e], Vs[:, h], start=True, stop=True)
                for h in range(LH):
                    mm = pe.matmul(ps[0:S, (H + h) * SP1:(H + h + 1) * SP1], Pl[:, h // 2, h % 2], Vl[:, h],
                                   start=True, stop=True)
                mm.then_inc(filled["A6"], 1)

            def B1(it):
                ps = MI[bank("B1", it)]
                free, there = held(pe, uses_before("B1", it)), held(pe, uses("A6", it))
                pe.wait_ge(started, 1)
                pe.wait_ge(emptied[bank("B1", it)], free)
                if bank("A6", it) != bank("B1", it):
                    pe.wait_ge(emptied[bank("A6", it)], there)
                pe.transpose(ps[0:64, 0:S], Os[:, H:H + LH].rearrange("p h d -> p (h d)"), ident[0:S, 0:S]).then_inc(filled["B1"], 1)

            def B2(it):
                ps = enter("B2", it, "B1")
                pe.matmul(ps[0:S, 0:D], latT[:], routw[:], start=True, stop=True).then_inc(filled["B2"], 1)

            def turned(step, it, source):
                ps = MI[bank(step, it)]
                for t in range(2):
                    mm = pe.transpose(ps[:, t * S:(t + 1) * S], source[:, t * 128:(t + 1) * 128], ident[0:S, 0:S])
                mm.then_inc(filled[step], 1)

            def B3(it):
                enter("B3", it)
                pe.wait_ge(b_mixed, it.of("B").done())
                turned("B3", it, mixed)

            def B4(it):
                ps = enter("B4", it, "B3")
                two(ps[0:S, 0:D], lambda k: mixT[:, k], lambda k: outw[:, k]).then_inc(filled["B4"], 1)

            def B5(it):
                enter("B5", it)
                pe.wait_ge(b_ln, it.of("B").done(per=3))
                turned("B5", it, x1)

            def B6(it):
                ps = enter("B6", it, "B5")
                for t in range(2):
                    mm = two(ps[:, t * S:(t + 1) * S], lambda k: WqC[:, k, t * 128:(t + 1) * 128], lambda k: x1T[:, k])
                mm.then_inc(filled["B6"], 1)

            def B7(it):
                ps = enter("B7", it)
                pe.wait_ge(b_sq, it.of("B").done())
                pe.matmul(ps[:, 0:2 * S], average[:], sqq[:].rearrange("p t q -> p (t q)"), start=True, stop=True).then_inc(filled["B7"], 1)

            def K12(it, t):
                step, b = f"K{t + 1}", it.of("K")
                p, ps = b.parity, enter(step, it)
                pe.wait_ge(loaded_c[p], b.pairs(16))
                two(ps[:, 0:M], lambda k: WkC[:, k, t * 128:(t + 1) * 128], lambda k: cT[p][:, k]).then_inc(filled[step], 1)

            def K34(it, t):
                step, b = f"K{t + 3}", it.of("K")
                ps = enter(step, it)
                pe.wait_ge(k_sq, b.done(per=2, k=t + 1))
                pe.matmul(ps[:, 0:M], average[:], sqk[:, t], start=True, stop=True).then_inc(filled[step], 1)

            def K56(it, tiles):
                step, b = ("K5" if tiles[0] == 0 else "K6"), it.of("K")
                p, ps = b.parity, enter(step, it)
                for n, kt in enumerate(tiles):
                    mm = two(ps[0:KN[kt], n * D:(n + 1) * D], lambda k: cT[p][:, k, KO[kt]:KO[kt] + KN[kt]],
                             lambda k: WvT[:, k])
                mm.then_inc(filled[step], 1)

            def cross_maximum(it, n):
                b = it.of("X")
                p, t, r, e = b.parity, n // 8, 32 * (n % 8 // 2), n % 2
                back = 1 if n == 6 and it.has("A") else 2
                pe.wait_ge(max_read, in_order(MAXIMA, f"X{n}", it, back=back))
                if n == 0:
                    pe.wait_ge(k_hi, b.done(per=2))
                    pe.wait_ge(b_qh, b.done())
                pe.matmul(MX[0:S, n % 2, 0:M], Qh[p][r:r + 32, t, e], Kh[p][r:r + 32, t],
                          start=True, stop=True).then_inc(max_full, 1)

            def X1(it):
                ps = enter("X1", it)
                pe.wait_ge(max_read, in_order(MAXIMA, "X15", it))
                pe.transpose(ps[:, 0:S // 2].bitcast(BF16), negmax_x[:], identb[0:S, 0:S]).then_inc(filled["X1"], 1)

            def cross_scores(it, u):
                b, first = it.of("X"), pair_of(f"X{u}", it)
                p, t, g = b.parity, u // 4, u // 2 % 2
                pe.wait_ge(st_exp, in_order(SCORES, f"X{u}", it, back=2))
                if u == 0:
                    pe.wait_ge(*left("X1", it))
                    pe.wait_ge(k_lo, b.done(per=2))
                    pe.wait_ge(b_q, b.done(per=3))
                for kt in ([0, 1] if u % 2 == 0 else [2]):
                    keys = slice(KO[kt], KO[kt] + KN[kt])
                    c = kt % 2 * 200
                    for n, (k, q) in enumerate(((Kh, Qh), (Kh, Qlo), (Klo, Qh))):
                        for i in range(2):
                            r = 32 * (2 * g + i)
                            pe.matmul(ST[0:KN[kt], first + i, c:c + 200], k[p][r:r + 32, t, keys],
                                      q[p][r:r + 32, t].rearrange("p e q -> p (e q)"), start=(n == 0), stop=True,
                                      skip_group_check=True)
                    for e in range(2):
                        for i in range(2):
                            r = 32 * (2 * g + i)
                            mm = pe.matmul(ST[0:KN[kt], first + i, c + e * S:c + e * S + S],
                                           select[r:r + 32, 2 * t + e, 0:KN[kt]], shift_x[r:r + 32],
                                           start=False, stop=True, skip_group_check=True)
                mm.then_inc(st_full, 1)

            def T1(it):
                b = it.of("T")
                p, ps = b.parity, enter("T1", it)
                pe.wait_ge(st_exp, it.value(st_count(it.n - 1), len(SCORES)))
                for h in range(H):
                    t, r, e = h // 8, h % 8 // 2, h % 2
                    for kt in range(3):
                        mm = pe.matmul(ps[0:S, h * SP1:(h + 1) * SP1], Px[0:KN[kt], 2 * t + r // 2, r % 2, kt, e],
                                       Vx[p][0:KN[kt], kt, h], start=(kt == 0), stop=(kt == 2))
                mm.then_inc(filled["T1"], 1)

            def T2(it):
                enter("T2", it)
                pe.wait_ge(t_pool, it.of("T").done())
                turned("T2", it, Oxb)

            def T3(it):
                ps = enter("T3", it, "T2")
                two(ps[0:S, 0:D], lambda k: OxT[:, k], lambda k: WpT[:, k]).then_inc(filled["T3"], 1)

            def T4(it):
                enter("T4", it)
                pe.wait_ge(t_ln, it.of("T").done(per=3))
                turned("T4", it, x2[it.of("T").parity])

            def T5(it):
                ps = enter("T5", it, "T4")
                two(ps[0:S, 0:E], lambda k: x2T[:, k], lambda k: wsw[:, k]).then_inc(filled["T5"], 1)

            def T6(it):
                ps = enter("T6", it)
                pe.wait_ge(t_top, it.of("T").done(per=5))
                pe.matmul(ps[0:S, 0:E], upto[:], onehot[:], start=True, stop=True)
                pe.matmul(ps[0:S, E:2 * E], ones[:], onehot[:], start=True, stop=True).then_inc(filled["T6"], 1)

            def body(it):
                a, x, t = it.has("A"), it.has("X"), it.has("T")
                if t: T1(it)
                if a: A1(it)
                if x: cross_maximum(it, 0); cross_maximum(it, 1)
                if a: K12(it, 0)
                if x: cross_maximum(it, 2)
                if a: A2(it)
                if x: cross_maximum(it, 3); cross_maximum(it, 4)
                if a: K12(it, 1)
                if x: cross_maximum(it, 5)
                if t: T2(it)
                if a: self_maxima(it, 0); K34(it, 0); self_maxima(it, 1)
                if x: cross_maximum(it, 6); cross_maximum(it, 7)
                if a: A4(it)
                if x: cross_maximum(it, 8)
                if a: K34(it, 1)
                if x: cross_maximum(it, 9)
                if a: self_scores(it, 0)
                if x: cross_maximum(it, 10)
                if t: T3(it)
                if a: self_scores(it, 1)
                if x: cross_maximum(it, 11)
                if a: self_scores(it, 2); K56(it, [0, 1])
                if x: cross_maximum(it, 12); cross_maximum(it, 13)
                if a: A6(it)
                if x: cross_maximum(it, 14)
                if a: K56(it, [2])
                if x: cross_maximum(it, 15)
                if t: T4(it)
                if x: X1(it)
                if a: B1(it)
                if x: cross_scores(it, 0)
                if a: B2(it)
                if x: cross_scores(it, 1)
                if t: T5(it)
                if x: cross_scores(it, 2)
                if a: B3(it)
                if x: cross_scores(it, 3)
                if t: T6(it)
                if a: B4(it)
                if x: cross_scores(it, 4); cross_scores(it, 5)
                if a: B5(it)
                if x: cross_scores(it, 6)
                if a: B6(it)
                if x: cross_scores(it, 7)
                if a: B7(it)

            iterations(pe, body)

            def expert(e):
                p = e.parity
                pe.wait_ge(xe_in[p], e.pairs(16))
                pe.wait_ge(xe_ok, e.done(back=1))
                for s in range(2):
                    for k in range(2):
                        mm = pe.transpose(MI[0][:, k * CAP + s * S:k * CAP + (s + 1) * S], Xe[p][:, s, k * 128:(k + 1) * 128],
                                          ident[0:S, 0:S])
                mm.then_inc(xe_mm, 1)
                pe.wait_ge(xe_ok, e.done())
                pe.wait_ge(w_in[p], e.pairs(64))
                for q in range(4):
                    pe.wait_ge(h_act if q % 2 == 0 else h_dve, e.done(per=2, k=q // 2 + 1, back=1))
                    for m in (2 * q, 2 * q + 1):
                        mm = two(ST[:, q, m % 2 * CAP:(m % 2 + 1) * CAP], lambda k: W1[p][:, k, m * 128:(m + 1) * 128],
                                 lambda k: XeT[:, k])
                    mm.then_inc(h_mm, 1)
                pe.wait_ge(h_act, e.done(per=2))
                pe.wait_ge(h_dve, e.done(per=2))
                pe.wait_ge(y_ok, e.done(per=2, back=1))
                for s in range(2):
                    for m in range(8):
                        mm = pe.matmul(MX[0:S, s, 0:D], hT[:, m, s * S:(s + 1) * S], W2[p][:, m], start=(m == 0), stop=(m == 7))
                    mm.then_inc(y_mm, 1)

            expert(Seq(0))
            expert(Seq(1))
            with pe.Fori(0, (E - 2) // 2) as j:
                expert(Seq(2, j))
                expert(Seq(3, j))

        @block.scalar
        def _(act):
            act.preload_act_table_set("natural_log_exp_and_others")
            act.wait_ge(cast_const, POOL_CONST)
            act.wait_ge(weights_ok, 4)
            act.wait_ge(zeroed, 48)

            def leave(ins, step, it):
                ins.then_inc(emptied[bank(step, it)], 1)

            def copy_out(step, it, out, source, free=None):
                act.wait_ge(filled[step], it.of(step[0]).done())
                if free:
                    act.wait_ge(*free)
                leave(act.activation(out, source(MI[bank(step, it)]), ACT.Copy), step, it)

            def K12(it, t):
                step, b = f"K{t + 1}", it.of("K")
                act.wait_ge(filled[step], b.done())
                act.wait_ge(k_n, b.done(per=2, k=t + 1, back=1))
                act.wait_ge(k_sq, b.done(per=2, k=t + 1, back=1))
                leave(act.activation(kc[:, t], MI[bank(step, it)][:, 0:M], ACT.Identity, bias=bkC[:, t:t + 1]), step, it)

            def K34(it, t):
                step, b = f"K{t + 3}", it.of("K")
                act.wait_ge(filled[step], b.done())
                act.wait_ge(k_rs, b.done(per=2, k=t + 1, back=1))
                leave(act.activation(lnk[:, t], MI[bank(step, it)][:, 0:M], ACT.Ln, bias=eps[:]), step, it)
                act.wait_ge(*left(step, it))
                act.wait_ge(k_n, b.done(per=2, k=t + 1, back=1))
                act.activation(rsk[:, t], lnk[:, t], ACT.Exp, scale=-0.5).then_inc(k_rs, 1)

            def rstd(b, out, log, mv, made, sem_):
                act.wait_ge(made, b.done(per=3, k=2))
                act.wait_ge(made, b.done(per=3, back=1))
                act.activation(log[:], mv[:, 1:2], ACT.Ln, bias=eps[0:S]).then_inc(sem_, 1)
                act.wait_ge(sem_, b.done(per=2, k=1))
                act.activation(out[:], log[:], ACT.Exp, scale=-0.5).then_inc(sem_, 1)

            def self_exp(it, u):
                b, first = it.of("A"), pair_of(f"As{u}", it)
                act.wait_ge(st_full, in_order(SCORES, f"As{u}", it))
                if u == 0:
                    act.wait_ge(filled["A6"], b.done(back=1))
                if u < 2:
                    out, source = Ps[:, 2 * u:2 * u + 2].rearrange("p r t e q -> p r (t e q)"), ST[0:S, first:first + 2, 0:400]
                else:
                    out, source = Pl[:].rearrange("p r e q -> p r (e q)"), ST[0:NL, first:first + 2, 0:200]
                act.activation(out, source, ACT.Exp).then_inc(st_exp, 1)

            def cross_exp(it, u):
                b, first = it.of("X"), pair_of(f"X{u}", it)
                act.wait_ge(st_full, in_order(SCORES, f"X{u}", it))
                if u == 0:
                    act.wait_ge(filled["T1"], b.done(back=1))
                if u % 2 == 0:
                    out = Px[:, u // 2, :, 0:2].rearrange("p r k e q -> p r (k e q)")
                    source = ST[0:KN[0], first:first + 2, 0:400]
                else:
                    out = Px[0:KN[2], u // 2, :, 2].rearrange("p r e q -> p r (e q)")
                    source = ST[0:KN[2], first:first + 2, 0:200]
                act.activation(out, source, ACT.Exp).then_inc(st_exp, 1)

            def gate_exp(it):
                b = it.of("B")
                act.wait_ge(b_z, b.done(per=4, k=1))
                act.activation(gate_e[:], gate_z[:], ACT.Exp, scale=-1.0).then_inc(b_e, 1)

            def B6(it):
                act.wait_ge(filled["B6"], it.of("B").done())
                act.wait_ge(b_q, it.of("B").done(per=3, k=1, back=1))
                for t in range(2):
                    ins = act.activation(qc[:, t], MI[bank("B6", it)][:, t * S:(t + 1) * S], ACT.Identity, bias=bqC[:, t:t + 1])
                leave(ins, "B6", it)

            def B7(it):
                b = it.of("B")
                act.wait_ge(filled["B7"], b.done())
                leave(act.activation(lnq[:].rearrange("p t q -> p (t q)"), MI[bank("B7", it)][:, 0:2 * S], ACT.Ln, bias=eps[:]), "B7", it)
                act.wait_ge(*left("B7", it))
                act.activation(rsq[:], lnq[:], ACT.Exp, scale=-0.5).then_inc(b_rsq, 1)

            def router_exp(it):
                b = it.of("T")
                act.wait_ge(t_top, b.done(per=5, k=2))
                act.wait_ge(t_exp, b.done(back=1))
                act.activation(exps8[:], logits[:], ACT.Exp, bias=negtop[:], accum_out=sum8[:, bass.ds(b.index(), 1)]).then_inc(t_exp, 1)

            halves = lambda ps: ps[:, 0:2 * S].rearrange("p (t q) -> p t q", t=2)
            shifts = lambda ps: ps[:, 0:S // 2].bitcast(BF16)

            def body(it):
                a, x, t = it.has("A"), it.has("X"), it.has("T")
                A, Bs, T, Xs = it.of("A"), it.of("B"), it.of("T"), it.of("X")
                if a: K12(it, 0); K12(it, 1)
                if t: copy_out("T2", it, OxT[:], halves)
                if a: K34(it, 0); copy_out("A4", it, shift_s[:], shifts); K34(it, 1); self_exp(it, 0)
                if t: rstd(T, rs2, ln2, mv2, t_ln, t_rs)
                if a: self_exp(it, 1); self_exp(it, 2)
                if t: copy_out("T4", it, x2T[:], halves)
                if x: copy_out("X1", it, shift_x[:], shifts)
                if a: copy_out("B1", it, latT[:], lambda ps: ps[0:64, 0:S])
                if x: cross_exp(it, 0)
                if x: cross_exp(it, 1)
                if a: gate_exp(it)
                if t: router_exp(it)
                if x: cross_exp(it, 2)
                if a: copy_out("B3", it, mixT[:], halves)
                if x: cross_exp(it, 3)
                if a: rstd(Bs, rs1, ln1, mv1, b_ln, b_rs)
                if x: cross_exp(it, 4)
                if a: copy_out("B5", it, x1T[:], halves)
                if x: cross_exp(it, 5)
                if a: B6(it)
                if x: cross_exp(it, 6)
                if a: B7(it)
                if x: cross_exp(it, 7)

            iterations(act, body)

            def expert(e):
                p = e.parity
                act.wait_ge(xe_mm, e.done())
                act.wait_ge(h_mm, e.done(per=4, back=1))
                act.activation(XeT[:], MI[0][:, 0:2 * CAP].rearrange("p (k c) -> p k c", k=2), ACT.Copy).then_inc(xe_ok, 1)
                for q in (0, 2):
                    act.wait_ge(h_mm, e.done(per=4, k=q + 1))
                    if q == 0:
                        act.wait_ge(y_mm, e.done(per=2, back=1))
                    for m in (2 * q, 2 * q + 1):
                        ins = act.activation(hT[:, m], ST[:, q, m % 2 * CAP:(m % 2 + 1) * CAP], ACT.Relu, bias=b1[p][:, m:m + 1])
                    ins.then_inc(h_act, 1)
                act.wait_ge(y_ok, e.done(per=2))
                act.dma_start(slots[bass.ds(e.index() * CAP, CAP), :].rearrange("(s p) d -> p s d", p=S), Y[p][:]).then_inc(y_out[p], 16)

            expert(Seq(0))
            expert(Seq(1))
            with act.Fori(0, (E - 2) // 2) as j:
                expert(Seq(2, j))
                expert(Seq(3, j))

            def rstd_round(j):
                act.wait_ge(e_mv, j * 4 + 4)
                act.wait_ge(e_out, j * 4)
                act.activation(ln3[:], mv3[:, :, 1], ACT.Ln, bias=eps[0:S]).then_inc(e_rs, 1)
                act.wait_ge(e_rs, j * 2 + 1)
                act.activation(rs3[:], ln3[:], ACT.Exp, scale=-0.5).then_inc(e_rs, 1)

            rounds(act, rstd_round)

        @block.vector
        def _(dve):
            dve.wait_ge(weights_mm, 2)
            for n, w in enumerate((WkC, WqC)):
                dve.tensor_copy(w[:].rearrange("p k o -> p (k o)"), MX[:, n]).then_inc(weights_ok, 1)
            dve.tensor_copy(bkC[:], MI[0][:, 0:2]).then_inc(weights_ok, 1)
            dve.tensor_copy(bqC[:], MI[0][:, 2:4]).then_inc(weights_ok, 1)
            dve.wait_ge(cast_const, POOL_CONST)

            def leave(ins, step, it):
                ins.then_inc(emptied[bank(step, it)], 1)

            def A1(it):
                b, ps = it.of("A"), MI[bank("A1", it)]
                dve.wait_ge(filled["A1"], b.done())
                if it.n > -1:
                    dve.wait_ge(st_full, it.value(self_scores_before(it), len(SCORES)))
                dve.wait_ge(a_cast, b.done(per=4, k=2, back=1))
                for t in range(2):
                    for e in range(2):
                        dve.tensor_scalar(Qs[:, t, e], ps[:, t * S:(t + 1) * S], bqk[:, t:t + 1], parity_s[:, e:e + 1], ALU.add, ALU.mult)
                    ins = dve.tensor_scalar(Ks[:, t], ps[:, (2 + t) * S:(3 + t) * S], bqk[:, 2 + t:3 + t], None, ALU.add)
                leave(ins, "A1", it)

            def A2(it):
                b, ps = it.of("A"), MI[bank("A2", it)]
                dve.wait_ge(filled["A2"], b.done())
                dve.wait_ge(filled["A6"], b.done(back=1))
                dve.wait_ge(a_cast, b.done(per=4, back=1))
                heads = lambda ap: ap.rearrange("p (h d) -> p h d", d=HD)
                dve.tensor_tensor(Vs[:, :, 0:HD], heads(ps[0:S, 0:D]), heads(bv_self[:]), ALU.add)
                for e in range(2):
                    dve.tensor_scalar(Ql[:, e], ps[0:64, 256:356], rqb[:], parity_s[0:64, e:e + 1], ALU.add, ALU.mult)
                dve.tensor_scalar(Kl[:], ps[0:64, 356:406], rkb[:], None, ALU.add)
                leave(dve.tensor_tensor(Vl[:, :, 0:HD], heads(ps[0:NL, 406:470]), heads(rvb[:]), ALU.add), "A2", it)

            def self_max(it, g):
                dve.wait_ge(max_full, in_order(MAXIMA, f"As{g}", it))
                if g == 0:
                    dve.wait_ge(filled["A4"], it.of("A").done(back=1))
                out = negmax_s[:].rearrange("p (r u) -> p r u", u=32)
                if g == 0:
                    dve.tensor_reduce(out[:, 0:2, 4:6], MX[0:S, :, 400:500].rearrange("p i (e k) -> p i e k", k=NL), X, ALU.max, negate=True)
                dve.tensor_reduce(out[:, 2 * g:2 * g + 2, 0:4], MX[0:S, :, 0:400].rearrange("p i (u k) -> p i u k", k=S), X, ALU.max,
                                  negate=True).then_inc(max_read, 1)

            def cross_max(it, n):
                dve.wait_ge(max_full, in_order(MAXIMA, f"X{n}", it))
                if n == 0:
                    dve.wait_ge(filled["X1"], it.of("X").done(back=1))
                c = 32 * (n % 8 // 2) + 2 * (n // 8) + n % 2
                dve.tensor_reduce(negmax_x[:, c:c + 1], MX[0:S, n % 2, 0:M], X, ALU.max, negate=True).then_inc(max_read, 1)

            def A6(it):
                b = it.of("A")
                dve.wait_ge(filled["A6"], b.done())
                heads = MI[bank("A6", it)][0:S, 0:(H + LH) * SP1].rearrange("p (h d) -> p h d", d=SP1)
                dve.wait_ge(b_pool, b.done(per=5, back=1))
                dve.reciprocal(recip_s[:], heads[:, :, HD]).then_inc(a_dve, 1)
                dve.wait_ge(a_dve, b.done(per=2, k=1))
                dve.tensor_tensor(recip_m[:], recip_s[:], some_key[:], ALU.mult).then_inc(a_dve, 1)
                dve.wait_ge(a_dve, b.done(per=2))
                leave(dve.tensor_tensor(Os[:], heads[:, :, 0:HD], recip_m[:].unsqueeze(2).to_broadcast([S, H + LH, HD]), ALU.mult), "A6", it)

            def B2(it):
                dve.wait_ge(filled["B2"], it.of("B").done())
                dve.wait_ge(b_mixed, it.of("B").done(back=1))
                leave(dve.tensor_tensor(rem[:], MI[bank("B2", it)][0:S, 0:D], routb[:], ALU.add), "B2", it)

            def gate_sum(it):
                b = it.of("B")
                dve.wait_ge(b_pool, b.done(per=5, k=4))
                dve.tensor_reduce(gate_z[:], gate_t[:].rearrange("p (h d) -> p h d", d=HD), X, ALU.add).then_inc(b_z, 1)

            def gating(it):
                b = it.of("B")
                dve.wait_ge(b_e, b.done())
                dve.tensor_scalar(gate_d[:], gate_e[:], 1.0, None, ALU.add).then_inc(b_z, 1)
                dve.wait_ge(b_z, b.done(per=4, k=2))
                dve.reciprocal(gate[:], gate_d[:]).then_inc(b_z, 1)
                dve.wait_ge(b_z, b.done(per=4, k=3))
                dve.wait_ge(b_pool, b.done(per=5))
                heads = lambda x: x[:].rearrange("p (h d) -> p h d", d=HD)
                dve.tensor_tensor(heads(gated), heads(differ), gate[:].unsqueeze(2).to_broadcast([S, H, HD]), ALU.mult).then_inc(b_z, 1)

            def B4(it):
                b = it.of("B")
                dve.wait_ge(filled["B4"], b.done())
                dve.wait_ge(b_pool, b.done(per=5, k=2))
                leave(dve.tensor_tensor(res1[:], MI[bank("B4", it)][0:S, 0:D], xob[:], ALU.add), "B4", it)
                dve.wait_ge(*left("B4", it))
                dve.bn_stats(bn1[:], res1[:]).then_inc(b_ln, 1)
                after = held(dve, b.done(per=3, k=1))
                dve.wait_ge(started, 1)
                dve.wait_ge(b_ln, after)
                dve.bn_aggr(mv1[:], bn1[:]).then_inc(b_ln, 1)

            def norm1(it):
                b = it.of("B")
                dve.wait_ge(b_rs, b.done(per=2))
                dve.wait_ge(filled["B5"], b.done(back=1))
                dve.wait_ge(b_x1bp, b.done(back=1))
                dve.tensor_scalar(x1[:], res1[:], mv1[:, 0:1], rs1[:], ALU.subtract, ALU.mult).then_inc(b_ln, 1)

            def queries(it):
                b = it.of("B")
                p = b.parity
                dve.wait_ge(b_rsq, b.done())
                dve.tensor_tensor(qn[:], qc[:], rsq[:], ALU.mult).then_inc(b_q, 1)
                dve.wait_ge(b_q, b.done(per=3, k=1))
                dve.wait_ge(b_qh, b.done(back=1))
                dve.tensor_scalar(Qx[:, :, 0], qn[:], gq2[:, 0:1], bq2n[:, 0:1], ALU.mult, ALU.add)
                dve.tensor_scalar(Qx[:, :, 1], qn[:], gq2[:, 1:2], bq2n[:, 1:2], ALU.mult, ALU.add).then_inc(b_q, 1)
                dve.wait_ge(b_qh, b.done())
                dve.tensor_tensor(Qlo[p][:], Qx[:], Qh[p][:], ALU.subtract).then_inc(b_q, 1)

            def key_norm(it, t):
                b = it.of("K")
                dve.wait_ge(k_rs, b.done(per=2, k=t + 1))
                dve.wait_ge(k_hi, b.done(per=2, k=t + 1, back=1))
                dve.scalar_tensor_tensor(kn[:, t], kc[:, t], norm4[:, 2:3], rsk[:, t], ALU.mult, ALU.mult).then_inc(k_n, 1)

            def key_low(it, t):
                b = it.of("K")
                p = b.parity
                dve.wait_ge(k_hi, b.done(per=2, k=t + 1))
                dve.scalar_tensor_tensor(Klo[p][:, t], kn[:, t], norm4[:, 3:4], Kh[p][:, t], ALU.add, ALU.subtract).then_inc(k_lo, 1)

            def values(it, tiles):
                step, b = ("K5" if tiles[0] == 0 else "K6"), it.of("K")
                dve.wait_ge(filled[step], b.done())
                dve.wait_ge(filled["T1"], b.done(back=2))
                n, k0 = KN[tiles[-1]], tiles[0]
                for i, kt in enumerate(tiles):
                    ins = dve.tensor_copy(Vx[b.parity][0:KN[kt], kt, :, 0:HD],
                                          MI[bank(step, it)][0:KN[kt], i * D:(i + 1) * D].rearrange("p (h d) -> p h d", d=HD))
                leave(ins, step, it)

            def T1(it):
                b = it.of("T")
                dve.wait_ge(filled["T1"], b.done())
                dve.wait_ge(t_pool, b.done(back=1))
                heads = MI[bank("T1", it)][0:S, 0:H * SP1].rearrange("p (h d) -> p h d", d=SP1)
                dve.reciprocal(recip_x[:], heads[:, :, HD]).then_inc(t_dve, 1)
                dve.wait_ge(t_dve, b.done())
                leave(dve.tensor_tensor(Ox[:], heads[:, :, 0:HD], recip_x[:].unsqueeze(2).to_broadcast([S, H, HD]), ALU.mult), "T1", it)

            def T3(it):
                b = it.of("T")
                dve.wait_ge(filled["T3"], b.done())
                dve.wait_ge(b_x1bp, b.done())
                leave(dve.tensor_tensor(res2[:], MI[bank("T3", it)][0:S, 0:D], x1bp[b.parity][:], ALU.add), "T3", it)
                dve.wait_ge(*left("T3", it))
                dve.bn_stats(bn2[:], res2[:]).then_inc(t_ln, 1)
                after = held(dve, b.done(per=3, k=1))
                dve.wait_ge(started, 1)
                dve.wait_ge(t_ln, after)
                dve.bn_aggr(mv2[:], bn2[:]).then_inc(t_ln, 1)

            def norm2(it):
                b = it.of("T")
                dve.wait_ge(t_rs, b.done(per=2))
                dve.wait_ge(scattered, b.done(per=16, back=1))
                dve.tensor_scalar(x2[b.parity][:], res2[:], mv2[:, 0:1], rs2[:], ALU.subtract, ALU.mult).then_inc(t_ln, 1)

            def route_to(it):
                b = it.of("T")
                dve.wait_ge(filled["T5"], b.done())
                dve.wait_ge(t_exp, b.done(back=1))
                leave(dve.tensor_tensor(logits[:], MI[bank("T5", it)][0:S, 0:E], bsw[:], ALU.add), "T5", it)
                after = held(dve, uses("T5", it))
                dve.wait_ge(started, 1)
                dve.wait_ge(emptied[bank("T5", it)], after)
                dve.max(top8[:], logits[:]).then_inc(t_top, 1)
                dve.wait_ge(t_top, b.done(per=5, k=1))
                dve.tensor_scalar(negtop[:], top8[:, 0:1], -1.0, None, ALU.mult).then_inc(t_top, 1)
                dve.max_index(index8[:], top8[:], logits[:]).then_inc(t_top, 1)
                dve.wait_ge(t_top, b.done(per=5, k=3))
                dve.wait_ge(t_pos, b.done(per=7, back=1))
                dve.tensor_copy(route[:], index8[:, 0:1]).then_inc(t_top, 1)
                dve.wait_ge(t_top, b.done(per=5, k=4))
                dve.tensor_scalar(onehot[:], expert_id[:], route[:], None, ALU.is_equal).then_inc(t_top, 1)

            def place_in(it):
                b = it.of("T")
                p, ps = b.parity, MI[bank("T6", it)]
                dve.wait_ge(filled["T6"], b.done())
                dve.tensor_tensor(place[:], ps[0:S, 0:E], carry[1 - p][:], ALU.add).then_inc(t_pos, 1)
                leave(dve.tensor_tensor(carry[p][:], ps[0:S, E:2 * E], carry[1 - p][:], ALU.add), "T6", it)
                dve.wait_ge(t_pos, b.done(per=7, k=1))
                dve.tensor_tensor_reduce(place1[:], place[:], onehot[:], 1.0, 0.0, ALU.mult, ALU.add, pos[:]).then_inc(t_pos, 1)
                dve.wait_ge(t_pos, b.done(per=7, k=2))
                dve.tensor_scalar(keep[:], pos[:], float(CAP), None, ALU.is_lt)
                dve.scalar_tensor_tensor(slot0[:], route[:], float(CAP), pos[:], ALU.mult, ALU.add).then_inc(t_pos, 1)
                dve.wait_ge(t_pos, b.done(per=7, k=3))
                own = own_row[:, bass.ds(b.index(), 1)]
                dve.tensor_tensor(slot1[:], slot0[:], own, ALU.subtract).then_inc(t_pos, 1)
                dve.wait_ge(t_pos, b.done(per=7, k=4))
                dve.scalar_tensor_tensor(slot2[:], slot1[:], keep[:], own, ALU.mult, ALU.add).then_inc(t_pos, 1)
                dve.wait_ge(t_pos, b.done(per=7, k=5))
                dve.wait_ge(*left("T6", it))
                dve.tensor_copy(slot_all[:, bass.ds(b.index(), 1)], slot2[:]).then_inc(t_pos, 1)
                dve.wait_ge(scattered, b.done(per=16, back=1))
                dve.tensor_copy(slot[p][:], slot2[:]).then_inc(t_pos, 1)

            def body(it):
                a, x, t = it.has("A"), it.has("X"), it.has("T")
                if t: T1(it)
                if a: A1(it)
                if x: cross_max(it, 0); cross_max(it, 1)
                if x: cross_max(it, 2)
                if a: A2(it)
                if x: cross_max(it, 3); cross_max(it, 4); cross_max(it, 5)
                if a: self_max(it, 0); self_max(it, 1); key_norm(it, 0)
                if x: cross_max(it, 6); cross_max(it, 7); cross_max(it, 8)
                if a: key_low(it, 0)
                if x: cross_max(it, 9)
                if a: key_norm(it, 1)
                if x: cross_max(it, 10)
                if t: T3(it)
                if x: cross_max(it, 11)
                if a: key_low(it, 1); values(it, [0, 1])
                if t: norm2(it)
                if x: cross_max(it, 12); cross_max(it, 13)
                if a: A6(it)
                if x: cross_max(it, 14)
                if a: values(it, [2])
                if x: cross_max(it, 15)
                if a: B2(it); gate_sum(it)
                if t: route_to(it)
                if a: gating(it)
                if t: place_in(it)
                if a: B4(it); norm1(it); queries(it)

            iterations(dve, body)

            dve.wait_ge(t_exp, B)
            dve.reciprocal(pmax[:], sum8[:]).then_inc(e_one, 1)
            dve.wait_ge(e_one, 1)
            dve.reciprocal(pinv[:], pmax[:]).then_inc(e_one, 1)
            dve.wait_ge(e_one, 2)
            dve.tensor_tensor(pone[:], pmax[:], pinv[:], ALU.mult).then_inc(e_one, 1)

            def expert(e):
                p = e.parity
                for q in (1, 3):
                    dve.wait_ge(h_mm, e.done(per=4, k=q + 1))
                    if q == 1:
                        dve.wait_ge(y_mm, e.done(per=2, back=1))
                    for m in (2 * q, 2 * q + 1):
                        ins = dve.tensor_scalar(hT[:, m], ST[:, q, m % 2 * CAP:(m % 2 + 1) * CAP], b1[p][:, m:m + 1], 0.0, ALU.add, ALU.max)
                    ins.then_inc(h_dve, 1)
                dve.wait_ge(y_out[p], e.pairs(16, back=1))
                for s in range(2):
                    dve.wait_ge(y_mm, e.done(per=2, k=s + 1))
                    dve.tensor_tensor(Y[p][:, s], MX[0:S, s, 0:D], b2[p][:], ALU.add).then_inc(y_ok, 1)

            expert(Seq(0))
            expert(Seq(1))
            with dve.Fori(0, (E - 2) // 2) as j:
                expert(Seq(2, j))
                expert(Seq(3, j))

            dve.wait_ge(e_one, 3)
            dve.wait_ge(t_keep, B)

            def last_round(j):
                for c in range(4):
                    n = j * 4 + c
                    dve.wait_ge(g_in[c], j * 16 + 16)
                    if c == 0:
                        dve.wait_ge(e_out, j * 4)
                    x2n = x2_all[:, bass.ds(n, 1), :].rearrange("p a d -> p (a d)")
                    dve.scalar_tensor_tensor(R[c][:], G[c][:], pone[:, bass.ds(n, 1)], x2n, ALU.mult, ALU.add).then_inc(e_sum, 1)
                for c in range(4):
                    dve.wait_ge(e_sum, j * 4 + (c + 1))
                    dve.bn_stats(bn3[:, c], R[c][:]).then_inc(e_bn, 1)
                for c in range(4):
                    after = held(dve, j * 4 + (c + 1))
                    dve.wait_ge(started, 1)
                    dve.wait_ge(e_bn, after)
                    dve.bn_aggr(mv3[:, c], bn3[:, c]).then_inc(e_mv, 1)
                dve.wait_ge(e_rs, j * 2 + 2)
                for c in range(4):
                    dve.wait_ge(stored[c], j * 16)
                    dve.tensor_scalar(O3[c][:], R[c][:], mv3[:, c, 0:1], rs3[:, c:c + 1], ALU.subtract, ALU.mult).then_inc(e_out, 1)

            rounds(dve, last_round)


POOL_CONST = 19


def st_count(n):
    return sum(OFFSET[u[0]] + i in range(B) for i in range(FIRST, n + 1) for u in SCORES)


def self_scores_before(it):
    return count(SCORES, "As2", It(it.n - 1))


def kernel(**inputs):
    import concourse.bacc as bacc
    from concourse.bass_utils import run_bass_kernel_spmd

    w = {k[3:]: np.asarray(v) for k, v in inputs.items() if k.startswith("L0_")}
    x = np.asarray(inputs["x"])
    c = np.asarray(inputs["ctx_1024"])

    def halves(a):
        return a.reshape(2, 128, -1).transpose(1, 0, 2)

    f = np.float32
    rows, cols = np.arange(128)[:, None], np.arange(128)[None, :]
    same_head = (rows // HD == cols // HD).astype(f)
    select = np.zeros((128, 6, 128), f)
    for r in range(4):
        for u in range(6):
            select[32 * r + u, u] = 1
    q = np.arange(S)[:, None]
    self_mask = np.where(np.arange(S)[None, :] >= q, NEG, 0).astype(f)
    latent_mask = np.where(np.arange(NL)[None, :] >= q // 2, NEG, 0).astype(f)
    some = np.ones((S, H + LH), f)
    some[0, :H] = 0
    some[0:2, H:] = 0
    arrays = {
        "ident": np.eye(128, dtype=f), "center": np.eye(128, dtype=f) - same_head / HD, "average": same_head / HD,
        "upto": (np.arange(S)[:, None] <= np.arange(S)[None, :]).astype(f), "select": select,
        "mask_q": np.concatenate([self_mask] * 4 + [latent_mask] * 2, axis=1),
        "mask_k": np.concatenate([self_mask.T] * 4, axis=1), "mask_l": np.concatenate([latent_mask.T] * 2, axis=1),
        "some_key": some, "expert_id": np.tile(np.arange(E, dtype=f), (S, 1)),
        "own_row": (E * CAP + np.arange(B)[None, :] * S + q).astype(f),
        "parity": np.stack([(np.arange(128) // HD % 2 == e).astype(f) for e in range(2)], axis=1),
        "qkv_w": halves(w["attn_qkv_w"]), "qk_b": w["attn_qkv_b"][:2 * D].reshape(4, 128).T,
        "rq_w": halves(w["attn_rq_w"]), "rq_b": w["attn_rq_b"][:, None], "rkv_w": halves(w["attn_rkv_w"]),
        "rk_b": w["attn_rkv_b"][:64, None], "rout_w": w["attn_rout_w"], "out_w": halves(w["attn_out_w"]),
        "Wq": halves(w["xattn_Wq"]), "Wk": halves(w["xattn_Wk"]), "bq": w["xattn_bq"].reshape(2, 128).T,
        "bk": w["xattn_bk"].reshape(2, 128).T, "WvT": halves(w["xattn_Wv"].T), "WpT": halves(w["xattn_Wp"].T),
        "norm4": np.stack([np.tile(w[f"xattn_{n}"], 8) for n in ("q_gamma", "q_beta", "k_gamma", "k_beta")], axis=1),
        "w_switch": halves(w["ffn_w_switch"]),
        "v_b": w["attn_qkv_b"][2 * D:], "rv_b": w["attn_rkv_b"][64:], "rout_b": w["attn_rout_b"], "out_b": w["attn_out_b"],
        "gl": np.tile(w["attn_gl_w"][:, 0], H), "gr": np.tile(w["attn_gr_w"][:, 0], H), "bv": w["xattn_bv"], "bp": w["xattn_bp"],
        "b_switch": w["ffn_b_switch"],
        "cT": halves(c.reshape(B * M, D).T), "xT": halves(x.reshape(B * S, D).T), "x": x.reshape(B * S, D),
        "w1": w["ffn_w1"], "w2": w["ffn_w2"], "b1": w["ffn_b1"].reshape(E, 8, 128).transpose(0, 2, 1), "b2": w["ffn_b2"],
    }
    nc = bacc.Bacc("TRN2", target_bir_lowering=False, num_devices=1)
    given, io = {}, {}
    for name, a in arrays.items():
        given[f"in_{name}"] = np.ascontiguousarray(a)
        io[name] = nc.dram_tensor(f"in_{name}", a.shape, F32, kind="ExternalInput").ap()
    io["out"] = nc.dram_tensor("out_x", (B * S, D), F32, kind="ExternalOutput").ap()
    decoder_kernel(nc, io)
    r = run_bass_kernel_spmd(nc, [given], core_ids=[0])
    return r.results[0]["out_x"].reshape(B, S, D)
```

```python
from contextlib import ExitStack

import numpy as np

import concourse.bass as bass
from concourse import mybir

ALU = mybir.AluOpType
ACT = mybir.ActivationFunctionType
X = mybir.AxisListType.X
F32, BF16, F16, U32 = mybir.dt.float32, mybir.dt.bfloat16, mybir.dt.float16, mybir.dt.uint32

B, S, D = 32, 100, 256
M = 361
H, HD = 16, 16
NL, LH = 50, 4
E, F, CAP = 8, 1024, 200
KN = [128, 128, M - 256]
KO = [0, 128, 256]
NEG = -1.0e30
EPS = 1e-5
SCALE = HD ** -0.5
SP1 = HD + 1
LIFT = 4.0
WEIGHT = 64.0
MOVES = 12
PAD = 128 - S

FIRST, LAST = -2, B
OFFSET = {"T": -1, "X": 0, "K": 1, "A": 2, "B": 1}

MISC = ["A1", "B1", "K1", "B2", "T1", "A2", "K2", "T2", "B3", "K3", "T3", "B4", "K4", "T4", "B5",
        "T5", "B6", "A4", "X1", "K5", "B7", "T6", "K6", "A6"]
MAXIMA = ["X0", "X1", "X2", "X3", "X4", "X5", "X6", "X7", "X8", "X9", "X10", "X11", "As0", "As1",
          "X12", "X13", "X14", "X15"]
SCORES = ["As0", "As1", "X0", "As2", "X1", "X2", "X3", "X4", "X5", "X6", "X7"]


class It:

    def __init__(self, n, j=None):
        self.n, self.j = n, j

    def value(self, here, per_iteration):
        return max(here, 0) if self.j is None else self.j * (2 * per_iteration) + here

    def before(self):
        return It(self.n - 1, self.j)

    def has(self, stage):
        return 0 <= self.n + OFFSET[stage] < B

    def of(self, stage):
        return Seq(self.n + OFFSET[stage], self.j)


class Seq:

    def __init__(self, n, j=None):
        self.n, self.j, self.parity = n, j, n % 2

    def done(self, per=1, k=None, back=0):
        here = (self.n - back) * per + (per if k is None else k)
        return max(here, 0) if self.j is None else self.j * (2 * per) + here

    def pairs(self, per, k=None, back=0):
        here = (self.n // 2 - back) * per + (per if k is None else k)
        return max(here, 0) if self.j is None else self.j * per + here

    def index(self):
        return self.n if self.j is None else self.j * 2 + self.n


def held(eng, value):
    return value if isinstance(value, int) else eng.to_reg(value)


def count(units, name, it):
    before = sum(OFFSET[u[0]] + i in range(B) for i in range(FIRST, it.n) for u in units)
    here = [u for u in units if it.has(u[0])]
    return before + here.index(name) + 1


def iterations(eng, body):
    for n in range(FIRST, 3):
        body(It(n))
    with eng.Fori(0, (B - 6) // 2) as j:
        body(It(3, j))
        body(It(4, j))
    for n in range(B - 3, LAST + 1):
        body(It(n))


def rounds(eng, body):
    body(0)
    with eng.Fori(1, B // 4) as j:
        body(j)


def decoder_kernel(nc, io):
    ctx = ExitStack()
    with ctx:
        def sb(name, shape, dt=F32):
            return ctx.enter_context(nc.sbuf_tensor(name, shape, dt))

        def sem(name):
            return ctx.enter_context(nc.semaphore(name))

        MI = [ctx.enter_context(nc.psum_tensor(f"MI{n}", [128, 512], F32)) for n in range(2)]
        MX = ctx.enter_context(nc.psum_tensor("MX", [128, 2, 512], F32))
        ST = ctx.enter_context(nc.psum_tensor("ST", [128, 4, 512], F32))

        early = sb("early", [128, 4 * F])
        wide = sb("wide", [128, 4828])

        stacked = sb("stacked", [128, 2 * 1456])

        def part(region, at, shape):
            n = int(np.prod(shape[1:]))
            ap = region[0:shape[0], at:at + n]
            names = "abcde"[:len(shape) - 1]
            sizes = dict(zip(names, shape[1:]))
            return ap.rearrange(f"p ({' '.join(names)}) -> p {' '.join(names)}", **sizes)

        ident = sb("ident", [128, 128])
        identb = sb("identb", [128, 128], BF16)
        center = sb("center", [128, 128])
        average = sb("average", [128, 128])
        upto = sb("upto", [S, S])
        ones = sb("ones", [S, S])
        select_f = part(early, 0, [128, 6, 128])
        select = sb("select", [128, 6, 128], BF16)
        mask_q_f = part(early, 768, [S, 500])
        mask_q = sb("mask_q", [S, 500], BF16)
        mask_k_f = part(early, 1268, [S, 400])
        mask_k = sb("mask_k", [S, 400], BF16)
        mask_l_f = part(early, 1668, [NL, 200])
        mask_l = sb("mask_l", [NL, 200], BF16)
        some_key = sb("some_key", [S, H + LH])
        expert_id = sb("expert_id", [S, E])
        own_row = sb("own_row", [S, B])
        parity = sb("parity", [128, 2])
        eps = sb("eps", [128, 1])
        zero1 = sb("zero1", [128, 1])
        lift = sb("lift", [128, 1])

        wqkv = sb("wqkv", [128, 2, 3 * D])
        bqk = sb("bqk", [128, 4])
        bv_self = sb("bv_self", [S, D])
        rqw = sb("rqw", [128, 2, 64])
        rqb = sb("rqb", [64, 1])
        rkvw = sb("rkvw", [128, 2, 128])
        rkvh = sb("rkvh", [128, 2, 128])
        rkb = sb("rkb", [64, 1])
        rvb = sb("rvb", [NL, 64])
        routw = sb("routw", [64, D])
        routb = sb("routb", [S, D])
        outw = sb("outw", [128, 2, D])
        outb = sb("outb", [S, D])
        glb = sb("glb", [S, D])
        grb = sb("grb", [S, D])
        Wq = part(early, 1868, [128, 2, D])
        Wk = part(early, 2380, [128, 2, D])
        WqC = sb("WqC", [128, 2, D])
        WkC = sb("WkC", [128, 2, D])
        bq2 = sb("bq2", [128, 2])
        bk2 = sb("bk2", [128, 2])
        bqC = sb("bqC", [128, 2])
        bkC = sb("bkC", [128, 2])
        WvT = sb("WvT", [128, 2, D])
        WpT = sb("WpT", [128, 2, D])
        bv_cross = sb("bv_cross", [S, D])
        bp = sb("bp", [S, D])
        norm4 = sb("norm4", [128, 4])
        parity_s = sb("parity_s", [128, 2])
        gq2 = sb("gq2", [128, 2])
        bq2n = sb("bq2n", [128, 2])
        wsw = sb("wsw", [128, 2, E])
        bsw = sb("bsw", [S, E])

        xT = [sb(f"xT{p}", [128, 2, S]) for p in range(2)]
        xn = [sb(f"xn{p}", [S, D]) for p in range(2)]
        pairsum = sb("pairsum", [128, 2, NL])
        Qs = sb("Qs", [128, 2, 2, S])
        Qsb = sb("Qsb", [128, 2, 2, S], BF16)
        Ks = sb("Ks", [128, 2, S])
        Ksb = sb("Ksb", [128, 2, S], BF16)
        Vs = sb("Vs", [S, H, HD])
        Vsh = sb("Vsh", [S, H, SP1], F16)
        Vsl = sb("Vsl", [S, H, SP1], F16)
        Ql = sb("Ql", [64, 2, S])
        Qlb = sb("Qlb", [64, 2, S], BF16)
        Kl = sb("Kl", [64, NL])
        Klb = sb("Klb", [64, NL], BF16)
        Vl = sb("Vl", [NL, LH, HD])
        Vlh = sb("Vlh", [NL, LH, SP1], F16)
        Vll = sb("Vll", [NL, LH, SP1], F16)
        negmax_s = sb("negmax_s", [S, 128], BF16)
        shift_s = sb("shift_s", [128, S], BF16)
        Psh = sb("Psh", [S, 16 * S + PAD], F16)
        Psl = sb("Psl", [S, 16 * S + PAD], F16)
        Plh = sb("Plh", [NL, 4 * S + PAD], F16)
        Pll = sb("Pll", [NL, 4 * S + PAD], F16)
        recip_s = sb("recip_s", [S, H + LH])
        recip_m = sb("recip_m", [S, H + LH])
        Os = sb("Os", [S, H + LH, HD])

        latT = sb("latT", [64, S])
        rem = sb("rem", [S, D])
        gate_l = sb("gate_l", [S, D])
        gate_r = sb("gate_r", [S, D])
        gate_t = sb("gate_t", [S, D])
        differ = sb("differ", [S, D])
        gate_z = sb("gate_z", [S, H])
        gate_e = sb("gate_e", [S, H])
        gate_d = sb("gate_d", [S, H])
        gate = sb("gate", [S, H])
        gated = sb("gated", [S, D])
        mixed = sb("mixed", [S, D])
        mixT = sb("mixT", [128, 2, S])
        xob = sb("xob", [S, D])
        res1 = sb("res1", [S, D])
        bn1 = sb("bn1", [S, 6])
        mv1 = sb("mv1", [S, 2])
        ln1 = sb("ln1", [S, 1])
        rs1 = sb("rs1", [S, 1])
        x1 = sb("x1", [S, D])
        x1bp = [sb(f"x1bp{p}", [S, D]) for p in range(2)]
        x1T = sb("x1T", [128, 2, S])
        qc = sb("qc", [128, 2, S])
        sqq = sb("sqq", [128, 2, S])
        lnq = sb("lnq", [128, 2, S])
        rsq = sb("rsq", [128, 2, S])
        qn = sb("qn", [128, 2, S])
        Qx = sb("Qx", [128, 2, 2, S])
        Qh = sb("Qh", [128, 2, 2, S], F16)
        Qlo = sb("Qlo", [128, 2, 2, S], F16)
        Qst = [sb(f"Qst{p}", [112, H * S + PAD], F16) for p in range(2)]
        Kst = [stacked[0:112, 1456 * p:1456 * (p + 1)].bitcast(F16) for p in range(2)]
        own_head = sb("own_head", [112, H])

        cT = [sb(f"cT{p}", [128, 2, M]) for p in range(2)]
        kc = part(early, 0 * 2 * M, [128, 2, M])
        sqk = part(early, 1 * 2 * M, [128, 2, M])
        lnk = part(early, 2 * 2 * M, [128, 2, M])
        rsk = part(early, 3 * 2 * M, [128, 2, M])
        kn = part(early, 4 * 2 * M, [128, 2, M])
        Kh = sb("Kh", [128, 2, M], F16)
        Klo = sb("Klo", [128, 2, M], F16)
        Vxh = [sb(f"Vxh{p}", [128, 3, H, SP1], F16) for p in range(2)]
        Vxl = [sb(f"Vxl{p}", [128, 3, H, SP1], F16) for p in range(2)]

        negmax_x = sb("negmax_x", [S, 128], BF16)
        Pxh = wide[:, 0:2414].bitcast(F16)
        Pxl = wide[:, 2414:4828].bitcast(F16)
        Pf = sb("Pf", [128, 2, 2, 400])
        recip_x = sb("recip_x", [S, H])
        Ox = sb("Ox", [S, H, HD])
        Oxb = sb("Oxb", [S, D])
        OxT = sb("OxT", [128, 2, S])
        res2 = sb("res2", [S, D])
        bn2 = sb("bn2", [S, 6])
        mv2 = sb("mv2", [S, 2])
        ln2 = sb("ln2", [S, 1])
        rs2 = sb("rs2", [S, 1])
        x2 = [sb(f"x2{p}", [S, D]) for p in range(2)]
        x2T = sb("x2T", [128, 2, S])
        x2_all = sb("x2_all", [S, B, D])
        logits = sb("logits", [S, E])
        top8 = sb("top8", [S, 8])
        negtop = sb("negtop", [S, 1])
        index8 = sb("index8", [S, 8], U32)
        route = sb("route", [S, 1])
        onehot = sb("onehot", [S, E])
        exps8 = sb("exps8", [S, E])
        sum8 = sb("sum8", [S, B])
        carry = [sb(f"carry{p}", [S, E]) for p in range(2)]
        place = sb("place", [S, E])
        place1 = sb("place1", [S, E])
        pos = sb("pos", [S, 1])
        keep = sb("keep", [S, 1])
        slot0 = sb("slot0", [S, 1])
        slot1 = sb("slot1", [S, 1])
        slot2 = sb("slot2", [S, 1])
        slot = [sb(f"slot{p}u", [S, 1], U32) for p in range(2)]
        slot_all = sb("slot_all", [S, B], U32)

        W1 = [sb("W1", [128, 2, F]), part(early, 0, [128, 2, F])]
        W2 = [part(stacked, 0, [128, 8, D]), part(early, 2 * F, [128, 8, D])]
        b1 = [sb(f"b1{p}", [128, 8]) for p in range(2)]
        b2 = [sb(f"b2{p}", [S, D]) for p in range(2)]
        Xe = [part(wide, 2000 + 512 * p, [S, 2, D]) for p in range(2)]
        XeT = part(wide, 1600, [128, 2, CAP])
        hT = part(wide, 0, [128, 8, CAP])
        Y = [part(wide, 3024 + 512 * p, [S, 2, D]) for p in range(2)]
        pmax = sb("pmax", [S, B])
        pinv = sb("pinv", [S, B])
        pone = sb("pone", [S, B])
        slot_g = [sb(f"slot_g{c}", [S, 1], U32) for c in range(4)]
        G = [part(early, (0 + c) * D, [S, D]) for c in range(4)]
        R = [part(early, (4 + c) * D, [S, D]) for c in range(4)]
        bn3 = sb("bn3", [S, 4, 6])
        mv3 = sb("mv3", [S, 4, 2])
        ln3 = sb("ln3", [S, 4])
        rs3 = sb("rs3", [S, 4])
        O3 = [part(early, (8 + c) * D, [S, D]) for c in range(4)]

        slots = nc.dram_tensor("slots", (E * CAP + B * S, D), F32, kind="Internal").ap()

        loaded_const = sem("loaded_const")
        cast_const = sem("cast_const")
        started = sem("started")
        zeroed = sem("zeroed")
        weights_mm = sem("weights_mm")
        weights_ok = sem("weights_ok")
        loaded_x = [sem(f"loaded_x{p}") for p in range(2)]
        loaded_n = [sem(f"loaded_n{p}") for p in range(2)]
        loaded_c = [sem(f"loaded_c{p}") for p in range(2)]
        filled = {s: sem(f"filled_{s}") for s in MISC}
        emptied = [sem(f"emptied_MI{n}") for n in range(2)]
        max_full = sem("max_full")
        max_read = sem("max_read")
        st_full = sem("st_full")
        st_exp = sem("st_exp")
        st_low = sem("st_low")
        a_vals = sem("a_vals")
        a_vhi = sem("a_vhi")
        a_vlo = sem("a_vlo")
        k_vhi = sem("k_vhi")
        a_pool = sem("a_pool")
        a_cast = sem("a_cast")
        a_dve = sem("a_dve")
        b_pool = sem("b_pool")
        b_mixed = sem("b_mixed")
        b_z = sem("b_z")
        b_e = sem("b_e")
        b_ln = sem("b_ln")
        b_rs = sem("b_rs")
        b_x1bp = sem("b_x1bp")
        b_c = sem("b_c")
        b_stack = [sem(f"b_stack{p}") for p in range(2)]
        k_stack = [sem(f"k_stack{p}") for p in range(2)]
        x_shift = sem("x_shift")
        b_rsq = sem("b_rsq")
        b_q = sem("b_q")
        b_qh = sem("b_qh")
        k_c = sem("k_c")
        k_rs = sem("k_rs")
        k_n = sem("k_n")
        k_hi = sem("k_hi")
        k_lo = sem("k_lo")
        t_dve = sem("t_dve")
        t_pool = sem("t_pool")
        t_ln = sem("t_ln")
        t_rs = sem("t_rs")
        t_keep = sem("t_keep")
        t_top = sem("t_top")
        t_exp = sem("t_exp")
        t_pos = sem("t_pos")
        scattered = sem("scattered")
        w_in = [sem(f"w_in{p}") for p in range(2)]
        xe_in = [sem(f"xe_in{p}") for p in range(2)]
        xe_mm = sem("xe_mm")
        xe_ok = sem("xe_ok")
        h_mm = sem("h_mm")
        h_act = sem("h_act")
        h_dve = sem("h_dve")
        y_mm = sem("y_mm")
        y_ok = sem("y_ok")
        y_out = [sem(f"y_out{p}") for p in range(2)]
        e_one = sem("e_one")
        g_idx = sem("g_idx")
        g_in = [sem(f"g_in{c}") for c in range(4)]
        e_sum = sem("e_sum")
        e_bn = sem("e_bn")
        e_mv = sem("e_mv")
        e_rs = sem("e_rs")
        e_out = sem("e_out")
        stored = [sem(f"stored{c}") for c in range(4)]

        block = ctx.enter_context(nc.Block())


        def bank(step, it):
            return (count(MISC, step, it) - 1) % 2

        def uses(step, it):
            return it.value((count(MISC, step, it) - 1) // 2 + 1, len(MISC) // 2)

        def uses_before(step, it):
            return it.value((count(MISC, step, it) - 1) // 2, len(MISC) // 2)

        def left(step, it):
            return emptied[bank(step, it)], uses(step, it)

        def in_order(units, name, it, back=0):
            return it.value(count(units, name, it) - back, len(units))

        def pair_of(name, it):
            return 2 * (count(SCORES, name, it) % 2)

        def self_part(main, latents, u):
            if u == 2:
                return latents[:, 0:4 * S].rearrange("p (r n) -> p r n", r=2)
            return main[:, 8 * S * u:8 * S * (u + 1)].rearrange("p (r n) -> p r n", r=2)

        def cross_part(whole, u):
            rows = whole[:, 12 * S * (u // 2):12 * S * (u // 2 + 1)].rearrange("p (r n) -> p r n", r=2)
            return rows[:, :, 0:4 * S] if u % 2 == 0 else rows[0:KN[2], :, 4 * S:6 * S]

        constants = [
            (ident, "ident"), (center, "center"), (average, "average"), (upto, "upto"),
            (select_f, "select"), (mask_q_f, "mask_q"), (mask_k_f, "mask_k"), (mask_l_f, "mask_l"),
            (some_key, "some_key"), (expert_id, "expert_id"), (own_head, "own_head"), (own_row, "own_row"), (parity, "parity"),
            (wqkv, "qkv_w"), (bqk, "qk_b"), (rqw, "rq_w"), (rqb, "rq_b"), (rkvw, "rkv_w"),
            (rkb, "rk_b"), (routw, "rout_w"), (outw, "out_w"), (Wq, "Wq"), (Wk, "Wk"), (bq2, "bq"),
            (bk2, "bk"), (WvT, "WvT"), (WpT, "WpT"), (norm4, "norm4"), (wsw, "w_switch"),
        ]
        rows = [
            (bv_self, "v_b"), (rvb, "rv_b"), (routb, "rout_b"), (outb, "out_b"), (glb, "gl"),
            (grb, "gr"), (bv_cross, "bv"), (bp, "bp"), (bsw, "b_switch"),
        ]
        N_CONST = 16 * (len(constants) + len(rows))

        @block.sync
        def _(sp):
            for tile, name in constants:
                sp.dma_start(tile[:], io[name]).then_inc(loaded_const, 16)
            for tile, name in rows:
                n = tile.shape[0]
                sp.dma_start(tile[:], io[name].partition_broadcast(n)).then_inc(loaded_const, 16)

            def load_c(b):
                p, n = b.parity, b.index()
                after = held(sp, b.done(back=2))
                sp.wait_ge(started, 1)
                sp.wait_ge(filled["K6"], after)
                sp.dma_start(cT[p][:], io["cT"][:, :, bass.ds(n * M, M)]).then_inc(loaded_c[p], 16)

            def load_x(b):
                p, n = b.parity, b.index()
                after = held(sp, b.done(back=2))
                sp.wait_ge(started, 1)
                sp.wait_ge(filled["A2"], after)
                sp.dma_start(xT[p][:], io["xT"][:, :, bass.ds(n * S, S)]).then_inc(loaded_x[p], 16)

            def load_n(b):
                p, n = b.parity, b.index()
                after = held(sp, b.done(per=5, back=2))
                sp.wait_ge(started, 1)
                sp.wait_ge(b_pool, after)
                sp.dma_start(xn[p][:], io["x"][bass.ds(n * S, S), :]).then_inc(loaded_n[p], 16)

            def stack(target, width, high, low, done):
                out = target[0:96, 0:8 * width].rearrange("p (t a n) -> p t a n", t=2, a=4)
                for a in range(4):
                    for row, half in enumerate((high, high, low) if target in Qst else (high, low, high)):
                        sp.dma_start(out[32 * row:32 * row + 32, :, a], half[32 * a:32 * a + 32]).then_inc(done, 16)

            def stack_keys(b):
                p = b.parity
                made, free = held(sp, b.done(per=2)), held(sp, b.done(back=2))
                sp.wait_ge(started, 1)
                sp.wait_ge(k_lo, made)
                sp.wait_ge(filled["T1"], free)
                stack(Kst[p], M, Kh, Klo, k_stack[p])

            def stack_queries(b):
                p = b.parity
                made, free = held(sp, b.done(per=3)), held(sp, b.done(back=2))
                sp.wait_ge(started, 1)
                sp.wait_ge(b_q, made)
                sp.wait_ge(filled["T1"], free)
                stack(Qst[p], 2 * S, Qh[:].rearrange("p t e q -> p t (e q)"), Qlo[:].rearrange("p t e q -> p t (e q)"), b_stack[p])

            load_x(Seq(0))

            def body(it):
                if it.n + 3 < B:
                    load_x(Seq(it.n + 3, it.j))
                if it.n + 2 < B:
                    load_c(Seq(it.n + 2, it.j))
                    load_n(Seq(it.n + 2, it.j))
                if it.has("K"):
                    stack_keys(it.of("K"))
                if it.has("B"):
                    stack_queries(it.of("B"))

            iterations(sp, body)

            def load_weights(e):
                p, n = e.parity, e.index()
                after = held(sp, e.done(per=2, back=2))
                sp.wait_ge(started, 1)
                sp.wait_ge(y_ok, after)
                sp.dma_start(W1[p][:], io["w1"][bass.ds(n, 1)].rearrange("a (k p) f -> p (a k) f", p=128)).then_inc(w_in[p], 16)
                sp.dma_start(W2[p][:], io["w2"][bass.ds(n, 1)].rearrange("a (k p) f -> p (a k) f", p=128)).then_inc(w_in[p], 16)
                sp.dma_start(b1[p][:], io["b1"][bass.ds(n, 1)].rearrange("a p f -> p (a f)")).then_inc(w_in[p], 16)
                sp.dma_start(b2[p][:], io["b2"][bass.ds(n, 1)].rearrange("a f -> (a f)").partition_broadcast(S)).then_inc(w_in[p], 16)

            def load_rows(e):
                p, n = e.parity, e.index()
                after = held(sp, e.done(back=2))
                sp.wait_ge(started, 1)
                sp.wait_ge(xe_mm, after)
                sp.dma_start(Xe[p][:], slots[bass.ds(n * CAP, CAP), :].rearrange("(s p) d -> p s d", p=S)).then_inc(xe_in[p], 16)

            sp.wait_ge(filled["T1"], B)
            load_weights(Seq(0))
            sp.wait_ge(k_lo, 2 * B)
            load_weights(Seq(1))
            sp.wait_ge(scattered, 16 * B)
            load_rows(Seq(0))
            load_rows(Seq(1))
            with sp.Fori(0, (E - 2) // 2) as j:
                for n in (2, 3):
                    load_rows(Seq(n, j))
                    load_weights(Seq(n, j))

            def store(j):
                for c in range(4):
                    after = held(sp, j * 4 + (c + 1))
                    sp.wait_ge(started, 1)
                    sp.wait_ge(e_out, after)
                    sp.dma_start(io["out"][bass.ds((j * 4 + c) * S, S), :], O3[c][:]).then_inc(stored[c], 16)

            rounds(sp, store)
            for c in range(4):
                sp.wait_ge(stored[c], 16 * (B // 4))

        @block.gpsimd
        def _(pool):
            pool.memset(wide[:], 0.0).then_inc(cast_const, 1)
            pool.memset(eps[:], EPS).then_inc(cast_const, 1)
            pool.memset(zero1[:], 0.0).then_inc(started, 1)
            pool.memset(negmax_s[:], 0.0).then_inc(cast_const, 1)
            pool.memset(negmax_x[:], 0.0).then_inc(cast_const, 1)
            for high in (Vsh, Vlh, Vxh[0], Vxh[1]):
                pool.memset(high[:], 1.0).then_inc(cast_const, 1)
            for low in (Vsl, Vll, Vxl[0], Vxl[1], Psh, Psl, Plh, Pll):
                pool.memset(low[:], 0.0).then_inc(cast_const, 1)
            for p in range(2):
                pool.memset(Qst[p][:], 0.0).then_inc(cast_const, 1)
                pool.memset(Kst[p], WEIGHT).then_inc(cast_const, 1)
            pool.memset(lift[:], LIFT).then_inc(cast_const, 1)
            pool.memset(ones[:], 1.0).then_inc(cast_const, 1)
            pool.memset(carry[1][:], -1.0).then_inc(cast_const, 1)
            pool.wait_ge(cast_const, 1)
            for n in range(0, E * CAP + B * S, E * CAP):
                pool.dma_start(slots[n:n + E * CAP, :].rearrange("(p n) d -> p (n d)", p=S),
                               wide[0:S, 0:16 * D]).then_inc(zeroed, 16)
            pool.wait_ge(loaded_const, N_CONST)
            pool.tensor_copy(identb[:], ident[:]).then_inc(cast_const, 1)
            pool.tensor_copy(select[:], select_f[:]).then_inc(cast_const, 1)
            pool.tensor_copy(mask_q[:], mask_q_f[:]).then_inc(cast_const, 1)
            pool.tensor_copy(mask_k[:], mask_k_f[:]).then_inc(cast_const, 1)
            pool.tensor_copy(mask_l[:], mask_l_f[:]).then_inc(cast_const, 1)
            pool.tensor_scalar(rkvh[:], rkvw[:], 0.5, None, ALU.mult).then_inc(cast_const, 1)
            pool.tensor_scalar(parity_s[:], parity[:], SCALE, None, ALU.mult).then_inc(cast_const, 1)
            pool.wait_ge(cast_const, POOL_CONST - 2)
            pool.tensor_scalar(gq2[:], parity_s[:], norm4[:, 0:1], None, ALU.mult).then_inc(cast_const, 1)
            pool.tensor_scalar(bq2n[:], parity_s[:], norm4[:, 1:2], None, ALU.mult).then_inc(cast_const, 1)
            pool.wait_ge(zeroed, 48)

            def pair_sums(b):
                pool.wait_ge(loaded_x[b.parity], b.pairs(16))
                pool.wait_ge(filled["A2"], b.done(back=1))
                x = xT[b.parity][:].rearrange("p t (n a) -> p t n a", a=2)
                pool.tensor_tensor(pairsum[:], x[:, :, :, 0], x[:, :, :, 1], ALU.add).then_inc(a_pool, 1)

            def cast_self(b, it):
                after1 = held(pool, uses("A1", it))
                after2 = held(pool, in_order(MAXIMA, "As1", it.before()) if it.n > FIRST else 0)
                pool.wait_ge(started, 1)
                pool.wait_ge(emptied[bank("A1", it)], after1)
                pool.wait_ge(max_full, after2)
                pool.tensor_copy(Qsb[:], Qs[:]).then_inc(a_cast, 1)
                pool.tensor_copy(Ksb[:], Ks[:]).then_inc(a_cast, 1)

            def cast_latent(b, it):
                after = held(pool, uses("A2", it))
                pool.wait_ge(started, 1)
                pool.wait_ge(emptied[bank("A2", it)], after)
                pool.tensor_copy(Qlb[:], Ql[:]).then_inc(a_cast, 1)
                pool.tensor_copy(Klb[:], Kl[:]).then_inc(a_cast, 1)

            def gate_local(b, it):
                pool.wait_ge(*left("A6", it.before()))
                pool.tensor_tensor(gate_l[:], Os[:, 0:H].rearrange("p h d -> p (h d)"), glb[:], ALU.mult).then_inc(b_pool, 1)
                pool.wait_ge(loaded_n[b.parity], b.pairs(16))
                pool.wait_ge(b_ln, b.done(per=3, back=1))
                pool.tensor_tensor(xob[:], xn[b.parity][:], outb[:], ALU.add).then_inc(b_pool, 1)

            def gate_remote(b, it):
                pool.wait_ge(*left("B2", it))
                pool.tensor_tensor(gate_r[:], rem[:], grb[:], ALU.mult).then_inc(b_pool, 1)
                pool.wait_ge(b_pool, b.done(per=5, k=3))
                pool.tensor_tensor(gate_t[:], gate_l[:], gate_r[:], ALU.add).then_inc(b_pool, 1)
                pool.tensor_tensor(differ[:], Os[:, 0:H].rearrange("p h d -> p (h d)"), rem[:], ALU.subtract).then_inc(b_pool, 1)

            def mix(b):
                pool.wait_ge(b_z, b.done(per=4))
                pool.wait_ge(filled["B3"], b.done(back=1))
                pool.tensor_tensor(mixed[:], gated[:], rem[:], ALU.add).then_inc(b_mixed, 1)

            def x1_bias(b):
                pool.wait_ge(b_ln, b.done(per=3))
                pool.wait_ge(t_ln, b.done(per=3, k=1, back=2))
                pool.tensor_tensor(x1bp[b.parity][:], x1[:], bp[:], ALU.add).then_inc(b_x1bp, 1)

            def value_bias(b, it):
                pool.wait_ge(*left("T1", it))
                pool.wait_ge(filled["T2"], b.done(back=1))
                pool.tensor_tensor(Oxb[:], Ox[:].rearrange("p h d -> p (h d)"), bv_cross[:], ALU.add).then_inc(t_pool, 1)

            def keep_x2(b):
                after = held(pool, b.done(per=3))
                pool.wait_ge(started, 1)
                pool.wait_ge(t_ln, after)
                pool.tensor_copy(x2_all[:, bass.ds(b.index(), 1), :].rearrange("p a d -> p (a d)"), x2[b.parity][:]).then_inc(t_keep, 1)

            def scatter(b):
                p = b.parity
                after1 = held(pool, b.done(per=7))
                after2 = held(pool, b.done(per=16, back=1))
                pool.wait_ge(started, 1)
                pool.wait_ge(t_pos, after1)
                pool.wait_ge(scattered, after2)
                pool.indirect_dma_start(
                    out=slots[:, :], out_offset=bass.IndirectOffsetOnAxis(ap=slot[p][:, 0:1], axis=0),
                    in_=x2[p][:], in_offset=None).then_inc(scattered, 16)

            def body(it):
                A, Bs, T = it.of("A"), it.of("B"), it.of("T")
                a, b, t = it.has("A"), it.has("B"), it.has("T")
                if b: gate_local(Bs, it)
                if a: pair_sums(A); cast_self(A, it)
                if b: gate_remote(Bs, it)
                if t: value_bias(T, it)
                if a: cast_latent(A, it)
                if b: mix(Bs)
                if t: keep_x2(T)
                if b: x1_bias(Bs)
                if t: scatter(T)

            iterations(pool, body)

            def gather(j, c):
                pool.tensor_copy(slot_g[c][:], slot_all[:, bass.ds(j * 4 + c, 1)]).then_inc(g_idx, 1)
                after = held(pool, j * 4 + (c + 1))
                pool.wait_ge(started, 1)
                pool.wait_ge(g_idx, after)
                pool.indirect_dma_start(
                    out=G[c][:], out_offset=None, in_=slots[:, :],
                    in_offset=bass.IndirectOffsetOnAxis(ap=slot_g[c][:, 0:1], axis=0)).then_inc(g_in[c], 16)

            for p in range(2):
                pool.wait_ge(y_out[p], 16 * (E // 2))
            pool.wait_ge(t_pos, 7 * B)

            def gather_round(j):
                used, arrived = held(pool, j * 4), held(pool, j * 16)
                pool.wait_ge(started, 1)
                pool.wait_ge(e_sum, used)
                for c in range(4):
                    pool.wait_ge(g_in[c], arrived)
                for c in range(4):
                    gather(j, c)

            rounds(pool, gather_round)

        @block.tensor
        def _(pe):
            pe.wait_ge(loaded_const, N_CONST)
            for n, w in enumerate((Wk, Wq)):
                for k in range(2):
                    for t in range(2):
                        mm = pe.matmul(MX[:, n, (2 * k + t) * 128:(2 * k + t + 1) * 128],
                                       w[:, t, k * 128:(k + 1) * 128], center[:], start=True, stop=True)
            mm.then_inc(weights_mm, 1)
            pe.matmul(MI[0][:, 0:2], center[:], bk2[:], start=True, stop=True)
            pe.matmul(MI[0][:, 2:4], center[:], bq2[:], start=True, stop=True).then_inc(weights_mm, 1)
            pe.wait_ge(weights_ok, 4)
            pe.wait_ge(cast_const, POOL_CONST)

            def enter(step, it, source=None):
                pe.wait_ge(emptied[bank(step, it)], uses_before(step, it))
                if source and bank(source, it) != bank(step, it):
                    pe.wait_ge(*left(source, it))
                return MI[bank(step, it)]

            def two(out, lhs, rhs):
                pe.matmul(out, lhs(0), rhs(0), start=True, stop=False)
                return pe.matmul(out, lhs(1), rhs(1), start=False, stop=True)

            def A1(it):
                b = it.of("A")
                p, ps = b.parity, enter("A1", it)
                pe.wait_ge(loaded_x[p], b.pairs(16))
                for m in range(4):
                    mm = two(ps[:, m * S:(m + 1) * S], lambda k: wqkv[:, k, m * 128:(m + 1) * 128],
                             lambda k: xT[p][:, k])
                mm.then_inc(filled["A1"], 1)

            def A2(it):
                b = it.of("A")
                p, ps = b.parity, enter("A2", it)
                pe.wait_ge(a_pool, b.done())
                two(ps[0:S, 0:D], lambda k: xT[p][:, k], lambda k: wqkv[:, k, 2 * D:3 * D])
                two(ps[0:64, 256:356], lambda k: rqw[:, k], lambda k: xT[p][:, k])
                two(ps[0:64, 356:406], lambda k: rkvh[:, k, 0:64], lambda k: pairsum[:, k])
                two(ps[0:NL, 406:470], lambda k: pairsum[:, k], lambda k: rkvh[:, k, 64:128]).then_inc(filled["A2"], 1)

            def self_maxima(it, g):
                b = it.of("A")
                pe.wait_ge(max_read, in_order(MAXIMA, f"As{g}", it, back=1))
                pe.wait_ge(a_cast, b.done(per=4))
                n = 500 if g == 0 else 400
                for i in range(2):
                    pe.matmul(MX[0:S, i, 0:n], identb[0:S, 0:S], mask_q[:, 0:n], start=True, stop=True)
                for t in range(2):
                    for e in range(2):
                        for i in range(2):
                            r = 32 * (2 * g + i)
                            c = (2 * t + e) * S
                            mm = pe.matmul(MX[0:S, i, c:c + S], Qsb[r:r + 32, t, e], Ksb[r:r + 32, t],
                                           start=False, stop=True, skip_group_check=True)
                if g == 0:
                    for e in range(2):
                        for i in range(2):
                            c = 400 + e * NL
                            mm = pe.matmul(MX[0:S, i, c:c + NL], Qlb[32 * i:32 * i + 32, e], Klb[32 * i:32 * i + 32],
                                           start=False, stop=True, skip_group_check=True)
                mm.then_inc(max_full, 1)

            def A4(it):
                ps = enter("A4", it)
                pe.wait_ge(max_read, in_order(MAXIMA, "As1", it))
                pe.transpose(ps[:, 0:S // 2].bitcast(BF16), negmax_s[:], identb[0:S, 0:S]).then_inc(filled["A4"], 1)

            def self_scores(it, u):
                first = pair_of(f"As{u}", it)
                after1 = held(pe, in_order(SCORES, f"As{u}", it, back=2))
                after2 = held(pe, uses("A4", it))
                pe.wait_ge(started, 1)
                pe.wait_ge(st_exp, after1)
                pe.wait_ge(emptied[bank("A4", it)], after2)
                nk, width = (S, 400) if u < 2 else (NL, 200)
                for i in range(2):
                    pe.matmul(ST[0:nk, first + i, 0:width], identb[0:nk, 0:nk], (mask_k if u < 2 else mask_l)[:],
                              start=True, stop=True)
                for t in range(2 if u < 2 else 1):
                    for i in range(2):
                        r = 32 * (2 * u + i) if u < 2 else 32 * i
                        out = ST[0:nk, first + i, t * 200:t * 200 + 200]
                        lhs = Ks[r:r + 32, t] if u < 2 else Kl[r:r + 32]
                        rhs = (Qs[r:r + 32, t] if u < 2 else Ql[r:r + 32]).rearrange("p e q -> p (e q)")
                        pe.matmul(out, lhs, rhs, start=False, stop=True, skip_group_check=True)
                    for e in range(2):
                        for i in range(2):
                            r = 32 * (2 * u + i) if u < 2 else 32 * i
                            c = t * 200 + e * S
                            row = 2 * t + e if u < 2 else 4 + e
                            mm = pe.matmul(ST[0:nk, first + i, c:c + S], select[r:r + 32, row, 0:nk], shift_s[r:r + 32],
                                           start=False, stop=True, skip_group_check=True)
                mm.then_inc(st_full, 1)

            def weighted(out, ph, pl, vh, vl, first, last):
                pe.matmul(out, ph, vh, start=first, stop=False)
                pe.matmul(out, ph, vl, start=False, stop=False)
                return pe.matmul(out, pl, vh, start=False, stop=last)

            def A6(it):
                ps = enter("A6", it)
                pe.wait_ge(st_low, in_order(SCORES, "As2", it))
                pe.wait_ge(a_vlo, it.of("A").done())
                for h in range(H):
                    t, r, e = h // 8, h % 8 // 2, h % 2
                    c = (4 * r + 2 * t + e) * S
                    weighted(ps[:, h * SP1:(h + 1) * SP1], Psh[:, c:c + 128], Psl[:, c:c + 128], Vsh[:, h], Vsl[:, h], True, True)
                for h in range(LH):
                    c = h * S
                    mm = weighted(ps[:, (H + h) * SP1:(H + h + 1) * SP1], Plh[:, c:c + 128], Pll[:, c:c + 128], Vlh[:, h], Vll[:, h], True, True)
                mm.then_inc(filled["A6"], 1)

            def B1(it):
                ps = MI[bank("B1", it)]
                source, there = left("A6", it.before())
                free, there = held(pe, uses_before("B1", it)), held(pe, there)
                pe.wait_ge(started, 1)
                pe.wait_ge(emptied[bank("B1", it)], free)
                if source is not emptied[bank("B1", it)]:
                    pe.wait_ge(source, there)
                pe.transpose(ps[0:64, 0:S], Os[:, H:H + LH].rearrange("p h d -> p (h d)"), ident[0:S, 0:S]).then_inc(filled["B1"], 1)

            def B2(it):
                ps = enter("B2", it, "B1")
                pe.matmul(ps[0:S, 0:D], latT[:], routw[:], start=True, stop=True).then_inc(filled["B2"], 1)

            def turned(step, it, source):
                ps = MI[bank(step, it)]
                for t in range(2):
                    mm = pe.transpose(ps[:, t * S:(t + 1) * S], source[:, t * 128:(t + 1) * 128], ident[0:S, 0:S])
                mm.then_inc(filled[step], 1)

            def B3(it):
                enter("B3", it)
                pe.wait_ge(b_mixed, it.of("B").done())
                turned("B3", it, mixed)

            def B4(it):
                ps = enter("B4", it, "B3")
                two(ps[0:S, 0:D], lambda k: mixT[:, k], lambda k: outw[:, k]).then_inc(filled["B4"], 1)

            def B5(it):
                enter("B5", it)
                pe.wait_ge(b_ln, it.of("B").done(per=3))
                turned("B5", it, x1)

            def B6(it):
                ps = enter("B6", it, "B5")
                for t in range(2):
                    mm = two(ps[:, t * S:(t + 1) * S], lambda k: WqC[:, k, t * 128:(t + 1) * 128], lambda k: x1T[:, k])
                mm.then_inc(filled["B6"], 1)

            def B7(it):
                ps = enter("B7", it, "B6")
                pe.matmul(ps[:, 0:2 * S], average[:], sqq[:].rearrange("p t q -> p (t q)"), start=True, stop=True).then_inc(filled["B7"], 1)

            def K12(it, t):
                step, b = f"K{t + 1}", it.of("K")
                p, ps = b.parity, enter(step, it)
                pe.wait_ge(loaded_c[p], b.pairs(16))
                two(ps[:, 0:M], lambda k: WkC[:, k, t * 128:(t + 1) * 128], lambda k: cT[p][:, k]).then_inc(filled[step], 1)

            def K34(it, t):
                step, b = f"K{t + 3}", it.of("K")
                ps = enter(step, it, f"K{t + 1}")
                pe.matmul(ps[:, 0:M], average[:], sqk[:, t], start=True, stop=True).then_inc(filled[step], 1)

            def K56(it, tiles):
                step, b = ("K5" if tiles[0] == 0 else "K6"), it.of("K")
                p, ps = b.parity, enter(step, it)
                for n, kt in enumerate(tiles):
                    mm = two(ps[0:KN[kt], n * D:(n + 1) * D], lambda k: cT[p][:, k, KO[kt]:KO[kt] + KN[kt]],
                             lambda k: WvT[:, k])
                mm.then_inc(filled[step], 1)

            def cross_maximum(it, n):
                b = it.of("X")
                p = b.parity
                back = 1 if MAXIMA[MAXIMA.index(f"X{n}") - 1] == "As1" and it.has("A") else 2
                pe.wait_ge(max_read, in_order(MAXIMA, f"X{n}", it, back=back))
                if n == 0:
                    pe.wait_ge(k_stack[p], b.pairs(16 * MOVES))
                    pe.wait_ge(b_stack[p], b.pairs(16 * MOVES))
                pe.matmul(MX[:, n % 2, 0:M], Qst[p][0:96, n * S:n * S + 128], Kst[p][0:96, n // 2 * M:(n // 2 + 1) * M],
                          start=True, stop=True).then_inc(max_full, 1)

            def X1(it):
                ps = enter("X1", it)
                pe.wait_ge(max_read, in_order(MAXIMA, "X15", it))
                pe.transpose(ps[:, 0:S // 2].bitcast(BF16), negmax_x[:], identb[0:S, 0:S]).then_inc(filled["X1"], 1)

            def cross_scores(it, u):
                p, first = it.of("X").parity, pair_of(f"X{u}", it)
                pe.wait_ge(st_exp, in_order(SCORES, f"X{u}", it, back=2))
                if u == 0:
                    pe.wait_ge(x_shift, it.of("X").done())
                if u == 4:
                    pe.wait_ge(*left("X1", it))
                for kt in ([0, 1] if u % 2 == 0 else [2]):
                    for i in range(2):
                        pair = u // 2 * 2 + i
                        k, c = pair * M + KO[kt], kt % 2 * 200
                        mm = pe.matmul(ST[:, first + i, c:c + 2 * S], Kst[p][:, k:k + 128], Qst[p][:, 2 * pair * S:2 * (pair + 1) * S],
                                       start=True, stop=True)
                mm.then_inc(st_full, 1)

            def T1(it):
                b = it.of("T")
                p, ps = b.parity, enter("T1", it)
                pe.wait_ge(st_low, it.value(st_count(it.n - 1), len(SCORES)))
                for h in range(H):
                    t, r, e = h // 8, h % 8 // 2, h % 2
                    for kt in range(3):
                        n, c = KN[kt], (12 * (2 * t + r // 2) + 6 * (r % 2) + 2 * kt + e) * S
                        mm = weighted(ps[:, h * SP1:(h + 1) * SP1], Pxh[0:n, c:c + 128], Pxl[0:n, c:c + 128],
                                      Vxh[p][0:n, kt, h], Vxl[p][0:n, kt, h], kt == 0, kt == 2)
                mm.then_inc(filled["T1"], 1)

            def T2(it):
                enter("T2", it)
                pe.wait_ge(t_pool, it.of("T").done())
                turned("T2", it, Oxb)

            def T3(it):
                ps = enter("T3", it, "T2")
                two(ps[0:S, 0:D], lambda k: OxT[:, k], lambda k: WpT[:, k]).then_inc(filled["T3"], 1)

            def T4(it):
                enter("T4", it)
                pe.wait_ge(t_ln, it.of("T").done(per=3))
                turned("T4", it, x2[it.of("T").parity])

            def T5(it):
                ps = enter("T5", it, "T4")
                two(ps[0:S, 0:E], lambda k: x2T[:, k], lambda k: wsw[:, k]).then_inc(filled["T5"], 1)

            def T6(it):
                ps = enter("T6", it)
                pe.wait_ge(t_top, it.of("T").done(per=5))
                pe.matmul(ps[0:S, 0:E], upto[:], onehot[:], start=True, stop=True)
                pe.matmul(ps[0:S, E:2 * E], ones[:], onehot[:], start=True, stop=True).then_inc(filled["T6"], 1)

            def body(it):
                a, k, b, x, t = (it.has(stage) for stage in "AKBXT")
                if a: A1(it)
                if x: cross_maximum(it, 0); cross_maximum(it, 1)
                if b: B1(it)
                if k: K12(it, 0)
                if x: cross_maximum(it, 2); cross_maximum(it, 3)
                if b: B2(it)
                if x: cross_maximum(it, 4)
                if t: T1(it)
                if x: cross_maximum(it, 5)
                if a: A2(it)
                if x: cross_maximum(it, 6)
                if k: K12(it, 1)
                if x: cross_maximum(it, 7)
                if t: T2(it)
                if x: cross_maximum(it, 8)
                if b: B3(it)
                if x: cross_maximum(it, 9)
                if k: K34(it, 0)
                if x: cross_maximum(it, 10)
                if t: T3(it)
                if b: B4(it)
                if x: cross_maximum(it, 11)
                if a: self_maxima(it, 0); self_maxima(it, 1)
                if k: K34(it, 1)
                if x: cross_maximum(it, 12)
                if t: T4(it)
                if x: cross_maximum(it, 13)
                if b: B5(it)
                if x: cross_maximum(it, 14)
                if t: T5(it)
                if x: cross_maximum(it, 15)
                if b: B6(it)
                if a: A4(it)
                if x: X1(it)
                if k: K56(it, [0, 1])
                if b: B7(it)
                if a: self_scores(it, 0); self_scores(it, 1)
                if t: T6(it)
                if x: cross_scores(it, 0)
                if a: self_scores(it, 2)
                if x: cross_scores(it, 1)
                if k: K56(it, [2])
                if x: cross_scores(it, 2)
                if a: A6(it)
                if x: cross_scores(it, 3); cross_scores(it, 4); cross_scores(it, 5); cross_scores(it, 6)
                if x: cross_scores(it, 7)

            iterations(pe, body)

            def expert(e):
                p = e.parity
                pe.wait_ge(xe_in[p], e.pairs(16))
                pe.wait_ge(xe_ok, e.done(back=1))
                for s in range(2):
                    for k in range(2):
                        mm = pe.transpose(MI[0][:, k * CAP + s * S:k * CAP + (s + 1) * S], Xe[p][:, s, k * 128:(k + 1) * 128],
                                          ident[0:S, 0:S])
                mm.then_inc(xe_mm, 1)
                pe.wait_ge(xe_ok, e.done())
                pe.wait_ge(w_in[p], e.pairs(64))
                for q in range(4):
                    pe.wait_ge(h_act if q % 2 == 0 else h_dve, e.done(per=2, k=q // 2 + 1, back=1))
                    for m in (2 * q, 2 * q + 1):
                        mm = two(ST[:, q, m % 2 * CAP:(m % 2 + 1) * CAP], lambda k: W1[p][:, k, m * 128:(m + 1) * 128],
                                 lambda k: XeT[:, k])
                    mm.then_inc(h_mm, 1)
                pe.wait_ge(h_act, e.done(per=2))
                pe.wait_ge(h_dve, e.done(per=2))
                pe.wait_ge(y_ok, e.done(per=2, back=1))
                for s in range(2):
                    for m in range(8):
                        mm = pe.matmul(MX[0:S, s, 0:D], hT[:, m, s * S:(s + 1) * S], W2[p][:, m], start=(m == 0), stop=(m == 7))
                    mm.then_inc(y_mm, 1)

            expert(Seq(0))
            expert(Seq(1))
            with pe.Fori(0, (E - 2) // 2) as j:
                expert(Seq(2, j))
                expert(Seq(3, j))

        @block.scalar
        def _(act):
            act.preload_act_table_set("natural_log_exp_and_others")
            act.wait_ge(cast_const, POOL_CONST)
            act.wait_ge(weights_ok, 4)
            act.wait_ge(zeroed, 48)

            def leave(ins, step, it):
                ins.then_inc(emptied[bank(step, it)], 1)

            def copy_out(step, it, out, source, free=None):
                act.wait_ge(filled[step], it.of(step[0]).done())
                if free:
                    act.wait_ge(*free)
                leave(act.activation(out, source(MI[bank(step, it)]), ACT.Copy), step, it)

            def K12(it, t):
                step, b = f"K{t + 1}", it.of("K")
                act.wait_ge(filled[step], b.done())
                act.wait_ge(k_n, b.done(per=2, k=t + 1, back=1))
                act.activation(kc[:, t], MI[bank(step, it)][:, 0:M], ACT.Identity, bias=bkC[:, t:t + 1]).then_inc(k_c, 1)
                act.wait_ge(filled[f"K{t + 3}"], b.done(back=1))
                leave(act.activation(sqk[:, t], MI[bank(step, it)][:, 0:M], ACT.Square, bias=bkC[:, t:t + 1]), step, it)

            def K34(it, t):
                step, b = f"K{t + 3}", it.of("K")
                act.wait_ge(filled[step], b.done())
                act.wait_ge(k_rs, b.done(per=2, k=t + 1, back=1))
                leave(act.activation(lnk[:, t], MI[bank(step, it)][:, 0:M], ACT.Ln, bias=eps[:]), step, it)
                act.wait_ge(*left(step, it))
                act.wait_ge(k_n, b.done(per=2, k=t + 1, back=1))
                act.activation(rsk[:, t], lnk[:, t], ACT.Exp, scale=-0.5).then_inc(k_rs, 1)

            def rstd(b, out, log, mv, made, sem_):
                act.wait_ge(made, b.done(per=3, k=2))
                act.wait_ge(made, b.done(per=3, back=1))
                act.activation(log[:], mv[:, 1:2], ACT.Ln, bias=eps[0:S]).then_inc(sem_, 1)
                act.wait_ge(sem_, b.done(per=2, k=1))
                act.activation(out[:], log[:], ACT.Exp, scale=-0.5).then_inc(sem_, 1)

            def self_exp(it, u):
                b, first = it.of("A"), pair_of(f"As{u}", it)
                act.wait_ge(st_full, in_order(SCORES, f"As{u}", it))
                if u == 0:
                    act.wait_ge(filled["A6"], b.done(back=1))
                if it.n > FIRST or u >= 2:
                    act.wait_ge(st_low, in_order(SCORES, f"As{u}", it, back=2))
                n, width = (S, 400) if u < 2 else (NL, 200)
                out, source = self_part(Psh, Plh, u), ST[0:n, first:first + 2, 0:width]
                act.activation(out, source, ACT.Exp, bias=lift[0:n])
                act.activation(Pf[0:n, first // 2, :, 0:width], source, ACT.Exp, bias=lift[0:n]).then_inc(st_exp, 1)

            def cross_exp(it, u):
                b, first = it.of("X"), pair_of(f"X{u}", it)
                act.wait_ge(st_full, in_order(SCORES, f"X{u}", it))
                if u == 0:
                    act.wait_ge(filled["T1"], b.done(back=1))
                act.wait_ge(st_low, in_order(SCORES, f"X{u}", it, back=2))
                n, width = (KN[0], 400) if u % 2 == 0 else (KN[2], 200)
                source = ST[0:n, first:first + 2, 0:width]
                act.activation(cross_part(Pxh, u), source, ACT.Exp, bias=lift[0:n])
                act.activation(Pf[0:n, first // 2, :, 0:width], source, ACT.Exp, bias=lift[0:n]).then_inc(st_exp, 1)

            def self_vhi(it):
                b = it.of("A")
                act.wait_ge(a_vals, b.done())
                act.wait_ge(filled["A6"], b.done(back=1))
                act.activation(Vsh[:, :, 0:HD], Vs[:], ACT.Copy)
                act.activation(Vlh[:, :, 0:HD], Vl[:], ACT.Copy).then_inc(a_vhi, 1)

            def cross_vhi(it, tiles):
                step, b = ("K5" if tiles[0] == 0 else "K6"), it.of("K")
                act.wait_ge(filled[step], b.done())
                act.wait_ge(filled["T1"], b.done(back=2))
                for i, kt in enumerate(tiles):
                    ins = act.activation(Vxh[b.parity][0:KN[kt], kt, :, 0:HD],
                                         MI[bank(step, it)][0:KN[kt], i * D:(i + 1) * D].rearrange("p (h d) -> p h d", d=HD), ACT.Copy)
                ins.then_inc(k_vhi, 1)

            def gate_exp(it):
                b = it.of("B")
                act.wait_ge(b_z, b.done(per=4, k=1))
                act.activation(gate_e[:], gate_z[:], ACT.Exp, scale=-1.0).then_inc(b_e, 1)

            def B6(it):
                act.wait_ge(filled["B6"], it.of("B").done())
                act.wait_ge(b_q, it.of("B").done(per=3, k=1, back=1))
                for t in range(2):
                    ins = act.activation(qc[:, t], MI[bank("B6", it)][:, t * S:(t + 1) * S], ACT.Identity, bias=bqC[:, t:t + 1])
                ins.then_inc(b_c, 1)
                act.wait_ge(filled["B7"], it.of("B").done(back=1))
                for t in range(2):
                    ins = act.activation(sqq[:, t], MI[bank("B6", it)][:, t * S:(t + 1) * S], ACT.Square, bias=bqC[:, t:t + 1])
                leave(ins, "B6", it)

            def B7(it):
                b = it.of("B")
                act.wait_ge(filled["B7"], b.done())
                leave(act.activation(lnq[:].rearrange("p t q -> p (t q)"), MI[bank("B7", it)][:, 0:2 * S], ACT.Ln, bias=eps[:]), "B7", it)
                act.wait_ge(*left("B7", it))
                act.activation(rsq[:], lnq[:], ACT.Exp, scale=-0.5).then_inc(b_rsq, 1)

            def high_k(it, t):
                b = it.of("K")
                act.wait_ge(k_n, b.done(per=2, k=t + 1))
                if t == 0:
                    act.wait_ge(k_stack[1 - b.parity], Seq(b.n - 1, b.j).pairs(16 * MOVES))
                act.activation(Kh[:, t], kn[:, t], ACT.Identity, bias=norm4[:, 3:4]).then_inc(k_hi, 1)

            def high_q(it):
                b = it.of("B")
                act.wait_ge(b_q, b.done(per=3, k=2))
                act.wait_ge(b_stack[1 - b.parity], Seq(b.n - 1, b.j).pairs(16 * MOVES))
                act.activation(Qh[:], Qx[:], ACT.Copy).then_inc(b_qh, 1)

            def router_exp(it):
                b = it.of("T")
                act.wait_ge(t_top, b.done(per=5, k=2))
                act.wait_ge(t_exp, b.done(back=1))
                act.activation(exps8[:], logits[:], ACT.Exp, bias=negtop[:], accum_out=sum8[:, bass.ds(b.index(), 1)]).then_inc(t_exp, 1)

            halves = lambda ps: ps[:, 0:2 * S].rearrange("p (t q) -> p t q", t=2)
            shifts = lambda ps: ps[:, 0:S // 2].bitcast(BF16)

            def body(it):
                a, k, b, x, t = (it.has(stage) for stage in "AKBXT")
                if b: copy_out("B1", it, latT[:], lambda ps: ps[0:64, 0:S])
                if k: K12(it, 0)
                if b: gate_exp(it)
                if a: self_vhi(it)
                if k: K12(it, 1)
                if t: copy_out("T2", it, OxT[:], halves)
                if b: copy_out("B3", it, mixT[:], halves)
                if k: K34(it, 0)
                if t: rstd(it.of("T"), rs2, ln2, mv2, t_ln, t_rs)
                if b: rstd(it.of("B"), rs1, ln1, mv1, b_ln, b_rs)
                if k: high_k(it, 0); K34(it, 1)
                if t: copy_out("T4", it, x2T[:], halves)
                if b: copy_out("B5", it, x1T[:], halves)
                if k: high_k(it, 1)
                if b: B6(it)
                if a: copy_out("A4", it, shift_s[:], shifts)
                if k: cross_vhi(it, [0, 1])
                if b: B7(it)
                if a: self_exp(it, 0)
                if t: router_exp(it)
                if b: high_q(it)
                if a: self_exp(it, 1)
                if x: cross_exp(it, 0)
                if a: self_exp(it, 2)
                if x: cross_exp(it, 1)
                if k: cross_vhi(it, [2])
                if x: cross_exp(it, 2); cross_exp(it, 3); cross_exp(it, 4); cross_exp(it, 5)
                if x: cross_exp(it, 6); cross_exp(it, 7)

            iterations(act, body)

            def expert(e):
                p = e.parity
                act.wait_ge(xe_mm, e.done())
                act.wait_ge(h_mm, e.done(per=4, back=1))
                act.activation(XeT[:], MI[0][:, 0:2 * CAP].rearrange("p (k c) -> p k c", k=2), ACT.Copy).then_inc(xe_ok, 1)
                for q in (0, 2):
                    act.wait_ge(h_mm, e.done(per=4, k=q + 1))
                    if q == 0:
                        act.wait_ge(y_mm, e.done(per=2, back=1))
                    for m in (2 * q, 2 * q + 1):
                        ins = act.activation(hT[:, m], ST[:, q, m % 2 * CAP:(m % 2 + 1) * CAP], ACT.Relu, bias=b1[p][:, m:m + 1])
                    ins.then_inc(h_act, 1)
                act.wait_ge(y_ok, e.done(per=2))
                act.dma_start(slots[bass.ds(e.index() * CAP, CAP), :].rearrange("(s p) d -> p s d", p=S), Y[p][:]).then_inc(y_out[p], 16)

            expert(Seq(0))
            expert(Seq(1))
            with act.Fori(0, (E - 2) // 2) as j:
                expert(Seq(2, j))
                expert(Seq(3, j))

            def rstd_round(j):
                act.wait_ge(e_mv, j * 4 + 4)
                act.wait_ge(e_out, j * 4)
                act.activation(ln3[:], mv3[:, :, 1], ACT.Ln, bias=eps[0:S]).then_inc(e_rs, 1)
                act.wait_ge(e_rs, j * 2 + 1)
                act.activation(rs3[:], ln3[:], ACT.Exp, scale=-0.5).then_inc(e_rs, 1)

            rounds(act, rstd_round)

        @block.vector
        def _(dve):
            dve.wait_ge(weights_mm, 2)
            for n, w in enumerate((WkC, WqC)):
                dve.tensor_copy(w[:].rearrange("p k o -> p (k o)"), MX[:, n]).then_inc(weights_ok, 1)
            dve.tensor_copy(bkC[:], MI[0][:, 0:2]).then_inc(weights_ok, 1)
            dve.tensor_copy(bqC[:], MI[0][:, 2:4]).then_inc(weights_ok, 1)
            dve.wait_ge(cast_const, POOL_CONST)

            def leave(ins, step, it):
                ins.then_inc(emptied[bank(step, it)], 1)

            def A1(it):
                b, ps = it.of("A"), MI[bank("A1", it)]
                dve.wait_ge(filled["A1"], b.done())
                if it.n > FIRST:
                    dve.wait_ge(st_full, it.value(self_scores_before(it), len(SCORES)))
                dve.wait_ge(a_cast, b.done(per=4, k=2, back=1))
                for t in range(2):
                    for e in range(2):
                        dve.tensor_scalar(Qs[:, t, e], ps[:, t * S:(t + 1) * S], bqk[:, t:t + 1], parity_s[:, e:e + 1], ALU.add, ALU.mult)
                    ins = dve.tensor_scalar(Ks[:, t], ps[:, (2 + t) * S:(3 + t) * S], bqk[:, 2 + t:3 + t], None, ALU.add)
                leave(ins, "A1", it)

            def A2(it):
                b, ps = it.of("A"), MI[bank("A2", it)]
                dve.wait_ge(filled["A2"], b.done())
                dve.wait_ge(filled["A6"], b.done(back=1))
                dve.wait_ge(a_cast, b.done(per=4, back=1))
                heads = lambda ap: ap.rearrange("p (h d) -> p h d", d=HD)
                dve.tensor_tensor(Vs[:], heads(ps[0:S, 0:D]), heads(bv_self[:]), ALU.add)
                for e in range(2):
                    dve.tensor_scalar(Ql[:, e], ps[0:64, 256:356], rqb[:], parity_s[0:64, e:e + 1], ALU.add, ALU.mult)
                dve.tensor_tensor(Vl[:], heads(ps[0:NL, 406:470]), heads(rvb[:]), ALU.add).then_inc(a_vals, 1)
                leave(dve.tensor_scalar(Kl[:], ps[0:64, 356:406], rkb[:], None, ALU.add), "A2", it)

            def self_max(it, g):
                dve.wait_ge(max_full, in_order(MAXIMA, f"As{g}", it))
                if g == 0:
                    dve.wait_ge(filled["A4"], it.of("A").done(back=1))
                out = negmax_s[:].rearrange("p (r u) -> p r u", u=32)
                if g == 0:
                    dve.tensor_reduce(out[:, 0:2, 4:6], MX[0:S, :, 400:500].rearrange("p i (e k) -> p i e k", k=NL), X, ALU.max, negate=True)
                dve.tensor_reduce(out[:, 2 * g:2 * g + 2, 0:4], MX[0:S, :, 0:400].rearrange("p i (u k) -> p i u k", k=S), X, ALU.max,
                                  negate=True).then_inc(max_read, 1)

            def self_vlo(it):
                dve.wait_ge(a_vhi, it.of("A").done())
                dve.tensor_tensor(Vsl[:, :, 0:HD], Vs[:], Vsh[:, :, 0:HD], ALU.subtract)
                dve.tensor_tensor(Vll[:, :, 0:HD], Vl[:], Vlh[:, :, 0:HD], ALU.subtract).then_inc(a_vlo, 1)

            def self_low(it, u):
                b, first = it.of("A"), pair_of(f"As{u}", it)
                n, width = (S, 400) if u < 2 else (NL, 200)
                dve.wait_ge(st_exp, in_order(SCORES, f"As{u}", it))
                if u == 0:
                    dve.wait_ge(filled["A6"], b.done(back=1))
                dve.tensor_tensor(self_part(Psl, Pll, u), Pf[0:n, first // 2, :, 0:width], self_part(Psh, Plh, u),
                                  ALU.subtract).then_inc(st_low, 1)

            def cross_low(it, u):
                b, first = it.of("X"), pair_of(f"X{u}", it)
                n, width = (KN[0], 400) if u % 2 == 0 else (KN[2], 200)
                dve.wait_ge(st_exp, in_order(SCORES, f"X{u}", it))
                if u == 0:
                    dve.wait_ge(filled["T1"], b.done(back=1))
                dve.tensor_tensor(cross_part(Pxl, u), Pf[0:n, first // 2, :, 0:width], cross_part(Pxh, u),
                                  ALU.subtract).then_inc(st_low, 1)

            def cross_max(it, n):
                dve.wait_ge(max_full, in_order(MAXIMA, f"X{n}", it))
                if n == 0:
                    dve.wait_ge(filled["X1"], it.of("X").done(back=1))
                dve.tensor_reduce(negmax_x[:, 96 + n:97 + n], MX[0:S, n % 2, 0:M], X, ALU.max, negate=True).then_inc(max_read, 1)

            def shift_rows(it):
                b = it.of("X")
                dve.wait_ge(filled["X1"], b.done())
                negmax = MI[bank("X1", it)][96:112, 0:S // 2].bitcast(BF16).unsqueeze(1).to_broadcast([H, 8, S])
                rows = Qst[b.parity][96:112, 0:H * S].rearrange("p (h q) -> p h q", q=S)
                for t in range(2):
                    ins = dve.tensor_tensor(rows[:, 8 * t:8 * t + 8], negmax,
                                            own_head[96:112, 8 * t:8 * t + 8].unsqueeze(2).to_broadcast([H, 8, S]), ALU.mult)
                    if t == 0:
                        ins.then_inc(x_shift, 1)
                leave(ins, "X1", it)

            def A6(it):
                b = it.of("A")
                dve.wait_ge(filled["A6"], b.done())
                heads = MI[bank("A6", it)][0:S, 0:(H + LH) * SP1].rearrange("p (h d) -> p h d", d=SP1)
                dve.wait_ge(b_pool, b.done(per=5, back=1))
                dve.reciprocal(recip_s[:], heads[:, :, HD]).then_inc(a_dve, 1)
                dve.wait_ge(a_dve, b.done(per=2, k=1))
                dve.tensor_tensor(recip_m[:], recip_s[:], some_key[:], ALU.mult).then_inc(a_dve, 1)
                dve.wait_ge(a_dve, b.done(per=2))
                leave(dve.tensor_tensor(Os[:], heads[:, :, 0:HD], recip_m[:].unsqueeze(2).to_broadcast([S, H + LH, HD]), ALU.mult), "A6", it)

            def B2(it):
                dve.wait_ge(filled["B2"], it.of("B").done())
                dve.wait_ge(b_mixed, it.of("B").done(back=1))
                leave(dve.tensor_tensor(rem[:], MI[bank("B2", it)][0:S, 0:D], routb[:], ALU.add), "B2", it)

            def gate_sum(it):
                b = it.of("B")
                dve.wait_ge(b_pool, b.done(per=5, k=4))
                dve.tensor_reduce(gate_z[:], gate_t[:].rearrange("p (h d) -> p h d", d=HD), X, ALU.add).then_inc(b_z, 1)

            def gating(it):
                b = it.of("B")
                dve.wait_ge(b_e, b.done())
                dve.tensor_scalar(gate_d[:], gate_e[:], 1.0, None, ALU.add).then_inc(b_z, 1)
                dve.wait_ge(b_z, b.done(per=4, k=2))
                dve.reciprocal(gate[:], gate_d[:]).then_inc(b_z, 1)
                dve.wait_ge(b_z, b.done(per=4, k=3))
                dve.wait_ge(b_pool, b.done(per=5))
                heads = lambda x: x[:].rearrange("p (h d) -> p h d", d=HD)
                dve.tensor_tensor(heads(gated), heads(differ), gate[:].unsqueeze(2).to_broadcast([S, H, HD]), ALU.mult).then_inc(b_z, 1)

            def B4(it):
                b = it.of("B")
                dve.wait_ge(filled["B4"], b.done())
                dve.wait_ge(b_pool, b.done(per=5, k=2))
                leave(dve.tensor_tensor(res1[:], MI[bank("B4", it)][0:S, 0:D], xob[:], ALU.add), "B4", it)
                dve.wait_ge(*left("B4", it))
                dve.bn_stats(bn1[:], res1[:]).then_inc(b_ln, 1)
                after = held(dve, b.done(per=3, k=1))
                dve.wait_ge(started, 1)
                dve.wait_ge(b_ln, after)
                dve.bn_aggr(mv1[:], bn1[:]).then_inc(b_ln, 1)

            def norm1(it):
                b = it.of("B")
                dve.wait_ge(b_rs, b.done(per=2))
                dve.wait_ge(filled["B5"], b.done(back=1))
                dve.wait_ge(b_x1bp, b.done(back=1))
                dve.tensor_scalar(x1[:], res1[:], mv1[:, 0:1], rs1[:], ALU.subtract, ALU.mult).then_inc(b_ln, 1)

            def queries(it):
                b = it.of("B")
                p = b.parity
                dve.wait_ge(b_rsq, b.done())
                dve.tensor_tensor(qn[:], qc[:], rsq[:], ALU.mult).then_inc(b_q, 1)
                dve.wait_ge(b_q, b.done(per=3, k=1))
                dve.wait_ge(b_qh, b.done(back=1))
                dve.tensor_scalar(Qx[:, :, 0], qn[:], gq2[:, 0:1], bq2n[:, 0:1], ALU.mult, ALU.add)
                dve.tensor_scalar(Qx[:, :, 1], qn[:], gq2[:, 1:2], bq2n[:, 1:2], ALU.mult, ALU.add).then_inc(b_q, 1)

            def query_low(it):
                b = it.of("B")
                dve.wait_ge(b_qh, b.done())
                dve.wait_ge(b_stack[1 - b.parity], Seq(b.n - 1, b.j).pairs(16 * MOVES))
                dve.tensor_tensor(Qlo[:], Qx[:], Qh[:], ALU.subtract).then_inc(b_q, 1)

            def key_norm(it, t):
                b = it.of("K")
                dve.wait_ge(k_rs, b.done(per=2, k=t + 1))
                dve.wait_ge(k_hi, b.done(per=2, k=t + 1, back=1))
                dve.scalar_tensor_tensor(kn[:, t], kc[:, t], norm4[:, 2:3], rsk[:, t], ALU.mult, ALU.mult).then_inc(k_n, 1)

            def key_low(it, t):
                b = it.of("K")
                p = b.parity
                dve.wait_ge(k_hi, b.done(per=2, k=t + 1))
                if t == 0:
                    dve.wait_ge(k_stack[1 - p], Seq(b.n - 1, b.j).pairs(16 * MOVES))
                dve.scalar_tensor_tensor(Klo[:, t], kn[:, t], norm4[:, 3:4], Kh[:, t], ALU.add, ALU.subtract).then_inc(k_lo, 1)

            def values(it, tiles):
                step, b = ("K5" if tiles[0] == 0 else "K6"), it.of("K")
                dve.wait_ge(k_vhi, b.done(per=2, k=1 if tiles[0] == 0 else 2))
                dve.wait_ge(filled["T1"], b.done(back=2))
                for i, kt in enumerate(tiles):
                    ins = dve.tensor_tensor(Vxl[b.parity][0:KN[kt], kt, :, 0:HD],
                                            MI[bank(step, it)][0:KN[kt], i * D:(i + 1) * D].rearrange("p (h d) -> p h d", d=HD),
                                            Vxh[b.parity][0:KN[kt], kt, :, 0:HD], ALU.subtract)
                leave(ins, step, it)

            def T1(it):
                b = it.of("T")
                dve.wait_ge(filled["T1"], b.done())
                dve.wait_ge(t_pool, b.done(back=1))
                heads = MI[bank("T1", it)][0:S, 0:H * SP1].rearrange("p (h d) -> p h d", d=SP1)
                dve.reciprocal(recip_x[:], heads[:, :, HD]).then_inc(t_dve, 1)
                dve.wait_ge(t_dve, b.done())
                leave(dve.tensor_tensor(Ox[:], heads[:, :, 0:HD], recip_x[:].unsqueeze(2).to_broadcast([S, H, HD]), ALU.mult), "T1", it)

            def T3(it):
                b = it.of("T")
                dve.wait_ge(filled["T3"], b.done())
                dve.wait_ge(b_x1bp, b.done())
                leave(dve.tensor_tensor(res2[:], MI[bank("T3", it)][0:S, 0:D], x1bp[b.parity][:], ALU.add), "T3", it)
                dve.wait_ge(*left("T3", it))
                dve.bn_stats(bn2[:], res2[:]).then_inc(t_ln, 1)
                after = held(dve, b.done(per=3, k=1))
                dve.wait_ge(started, 1)
                dve.wait_ge(t_ln, after)
                dve.bn_aggr(mv2[:], bn2[:]).then_inc(t_ln, 1)

            def norm2(it):
                b = it.of("T")
                dve.wait_ge(t_rs, b.done(per=2))
                dve.wait_ge(scattered, b.done(per=16, back=1))
                dve.tensor_scalar(x2[b.parity][:], res2[:], mv2[:, 0:1], rs2[:], ALU.subtract, ALU.mult).then_inc(t_ln, 1)

            def route_to(it):
                b = it.of("T")
                dve.wait_ge(filled["T5"], b.done())
                dve.wait_ge(t_exp, b.done(back=1))
                leave(dve.tensor_tensor(logits[:], MI[bank("T5", it)][0:S, 0:E], bsw[:], ALU.add), "T5", it)
                after = held(dve, uses("T5", it))
                dve.wait_ge(started, 1)
                dve.wait_ge(emptied[bank("T5", it)], after)
                dve.max(top8[:], logits[:]).then_inc(t_top, 1)
                dve.wait_ge(t_top, b.done(per=5, k=1))
                dve.tensor_scalar(negtop[:], top8[:, 0:1], -1.0, None, ALU.mult).then_inc(t_top, 1)
                dve.max_index(index8[:], top8[:], logits[:]).then_inc(t_top, 1)
                dve.wait_ge(t_top, b.done(per=5, k=3))
                dve.wait_ge(t_pos, b.done(per=7, back=1))
                dve.tensor_copy(route[:], index8[:, 0:1]).then_inc(t_top, 1)
                dve.wait_ge(t_top, b.done(per=5, k=4))
                dve.tensor_scalar(onehot[:], expert_id[:], route[:], None, ALU.is_equal).then_inc(t_top, 1)

            def place_in(it):
                b = it.of("T")
                p, ps = b.parity, MI[bank("T6", it)]
                dve.wait_ge(filled["T6"], b.done())
                dve.tensor_tensor(place[:], ps[0:S, 0:E], carry[1 - p][:], ALU.add).then_inc(t_pos, 1)
                leave(dve.tensor_tensor(carry[p][:], ps[0:S, E:2 * E], carry[1 - p][:], ALU.add), "T6", it)
                dve.wait_ge(t_pos, b.done(per=7, k=1))
                dve.tensor_tensor_reduce(place1[:], place[:], onehot[:], 1.0, 0.0, ALU.mult, ALU.add, pos[:]).then_inc(t_pos, 1)
                dve.wait_ge(t_pos, b.done(per=7, k=2))
                dve.tensor_scalar(keep[:], pos[:], float(CAP), None, ALU.is_lt)
                dve.scalar_tensor_tensor(slot0[:], route[:], float(CAP), pos[:], ALU.mult, ALU.add).then_inc(t_pos, 1)
                dve.wait_ge(t_pos, b.done(per=7, k=3))
                own = own_row[:, bass.ds(b.index(), 1)]
                dve.tensor_tensor(slot1[:], slot0[:], own, ALU.subtract).then_inc(t_pos, 1)
                dve.wait_ge(t_pos, b.done(per=7, k=4))
                dve.scalar_tensor_tensor(slot2[:], slot1[:], keep[:], own, ALU.mult, ALU.add).then_inc(t_pos, 1)
                dve.wait_ge(t_pos, b.done(per=7, k=5))
                dve.wait_ge(*left("T6", it))
                dve.tensor_copy(slot_all[:, bass.ds(b.index(), 1)], slot2[:]).then_inc(t_pos, 1)
                dve.wait_ge(scattered, b.done(per=16, back=1))
                dve.tensor_copy(slot[p][:], slot2[:]).then_inc(t_pos, 1)

            def body(it):
                a, k, b, x, t = (it.has(stage) for stage in "AKBXT")
                if a: A1(it)
                if x: cross_max(it, 0); cross_max(it, 1); cross_max(it, 2); cross_max(it, 3)
                if b: B2(it)
                if x: cross_max(it, 4)
                if t: T1(it)
                if b: gate_sum(it)
                if x: cross_max(it, 5)
                if a: A2(it)
                if x: cross_max(it, 6)
                if b: gating(it)
                if x: cross_max(it, 7); cross_max(it, 8)
                if a: self_vlo(it)
                if x: cross_max(it, 9); cross_max(it, 10)
                if t: T3(it)
                if b: B4(it)
                if x: cross_max(it, 11)
                if a: self_max(it, 0); self_max(it, 1)
                if t: norm2(it)
                if x: cross_max(it, 12)
                if b: norm1(it)
                if x: cross_max(it, 13)
                if k: key_norm(it, 0)
                if x: cross_max(it, 14)
                if t: route_to(it)
                if k: key_norm(it, 1)
                if x: cross_max(it, 15)
                if k: key_low(it, 0); key_low(it, 1)
                if x: shift_rows(it)
                if k: values(it, [0, 1])
                if b: queries(it)
                if a: self_low(it, 0)
                if b: query_low(it)
                if a: self_low(it, 1)
                if t: place_in(it)
                if x: cross_low(it, 0)
                if a: self_low(it, 2)
                if x: cross_low(it, 1)
                if k: values(it, [2])
                if x: cross_low(it, 2)
                if a: A6(it)
                if x: cross_low(it, 3); cross_low(it, 4); cross_low(it, 5); cross_low(it, 6)
                if x: cross_low(it, 7)

            iterations(dve, body)

            dve.wait_ge(t_exp, B)
            dve.reciprocal(pmax[:], sum8[:]).then_inc(e_one, 1)
            dve.wait_ge(e_one, 1)
            dve.reciprocal(pinv[:], pmax[:]).then_inc(e_one, 1)
            dve.wait_ge(e_one, 2)
            dve.tensor_tensor(pone[:], pmax[:], pinv[:], ALU.mult).then_inc(e_one, 1)

            def expert(e):
                p = e.parity
                for q in (1, 3):
                    dve.wait_ge(h_mm, e.done(per=4, k=q + 1))
                    if q == 1:
                        dve.wait_ge(y_mm, e.done(per=2, back=1))
                    for m in (2 * q, 2 * q + 1):
                        ins = dve.tensor_scalar(hT[:, m], ST[:, q, m % 2 * CAP:(m % 2 + 1) * CAP], b1[p][:, m:m + 1], 0.0, ALU.add, ALU.max)
                    ins.then_inc(h_dve, 1)
                dve.wait_ge(y_out[p], e.pairs(16, back=1))
                for s in range(2):
                    dve.wait_ge(y_mm, e.done(per=2, k=s + 1))
                    dve.tensor_tensor(Y[p][:, s], MX[0:S, s, 0:D], b2[p][:], ALU.add).then_inc(y_ok, 1)

            expert(Seq(0))
            expert(Seq(1))
            with dve.Fori(0, (E - 2) // 2) as j:
                expert(Seq(2, j))
                expert(Seq(3, j))

            dve.wait_ge(e_one, 3)
            dve.wait_ge(t_keep, B)

            def last_round(j):
                for c in range(4):
                    n = j * 4 + c
                    dve.wait_ge(g_in[c], j * 16 + 16)
                    if c == 0:
                        dve.wait_ge(e_out, j * 4)
                    x2n = x2_all[:, bass.ds(n, 1), :].rearrange("p a d -> p (a d)")
                    dve.scalar_tensor_tensor(R[c][:], G[c][:], pone[:, bass.ds(n, 1)], x2n, ALU.mult, ALU.add).then_inc(e_sum, 1)
                for c in range(4):
                    dve.wait_ge(e_sum, j * 4 + (c + 1))
                    dve.bn_stats(bn3[:, c], R[c][:]).then_inc(e_bn, 1)
                for c in range(4):
                    after = held(dve, j * 4 + (c + 1))
                    dve.wait_ge(started, 1)
                    dve.wait_ge(e_bn, after)
                    dve.bn_aggr(mv3[:, c], bn3[:, c]).then_inc(e_mv, 1)
                dve.wait_ge(e_rs, j * 2 + 2)
                for c in range(4):
                    dve.wait_ge(stored[c], j * 16)
                    dve.tensor_scalar(O3[c][:], R[c][:], mv3[:, c, 0:1], rs3[:, c:c + 1], ALU.subtract, ALU.mult).then_inc(e_out, 1)

            rounds(dve, last_round)


POOL_CONST = 32


def st_count(n):
    return sum(OFFSET[u[0]] + i in range(B) for i in range(FIRST, n + 1) for u in SCORES)


def self_scores_before(it):
    return count(SCORES, "As2", It(it.n - 1))


def kernel(**inputs):
    import concourse.bacc as bacc
    from concourse.bass_utils import run_bass_kernel_spmd

    w = {k[3:]: np.asarray(v) for k, v in inputs.items() if k.startswith("L0_")}
    x = np.asarray(inputs["x"])
    c = np.asarray(inputs["ctx_1024"])

    def halves(a):
        return a.reshape(2, 128, -1).transpose(1, 0, 2)

    f = np.float32
    rows, cols = np.arange(128)[:, None], np.arange(128)[None, :]
    same_head = (rows // HD == cols // HD).astype(f)
    select = np.zeros((128, 6, 128), f)
    for r in range(4):
        for u in range(6):
            select[32 * r + u, u] = 1
    q = np.arange(S)[:, None]
    self_mask = np.where(np.arange(S)[None, :] >= q, NEG, 0).astype(f)
    latent_mask = np.where(np.arange(NL)[None, :] >= q // 2, NEG, 0).astype(f)
    some = np.ones((S, H + LH), f)
    some[0, :H] = 0
    some[0:2, H:] = 0
    arrays = {
        "ident": np.eye(128, dtype=f), "center": np.eye(128, dtype=f) - same_head / HD, "average": same_head / HD,
        "upto": (np.arange(S)[:, None] <= np.arange(S)[None, :]).astype(f), "select": select,
        "mask_q": np.concatenate([self_mask] * 4 + [latent_mask] * 2, axis=1),
        "mask_k": np.concatenate([self_mask.T] * 4, axis=1), "mask_l": np.concatenate([latent_mask.T] * 2, axis=1),
        "some_key": some, "expert_id": np.tile(np.arange(E, dtype=f), (S, 1)),
        "own_head": np.concatenate([np.zeros((96, H), f), np.eye(H, dtype=f) / WEIGHT]),
        "own_row": (E * CAP + np.arange(B)[None, :] * S + q).astype(f),
        "parity": np.stack([(np.arange(128) // HD % 2 == e).astype(f) for e in range(2)], axis=1),
        "qkv_w": halves(w["attn_qkv_w"]), "qk_b": w["attn_qkv_b"][:2 * D].reshape(4, 128).T,
        "rq_w": halves(w["attn_rq_w"]), "rq_b": w["attn_rq_b"][:, None], "rkv_w": halves(w["attn_rkv_w"]),
        "rk_b": w["attn_rkv_b"][:64, None], "rout_w": w["attn_rout_w"], "out_w": halves(w["attn_out_w"]),
        "Wq": halves(w["xattn_Wq"]), "Wk": halves(w["xattn_Wk"]), "bq": w["xattn_bq"].reshape(2, 128).T,
        "bk": w["xattn_bk"].reshape(2, 128).T, "WvT": halves(w["xattn_Wv"].T), "WpT": halves(w["xattn_Wp"].T),
        "norm4": np.stack([np.tile(w[f"xattn_{n}"], 8) for n in ("q_gamma", "q_beta", "k_gamma", "k_beta")], axis=1),
        "w_switch": halves(w["ffn_w_switch"]),
        "v_b": w["attn_qkv_b"][2 * D:], "rv_b": w["attn_rkv_b"][64:], "rout_b": w["attn_rout_b"], "out_b": w["attn_out_b"],
        "gl": np.tile(w["attn_gl_w"][:, 0], H), "gr": np.tile(w["attn_gr_w"][:, 0], H), "bv": w["xattn_bv"], "bp": w["xattn_bp"],
        "b_switch": w["ffn_b_switch"],
        "cT": halves(c.reshape(B * M, D).T), "xT": halves(x.reshape(B * S, D).T), "x": x.reshape(B * S, D),
        "w1": w["ffn_w1"], "w2": w["ffn_w2"], "b1": w["ffn_b1"].reshape(E, 8, 128).transpose(0, 2, 1), "b2": w["ffn_b2"],
    }
    nc = bacc.Bacc("TRN2", target_bir_lowering=False, num_devices=1)
    given, io = {}, {}
    for name, a in arrays.items():
        given[f"in_{name}"] = np.ascontiguousarray(a)
        io[name] = nc.dram_tensor(f"in_{name}", a.shape, F32, kind="ExternalInput").ap()
    io["out"] = nc.dram_tensor("out_x", (B * S, D), F32, kind="ExternalOutput").ap()
    decoder_kernel(nc, io)
    r = run_bass_kernel_spmd(nc, [given], core_ids=[0])
    return r.results[0]["out_x"].reshape(B, S, D)
```

```python
from contextlib import ExitStack

import numpy as np

import concourse.bass as bass
from concourse import mybir

ALU = mybir.AluOpType
ACT = mybir.ActivationFunctionType
X = mybir.AxisListType.X
F32, BF16, F16, U32 = mybir.dt.float32, mybir.dt.bfloat16, mybir.dt.float16, mybir.dt.uint32

B, S, D = 32, 100, 256
M = 361
H, HD = 16, 16
NL, LH = 50, 4
E, F, CAP = 8, 1024, 200
KN = [128, 128, M - 256]
KO = [0, 128, 256]
NEG = -1.0e30
EPS = 1e-5
SCALE = HD ** -0.5
SP1 = HD + 1
LIFT = 4.0
WEIGHT = 64.0
HIGH, LOW = 0, 1
Q_ROWS = (HIGH, HIGH, LOW)
K_ROWS = (HIGH, LOW, HIGH)
PAD = 128 - S

FIRST, LAST = -2, B + 1
OFFSET = {"T": -2, "Y": -1, "X": 0, "K": 1, "A": 2, "B": 1}

MISC = ["A1", "A2", "K1", "B1", "T2", "K2", "B2", "T3", "K3", "T4", "B3", "K4", "B4", "T5", "A4",
        "B5", "T6", "X1", "B6", "B7", "Y1", "K5", "A6", "K6"]
MAXIMA = ["X0", "X1", "X2", "X3", "X4", "X5", "X6", "X7", "X8", "X9", "X10", "X11", "X12", "As0",
          "As1", "X13", "X14", "X15"]
SCORES = ["Y0", "Y1", "Y2", "Y3", "Y4", "Y5", "Y6", "Y7", "As0", "As1", "As2"]


class It:

    def __init__(self, n, j=None):
        self.n, self.j = n, j

    def value(self, here, per_iteration):
        return max(here, 0) if self.j is None else self.j * (2 * per_iteration) + here

    def before(self):
        return It(self.n - 1, self.j)

    def has(self, stage):
        return 0 <= self.n + OFFSET[stage] < B

    def of(self, stage):
        return Seq(self.n + OFFSET[stage], self.j)


class Seq:

    def __init__(self, n, j=None):
        self.n, self.j, self.parity = n, j, n % 2

    def done(self, per=1, k=None, back=0):
        here = (self.n - back) * per + (per if k is None else k)
        return max(here, 0) if self.j is None else self.j * (2 * per) + here

    def pairs(self, per, k=None, back=0):
        here = (self.n // 2 - back) * per + (per if k is None else k)
        return max(here, 0) if self.j is None else self.j * per + here

    def index(self):
        return self.n if self.j is None else self.j * 2 + self.n


SMALL = [("ident", 128, [128]), ("center", 128, [128]), ("average", 128, [128]), ("upto", S, [S]),
         ("some_key", S, [H + LH]), ("expert_id", S, [E]), ("own_head", 112, [H]), ("own_row", S, [B]),
         ("parity", 128, [2]), ("own20", 20, [20]), ("qk_b", 128, [4]), ("rq_b", 64, [1]), ("rk_b", 64, [1]),
         ("bq", 128, [2]), ("bk", 128, [2]), ("norm4", 128, [4])]
WEIGHTS = [("qkv_w", 128, [2, 3 * D]), ("rq_w", 128, [2, 64]), ("rkv_w", 128, [2, 128]), ("rout_w", 64, [D]),
           ("out_w", 128, [2, D]), ("WvT", 128, [2, D]), ("WpT", 128, [2, D]), ("w_switch", 128, [2, E])]
ROWS = [("v_b", S, [D]), ("rv_b", NL, [64]), ("rout_b", S, [D]), ("out_b", S, [D]), ("gl", S, [D]), ("gr", S, [D]),
        ("bv", S, [D]), ("bp", S, [D]), ("b_switch", S, [E])]


def columns(specs):
    return sum(int(np.prod(shape)) for _, _, shape in specs)


def held(eng, value):
    return value if isinstance(value, int) else eng.to_reg(value)


def count(units, name, it):
    before = sum(OFFSET[u[0]] + i in range(B) for i in range(FIRST, it.n) for u in units)
    here = [u for u in units if it.has(u[0])]
    return before + here.index(name) + 1


def iterations(eng, body):
    for n in range(FIRST, 5):
        body(It(n))
    with eng.Fori(0, (B - 8) // 2) as j:
        body(It(5, j))
        body(It(6, j))
    for n in range(B - 3, LAST + 1):
        body(It(n))


def rounds(eng, body):
    body(Seq(0))
    body(Seq(1))
    with eng.Fori(0, (B // 4 - 2) // 2) as j:
        body(Seq(2, j))
        body(Seq(3, j))


def decoder_kernel(nc, io):
    ctx = ExitStack()
    with ctx:
        def sb(name, shape, dt=F32):
            return ctx.enter_context(nc.sbuf_tensor(name, shape, dt))

        def sem(name):
            return ctx.enter_context(nc.semaphore(name))

        MI = [ctx.enter_context(nc.psum_tensor(f"MI{n}", [128, 512], F32)) for n in range(2)]
        MX = ctx.enter_context(nc.psum_tensor("MX", [128, 2, 512], F32))
        ST = ctx.enter_context(nc.psum_tensor("ST", [128, 4, 512], F32))

        early = sb("early", [128, 4 * F])
        wide = sb("wide", [128, 4828])

        self_stack = sb("self_stack", [128, 2 * F])
        stacked = sb("stacked", [128, 2 * 1456])

        def part(region, at, shape):
            n = int(np.prod(shape[1:]))
            ap = region[0:shape[0], at:at + n]
            names = "abcde"[:len(shape) - 1]
            sizes = dict(zip(names, shape[1:]))
            return ap.rearrange(f"p ({' '.join(names)}) -> p {' '.join(names)}", **sizes)

        small = sb("small", [128, columns(SMALL)])
        weights = sb("weights", [128, columns(WEIGHTS)])
        biases = sb("biases", [S, columns(ROWS)])

        def laid(region, specs, name):
            n = [spec[0] for spec in specs].index(name)
            return part(region, columns(specs[:n]), [specs[n][1], *specs[n][2]])

        ident = laid(small, SMALL, "ident")
        identb = sb("identb", [128, 128], BF16)
        center = laid(small, SMALL, "center")
        average = laid(small, SMALL, "average")
        upto = laid(small, SMALL, "upto")
        ones = sb("ones", [S, S])
        mask_s_f = part(early, 0, [120, 2, S])
        mask_s = sb("mask_s", [120, 20 * S], BF16)
        eye20_f = part(early, 2500, [120, 128])
        eye20 = sb("eye20", [120, 128], BF16)
        own20 = laid(small, SMALL, "own20")
        mask_q_f = part(early, 2000, [S, S + NL])
        mask_q = sb("mask_q", [S, 500], BF16)
        some_key = laid(small, SMALL, "some_key")
        expert_id = laid(small, SMALL, "expert_id")
        own_row = laid(small, SMALL, "own_row")
        parity = laid(small, SMALL, "parity")
        eps = sb("eps", [128, 1])
        zero1 = sb("zero1", [128, 1])
        lift = sb("lift", [128, 1])

        wqkv = laid(weights, WEIGHTS, "qkv_w")
        bqk = laid(small, SMALL, "qk_b")
        bv_self = laid(biases, ROWS, "v_b")
        rqw = laid(weights, WEIGHTS, "rq_w")
        rqb = laid(small, SMALL, "rq_b")
        rkvw = laid(weights, WEIGHTS, "rkv_w")
        rkvh = sb("rkvh", [128, 2, 128])
        rkb = laid(small, SMALL, "rk_b")
        rvb = laid(biases, ROWS, "rv_b")
        routw = laid(weights, WEIGHTS, "rout_w")
        routb = laid(biases, ROWS, "rout_b")
        outw = laid(weights, WEIGHTS, "out_w")
        outb = laid(biases, ROWS, "out_b")
        glb = laid(biases, ROWS, "gl")
        grb = laid(biases, ROWS, "gr")
        Wq = part(early, 2628, [128, 2, D])
        Wk = part(early, 3140, [128, 2, D])
        WqC = sb("WqC", [128, 2, D])
        WkC = sb("WkC", [128, 2, D])
        bq2 = laid(small, SMALL, "bq")
        bk2 = laid(small, SMALL, "bk")
        bqC = sb("bqC", [128, 2])
        bkC = sb("bkC", [128, 2])
        WvT = laid(weights, WEIGHTS, "WvT")
        WpT = laid(weights, WEIGHTS, "WpT")
        bv_cross = laid(biases, ROWS, "bv")
        bp = laid(biases, ROWS, "bp")
        norm4 = laid(small, SMALL, "norm4")
        parity_s = sb("parity_s", [128, 2])
        gq2 = sb("gq2", [128, 2])
        bq2n = sb("bq2n", [128, 2])
        wsw = laid(weights, WEIGHTS, "w_switch")
        bsw = laid(biases, ROWS, "b_switch")

        xT = [sb(f"xT{p}", [128, 2, S]) for p in range(2)]
        xn = [sb(f"xn{p}", [S, D]) for p in range(2)]
        pairsum = sb("pairsum", [128, 2, NL])
        QK = sb("QK", [128, 3, 3 * S])
        QKhl = sb("QKhl", [128, 2, 9 * S], F16)
        QKst = self_stack[0:96, 0:18 * S].bitcast(F16).rearrange("p (g n) -> p g n", g=12)
        Vs = sb("Vs", [S, H, HD])
        Vsh = sb("Vsh", [S, H, SP1], F16)
        Vsl = sb("Vsl", [S, H, SP1], F16)
        Vl = sb("Vl", [NL, LH, HD])
        Vlh = sb("Vlh", [NL, LH, SP1], F16)
        Vll = sb("Vll", [NL, LH, SP1], F16)
        negmax_s = sb("negmax_s", [S, 128], BF16)
        Psh = sb("Psh", [S, 16 * S + PAD], F16)
        Psl = sb("Psl", [S, 16 * S + PAD], F16)
        Plh = sb("Plh", [NL, 4 * S + PAD], F16)
        Pll = sb("Pll", [NL, 4 * S + PAD], F16)
        recip_s = sb("recip_s", [S, H + LH])
        recip_m = sb("recip_m", [S, H + LH])
        Os = sb("Os", [S, H + LH, HD])

        latT = sb("latT", [64, S])
        rem = sb("rem", [S, D])
        gate_l = sb("gate_l", [S, D])
        gate_r = sb("gate_r", [S, D])
        gate_t = sb("gate_t", [S, D])
        differ = sb("differ", [S, D])
        gate_z = sb("gate_z", [S, H])
        gate_e = sb("gate_e", [S, H])
        gate_d = sb("gate_d", [S, H])
        gate = sb("gate", [S, H])
        gated = sb("gated", [S, D])
        mixed = sb("mixed", [S, D])
        mixT = sb("mixT", [128, 2, S])
        xob = sb("xob", [S, D])
        res1 = sb("res1", [S, D])
        bn1 = sb("bn1", [S, 6])
        mv1 = sb("mv1", [S, 2])
        ln1 = sb("ln1", [S, 1])
        rs1 = sb("rs1", [S, 1])
        x1 = sb("x1", [S, D])
        x1T = sb("x1T", [128, 2, S])
        qc = sb("qc", [128, 2, S])
        sqq = sb("sqq", [128, 2, S])
        lnq = sb("lnq", [128, 2, S])
        rsq = sb("rsq", [128, 2, S])
        qn = sb("qn", [128, 2, S])
        Qx = sb("Qx", [128, 2, 2, S])
        Qhl = sb("Qhl", [128, 2, 4 * S], F16)
        Qst = [sb(f"Qst{p}", [112, H * S + PAD], F16) for p in range(2)]
        Kst = [stacked[0:112, 1456 * p:1456 * (p + 1)].bitcast(F16) for p in range(2)]
        own_head = laid(small, SMALL, "own_head")

        cT = [sb(f"cT{p}", [128, 2, M]) for p in range(2)]
        kc = part(early, 0 * 2 * M, [128, 2, M])
        sqk = part(early, 1 * 2 * M, [128, 2, M])
        lnk = part(early, 2 * 2 * M, [128, 2, M])
        rsk = part(early, 3 * 2 * M, [128, 2, M])
        kn = part(early, 4 * 2 * M, [128, 2, M])
        Khl = sb("Khl", [128, 2, 2 * M], F16)
        Vxh = [sb(f"Vxh{p}", [128, 3, H, SP1], F16) for p in range(2)]
        Vxl = [sb(f"Vxl{p}", [128, 3, H, SP1], F16) for p in range(2)]

        turned_s = sb("turned_s", [20, S], BF16)
        negmax_x = sb("negmax_x", [S, 128], BF16)
        Pxh = wide[:, 0:2414].bitcast(F16)
        Pxl = wide[:, 2414:4828].bitcast(F16)
        Pf = sb("Pf", [128, 2, 2, 400])
        recip_x = sb("recip_x", [S, H])
        Ox = sb("Ox", [S, H, HD])
        Oxb = sb("Oxb", [S, D])
        OxT = sb("OxT", [128, 2, S])
        res2 = sb("res2", [S, D])
        bn2 = sb("bn2", [S, 6])
        mv2 = sb("mv2", [S, 2])
        ln2 = sb("ln2", [S, 1])
        rs2 = sb("rs2", [S, 1])
        x2 = [sb(f"x2{p}", [S, D]) for p in range(2)]
        x2T = sb("x2T", [128, 2, S])
        x2_all = sb("x2_all", [S, B, D])
        logits = sb("logits", [S, E])
        top8 = sb("top8", [S, 8])
        negtop = sb("negtop", [S, 1])
        index8 = sb("index8", [S, 8], U32)
        route = sb("route", [S, 1])
        onehot = sb("onehot", [S, E])
        exps8 = sb("exps8", [S, E])
        sum8 = sb("sum8", [S, B])
        carry = [sb(f"carry{p}", [S, E]) for p in range(2)]
        place = sb("place", [S, E])
        place1 = sb("place1", [S, E])
        pos = sb("pos", [S, 1])
        keep = sb("keep", [S, 1])
        slot0 = sb("slot0", [S, 1])
        slot1 = sb("slot1", [S, 1])
        slot2 = sb("slot2", [S, 1])
        slot = [sb(f"slot{p}u", [S, 1], U32) for p in range(2)]
        slot_all = sb("slot_all", [S, B], U32)

        W1 = [part(self_stack, 0, [128, 2, F]), part(early, 0, [128, 2, F])]
        W2 = [part(stacked, 0, [128, 8, D]), part(early, 2 * F, [128, 8, D])]
        b1 = [sb(f"b1{p}", [128, 8]) for p in range(2)]
        b2 = [sb(f"b2{p}", [S, D]) for p in range(2)]
        Xe = [part(wide, 2000 + 512 * p, [S, 2, D]) for p in range(2)]
        XeT = part(wide, 1600, [128, 2, CAP])
        hT = part(wide, 0, [128, 8, CAP])
        Y = [part(wide, 3024 + 512 * p, [S, 2, D]) for p in range(2)]
        pmax = sb("pmax", [S, B])
        pinv = sb("pinv", [S, B])
        pone = sb("pone", [S, B])
        slot_g = [sb(f"slot_g{c}", [S, 1], U32) for c in range(8)]
        G = [part(early, (0 + c) * D, [S, D]) for c in range(8)]
        R = [part(early, (8 + c) * D, [S, D]) for c in range(4)]
        bn3 = sb("bn3", [S, 4, 6])
        mv3 = sb("mv3", [S, 4, 2])
        ln3 = sb("ln3", [S, 4])
        rs3 = sb("rs3", [S, 4])
        O3 = [part(early, (12 + c) * D, [S, D]) for c in range(4)]

        slots = nc.dram_tensor("slots", (E * CAP + B * S, D), F32, kind="Internal").ap()
        self_halves = nc.dram_tensor("self_halves", (2, 128, 9 * S), F16, kind="Internal").ap()
        key_halves = nc.dram_tensor("key_halves", (2, 128, 2 * M), F16, kind="Internal").ap()
        query_halves = nc.dram_tensor("query_halves", (2, 128, 4 * S), F16, kind="Internal").ap()

        loaded_const = sem("loaded_const")
        cast_const = sem("cast_const")
        started = sem("started")
        zeroed = sem("zeroed")
        weights_mm = sem("weights_mm")
        weights_ok = sem("weights_ok")
        loaded_x = [sem(f"loaded_x{p}") for p in range(2)]
        loaded_n = [sem(f"loaded_n{p}") for p in range(2)]
        loaded_c = [sem(f"loaded_c{p}") for p in range(2)]
        filled = {s: sem(f"filled_{s}") for s in MISC}
        emptied = [sem(f"emptied_MI{n}") for n in range(2)]
        max_full = sem("max_full")
        max_read = sem("max_read")
        st_full = sem("st_full")
        st_exp = sem("st_exp")
        st_low = sem("st_low")
        a_vals = sem("a_vals")
        a_vhi = sem("a_vhi")
        a_vlo = sem("a_vlo")
        k_vhi = sem("k_vhi")
        a_pool = sem("a_pool")
        a_hi = sem("a_hi")
        a_lo = sem("a_lo")
        a_out = sem("a_out")
        a_stack = sem("a_stack")
        a_dve = sem("a_dve")
        b_pool = sem("b_pool")
        b_mixed = sem("b_mixed")
        b_z = sem("b_z")
        b_e = sem("b_e")
        b_ln = sem("b_ln")
        b_rs = sem("b_rs")
        b_x1bp = sem("b_x1bp")
        b_c = sem("b_c")
        b_out = sem("b_out")
        b_stack = [sem(f"b_stack{p}") for p in range(2)]
        k_out = sem("k_out")
        k_stack = [sem(f"k_stack{p}") for p in range(2)]
        a_shift = sem("a_shift")
        b_rsq = sem("b_rsq")
        b_q = sem("b_q")
        b_ql = sem("b_ql")
        b_qh = sem("b_qh")
        k_c = sem("k_c")
        k_rs = sem("k_rs")
        k_n = sem("k_n")
        k_hi = sem("k_hi")
        k_lo = sem("k_lo")
        t_dve = sem("t_dve")
        t_pool = sem("t_pool")
        t_ln = sem("t_ln")
        t_rs = sem("t_rs")
        t_keep = sem("t_keep")
        t_top = sem("t_top")
        t_exp = sem("t_exp")
        t_pos = sem("t_pos")
        scattered = sem("scattered")
        w_in = [sem(f"w_in{p}") for p in range(2)]
        xe_in = [sem(f"xe_in{p}") for p in range(2)]
        xe_mm = sem("xe_mm")
        xe_ok = sem("xe_ok")
        h_mm = sem("h_mm")
        h_act = sem("h_act")
        h_dve = sem("h_dve")
        y_mm = sem("y_mm")
        y_ok = sem("y_ok")
        y_out = [sem(f"y_out{p}") for p in range(2)]
        e_one = sem("e_one")
        g_idx = sem("g_idx")
        g_in = [sem(f"g_in{c}") for c in range(8)]
        e_sum = sem("e_sum")
        e_bn = sem("e_bn")
        e_mv = sem("e_mv")
        e_rs = sem("e_rs")
        e_out = sem("e_out")
        stored = [sem(f"stored{c}") for c in range(4)]

        block = ctx.enter_context(nc.Block())


        def bank(step, it):
            return (count(MISC, step, it) - 1) % 2

        def uses(step, it):
            return it.value((count(MISC, step, it) - 1) // 2 + 1, len(MISC) // 2)

        def uses_before(step, it):
            return it.value((count(MISC, step, it) - 1) // 2, len(MISC) // 2)

        def left(step, it):
            return emptied[bank(step, it)], uses(step, it)

        def in_order(units, name, it, back=0):
            return it.value(count(units, name, it) - back, len(units))

        def pair_of(name, it):
            return 2 * (count(SCORES, name, it) % 2)

        def self_part(main, latents, u):
            if u == 2:
                return latents[:, 0:4 * S].rearrange("p (r n) -> p r n", r=2)
            return main[:, 8 * S * u:8 * S * (u + 1)].rearrange("p (r n) -> p r n", r=2)

        def cross_part(whole, u):
            rows = whole[:, 12 * S * (u // 2):12 * S * (u // 2 + 1)].rearrange("p (r n) -> p r n", r=2)
            return rows[:, :, 0:4 * S] if u % 2 == 0 else rows[0:KN[2], :, 4 * S:6 * S]

        constants = [(small, "small"), (Wk, "Wk"), (Wq, "Wq"), (mask_s_f, "mask_s"), (mask_q_f, "mask_q"),
                     (eye20_f, "eye20"), (weights, "weights")]
        N_CONST = 16 * (len(constants) + 1)

        @block.sync
        def _(sp):
            for tile, name in constants:
                sp.dma_start(tile[:], io[name]).then_inc(loaded_const, 16)
            sp.dma_start(biases[:], io["biases"].partition_broadcast(S)).then_inc(loaded_const, 16)

            def load_c(b):
                p, n = b.parity, b.index()
                after = held(sp, b.done(back=2))
                sp.wait_ge(started, 1)
                sp.wait_ge(filled["K6"], after)
                sp.dma_start(cT[p][:], io["cT"][:, :, bass.ds(n * M, M)]).then_inc(loaded_c[p], 16)

            def load_x(b):
                p, n = b.parity, b.index()
                after = held(sp, b.done(back=2))
                sp.wait_ge(started, 1)
                sp.wait_ge(filled["A2"], after)
                sp.dma_start(xT[p][:], io["xT"][:, :, bass.ds(n * S, S)]).then_inc(loaded_x[p], 16)

            def load_n(b):
                p, n = b.parity, b.index()
                after = held(sp, b.done(per=5, back=2))
                sp.wait_ge(started, 1)
                sp.wait_ge(b_pool, after)
                sp.dma_start(xn[p][:], io["x"][bass.ds(n * S, S), :]).then_inc(loaded_n[p], 16)

            def groups(halves, which, tiles):
                return halves[which].rearrange("(a x) (t n) -> x t a n", a=4, t=tiles)

            def stack_self(it):
                a = it.of("A")
                made, read = held(sp, a.done()), held(sp, a.done(per=80, back=1))
                sp.wait_ge(started, 1)
                sp.wait_ge(a_lo, made)
                sp.wait_ge(a_stack, read)
                sp.dma_start(self_halves.rearrange("h p n -> p h n"), QKhl[:]).then_inc(a_out, 16)
                out, free = held(sp, a.done(per=16)), held(sp, in_order(SCORES, "As2", it.before()) if it.n > FIRST else 0)
                sp.wait_ge(started, 1)
                sp.wait_ge(a_out, out)
                sp.wait_ge(st_full, free)
                rows = QKst.rearrange("p (t a) n -> p t a n", a=4)
                sp.dma_start(rows[0:32], groups(self_halves, HIGH, 3)).then_inc(a_stack, 16)
                for row in (1, 2):
                    for part_of, which in ((slice(0, 2 * S), Q_ROWS[row]), (slice(2 * S, 3 * S), K_ROWS[row])):
                        for_rows = rows[32 * row:32 * row + 32, :, :, part_of]
                        sp.dma_start(for_rows, groups(self_halves, which, 3)[:, :, :, part_of]).then_inc(a_stack, 16)

            def stack(it, b, target, source, halves, order, made, count_made, out, stacked):
                ready, read = held(sp, b.done(per=count_made)), held(sp, Seq(b.n - 1, b.j).pairs(48))
                sp.wait_ge(started, 1)
                sp.wait_ge(made, ready)
                sp.wait_ge(stacked[1 - b.parity], read)
                sp.dma_start(halves.rearrange("h p n -> p h n"), source[:]).then_inc(out, 16)
                there, free = held(sp, b.done(per=16)), held(sp, in_order(SCORES, "Y7", it) if it.has("Y") else 0)
                sp.wait_ge(started, 1)
                sp.wait_ge(out, there)
                sp.wait_ge(st_full, free)
                width = source.shape[2] // 2
                rows = target[0:96, 0:8 * width].rearrange("p (t a n) -> p t a n", t=2, a=4)
                for row, which in enumerate(order):
                    sp.dma_start(rows[32 * row:32 * row + 32], groups(halves, which, 2)).then_inc(stacked[b.parity], 16)

            def stack_keys(it):
                b = it.of("K")
                stack(it, b, Kst[b.parity], Khl, key_halves, K_ROWS, k_lo, 2, k_out, k_stack)

            def stack_queries(it):
                b = it.of("B")
                stack(it, b, Qst[b.parity], Qhl, query_halves, Q_ROWS, b_ql, 1, b_out, b_stack)

            load_x(Seq(0))

            def body(it):
                if it.n + 3 < B:
                    load_x(Seq(it.n + 3, it.j))
                if it.n + 2 < B:
                    load_c(Seq(it.n + 2, it.j))
                    load_n(Seq(it.n + 2, it.j))
                if it.has("A"):
                    stack_self(it)
                if it.has("K"):
                    stack_keys(it)
                if it.has("B"):
                    stack_queries(it)

            iterations(sp, body)

            def load_weights(e):
                p, n = e.parity, e.index()
                after = held(sp, e.done(per=2, back=2))
                sp.wait_ge(started, 1)
                sp.wait_ge(y_ok, after)
                sp.dma_start(W1[p][:], io["w1"][bass.ds(n, 1)].rearrange("a (k p) f -> p (a k) f", p=128)).then_inc(w_in[p], 16)
                sp.dma_start(W2[p][:], io["w2"][bass.ds(n, 1)].rearrange("a (k p) f -> p (a k) f", p=128)).then_inc(w_in[p], 16)
                sp.dma_start(b1[p][:], io["b1"][bass.ds(n, 1)].rearrange("a p f -> p (a f)")).then_inc(w_in[p], 16)
                sp.dma_start(b2[p][:], io["b2"][bass.ds(n, 1)].rearrange("a f -> (a f)").partition_broadcast(S)).then_inc(w_in[p], 16)

            def load_rows(e):
                p, n = e.parity, e.index()
                after = held(sp, e.done(back=2))
                sp.wait_ge(started, 1)
                sp.wait_ge(xe_mm, after)
                sp.dma_start(Xe[p][:], slots[bass.ds(n * CAP, CAP), :].rearrange("(s p) d -> p s d", p=S)).then_inc(xe_in[p], 16)

            sp.wait_ge(filled["Y1"], B)
            load_weights(Seq(0))
            sp.wait_ge(k_lo, 2 * B)
            load_weights(Seq(1))
            sp.wait_ge(scattered, 16 * B)
            load_rows(Seq(0))
            load_rows(Seq(1))
            with sp.Fori(0, (E - 2) // 2) as j:
                for n in (2, 3):
                    load_rows(Seq(n, j))
                    load_weights(Seq(n, j))

            def store(r):
                for c in range(4):
                    after = held(sp, r.done(per=4, k=c + 1))
                    sp.wait_ge(started, 1)
                    sp.wait_ge(e_out, after)
                    sp.dma_start(io["out"][bass.ds((r.index() * 4 + c) * S, S), :], O3[c][:]).then_inc(stored[c], 16)

            rounds(sp, store)
            for c in range(4):
                sp.wait_ge(stored[c], 16 * (B // 4))

        @block.gpsimd
        def _(pool):
            pool.memset(wide[:], 0.0).then_inc(cast_const, 1)
            pool.memset(eps[:], EPS).then_inc(cast_const, 1)
            pool.memset(zero1[:], 0.0).then_inc(started, 1)
            pool.memset(negmax_s[:], 0.0).then_inc(cast_const, 1)
            pool.memset(negmax_x[:], 0.0).then_inc(cast_const, 1)
            for high in (Vsh, Vlh, Vxh[0], Vxh[1]):
                pool.memset(high[:], 1.0).then_inc(cast_const, 1)
            for low in (Vsl, Vll, Vxl[0], Vxl[1]):
                pool.memset(low[:], 0.0).then_inc(cast_const, 1)
            pool.memset(lift[:], LIFT).then_inc(cast_const, 1)
            pool.memset(ones[:], 1.0).then_inc(cast_const, 1)
            pool.memset(carry[1][:], -1.0).then_inc(cast_const, 1)
            pool.wait_ge(loaded_const, N_CONST)
            pool.wait_ge(cast_const, CONSTS_MADE)
            for n in range(0, E * CAP + B * S, E * CAP):
                pool.dma_start(slots[n:n + E * CAP, :].rearrange("(p n) d -> p (n d)", p=S),
                               wide[0:S, 0:16 * D]).then_inc(zeroed, 16)

            def pair_sums(b):
                pool.wait_ge(loaded_x[b.parity], b.pairs(16))
                pool.wait_ge(filled["A2"], b.done(back=1))
                x = xT[b.parity][:].rearrange("p t (n a) -> p t n a", a=2)
                pool.tensor_tensor(pairsum[:], x[:, :, :, 0], x[:, :, :, 1], ALU.add).then_inc(a_pool, 1)

            def gate_local(b, it):
                pool.wait_ge(*left("A6", it.before()))
                pool.tensor_tensor(gate_l[:], Os[:, 0:H].rearrange("p h d -> p (h d)"), glb[:], ALU.mult).then_inc(b_pool, 1)
                pool.wait_ge(loaded_n[b.parity], b.pairs(16))
                pool.wait_ge(b_ln, b.done(per=3, back=1))
                pool.tensor_tensor(xob[:], xn[b.parity][:], outb[:], ALU.add).then_inc(b_pool, 1)

            def gate_remote(b, it):
                pool.wait_ge(*left("B2", it))
                pool.tensor_tensor(gate_r[:], rem[:], grb[:], ALU.mult).then_inc(b_pool, 1)
                pool.wait_ge(b_pool, b.done(per=5, k=3))
                pool.tensor_tensor(gate_t[:], gate_l[:], gate_r[:], ALU.add).then_inc(b_pool, 1)
                pool.tensor_tensor(differ[:], Os[:, 0:H].rearrange("p h d -> p (h d)"), rem[:], ALU.subtract).then_inc(b_pool, 1)

            def self_shift(it):
                after1 = held(pool, uses("A4", it))
                after2 = held(pool, in_order(SCORES, "As2", it.before()) if it.n > FIRST else 0)
                pool.wait_ge(started, 1)
                pool.wait_ge(emptied[bank("A4", it)], after1)
                pool.wait_ge(st_full, after2)
                pool.tensor_tensor(mask_s[0:20].rearrange("p (h q) -> p h q", q=S), turned_s[:].unsqueeze(1).to_broadcast([20, 20, S]),
                                   own20[:].unsqueeze(2).to_broadcast([20, 20, S]), ALU.mult).then_inc(a_shift, 1)

            def self_lo(it):
                b = it.of("A")
                pool.wait_ge(a_hi, b.done())
                pool.wait_ge(a_out, b.done(per=16, back=1))
                pool.tensor_tensor(QKhl[:, LOW], QK[:].rearrange("p t n -> p (t n)"), QKhl[:, HIGH], ALU.subtract).then_inc(a_lo, 1)

            def self_vlo(it):
                pool.wait_ge(a_vhi, it.of("A").done())
                pool.tensor_tensor(Vsl[:, :, 0:HD], Vs[:], Vsh[:, :, 0:HD], ALU.subtract)
                pool.tensor_tensor(Vll[:, :, 0:HD], Vl[:], Vlh[:, :, 0:HD], ALU.subtract).then_inc(a_vlo, 1)

            def query_low(it):
                b = it.of("B")
                pool.wait_ge(b_qh, b.done())
                pool.wait_ge(b_out, b.done(per=16, back=1))
                pool.tensor_tensor(Qhl[:, LOW], Qx[:].rearrange("p t e q -> p (t e q)"), Qhl[:, HIGH], ALU.subtract).then_inc(b_ql, 1)

            def mix(b):
                pool.wait_ge(b_z, b.done(per=4))
                pool.wait_ge(filled["B3"], b.done(back=1))
                pool.tensor_tensor(mixed[:], gated[:], rem[:], ALU.add).then_inc(b_mixed, 1)

            def x1_bias(b):
                pool.wait_ge(b_ln, b.done(per=3))
                pool.tensor_tensor(x2_all[:, bass.ds(b.index(), 1), :].rearrange("p a d -> p (a d)"), x1[:], bp[:], ALU.add).then_inc(b_x1bp, 1)

            def value_bias(b, it):
                pool.wait_ge(*left("Y1", it.before()))
                pool.wait_ge(filled["T2"], b.done(back=1))
                pool.tensor_tensor(Oxb[:], Ox[:].rearrange("p h d -> p (h d)"), bv_cross[:], ALU.add).then_inc(t_pool, 1)

            def keep_x2(b):
                after = held(pool, b.done(per=3))
                pool.wait_ge(started, 1)
                pool.wait_ge(t_ln, after)
                pool.tensor_copy(x2_all[:, bass.ds(b.index(), 1), :].rearrange("p a d -> p (a d)"), x2[b.parity][:]).then_inc(t_keep, 1)

            def scatter(b):
                p = b.parity
                if b.n == 0:
                    pool.wait_ge(zeroed, 48)
                after1 = held(pool, b.done(per=7))
                after2 = held(pool, b.done(per=16, back=1))
                pool.wait_ge(started, 1)
                pool.wait_ge(t_pos, after1)
                pool.wait_ge(scattered, after2)
                pool.indirect_dma_start(
                    out=slots[:, :], out_offset=bass.IndirectOffsetOnAxis(ap=slot[p][:, 0:1], axis=0),
                    in_=x2[p][:], in_offset=None).then_inc(scattered, 16)

            def body(it):
                A, Bs, T = it.of("A"), it.of("B"), it.of("T")
                a, k, b, x, y, t = (it.has(stage) for stage in "AKBXYT")
                if a: pair_sums(A)
                if t: value_bias(T, it)
                if b: gate_local(Bs, it)
                if a: self_lo(it)
                if b: gate_remote(Bs, it)
                if a: self_vlo(it)
                if b: mix(Bs)
                if t: keep_x2(T)
                if a: self_shift(it)
                if t: scatter(T)
                if b: query_low(it); x1_bias(Bs)

            iterations(pool, body)

            def gather(r, c):
                g = 4 * r.parity + c
                pool.tensor_copy(slot_g[g][:], slot_all[:, bass.ds(r.index() * 4 + c, 1)]).then_inc(g_idx, 1)
                after = held(pool, r.done(per=4, k=c + 1))
                pool.wait_ge(started, 1)
                pool.wait_ge(g_idx, after)
                pool.indirect_dma_start(
                    out=G[g][:], out_offset=None, in_=slots[:, :],
                    in_offset=bass.IndirectOffsetOnAxis(ap=slot_g[g][:, 0:1], axis=0)).then_inc(g_in[g], 16)

            for p in range(2):
                pool.wait_ge(y_out[p], 16 * (E // 2))
            pool.wait_ge(t_pos, 7 * B)

            def gather_round(r):
                used, arrived = held(pool, r.done(per=4, back=2)), held(pool, r.pairs(16, back=1))
                pool.wait_ge(started, 1)
                pool.wait_ge(e_sum, used)
                for c in range(4):
                    pool.wait_ge(g_in[4 * r.parity + c], arrived)
                for c in range(4):
                    gather(r, c)

            rounds(pool, gather_round)

        @block.tensor
        def _(pe):
            pe.wait_ge(loaded_const, N_CONST)
            for n, w in enumerate((Wk, Wq)):
                for k in range(2):
                    for t in range(2):
                        mm = pe.matmul(MX[:, n, (2 * k + t) * 128:(2 * k + t + 1) * 128],
                                       w[:, t, k * 128:(k + 1) * 128], center[:], start=True, stop=True)
            mm.then_inc(weights_mm, 1)
            pe.matmul(MI[0][:, 0:2], center[:], bk2[:], start=True, stop=True)
            pe.matmul(MI[0][:, 2:4], center[:], bq2[:], start=True, stop=True).then_inc(weights_mm, 1)
            pe.wait_ge(weights_ok, 4)
            pe.wait_ge(cast_const, CONSTS_MADE)

            def enter(step, it, source=None):
                pe.wait_ge(emptied[bank(step, it)], uses_before(step, it))
                if source and bank(source, it) != bank(step, it):
                    pe.wait_ge(*left(source, it))
                return MI[bank(step, it)]

            def two(out, lhs, rhs):
                pe.matmul(out, lhs(0), rhs(0), start=True, stop=False)
                return pe.matmul(out, lhs(1), rhs(1), start=False, stop=True)

            def A1(it):
                b = it.of("A")
                p, ps = b.parity, enter("A1", it)
                pe.wait_ge(loaded_x[p], b.pairs(16))
                for m in range(4):
                    mm = two(ps[:, m * S:(m + 1) * S], lambda k: wqkv[:, k, m * 128:(m + 1) * 128],
                             lambda k: xT[p][:, k])
                mm.then_inc(filled["A1"], 1)

            def A2(it):
                b = it.of("A")
                p, ps = b.parity, enter("A2", it)
                pe.wait_ge(a_pool, b.done())
                two(ps[0:S, 0:D], lambda k: xT[p][:, k], lambda k: wqkv[:, k, 2 * D:3 * D])
                two(ps[0:64, 256:356], lambda k: rqw[:, k], lambda k: xT[p][:, k])
                two(ps[0:64, 356:406], lambda k: rkvh[:, k, 0:64], lambda k: pairsum[:, k])
                two(ps[0:NL, 406:470], lambda k: pairsum[:, k], lambda k: rkvh[:, k, 64:128]).then_inc(filled["A2"], 1)

            def self_maxima(it, g):
                b = it.of("A")
                pe.wait_ge(max_read, in_order(MAXIMA, f"As{g}", it, back=1))
                pe.wait_ge(a_stack, b.done(per=80))
                n = 500 if g == 0 else 400
                for i in range(2):
                    pe.matmul(MX[:, i, 0:n], identb[0:S], mask_q[:, 0:n], start=True, stop=True)
                for t in range(2):
                    for e in range(2):
                        for i in range(2):
                            pair = 4 * t + 2 * g + i
                            c = (2 * t + e) * S
                            mm = pe.matmul(MX[:, i, c:c + S], QKst[:, pair, e * S:e * S + 128], QKst[:, pair, 2 * S:],
                                           start=False, stop=True, skip_group_check=True)
                if g == 0:
                    for e in range(2):
                        for i in range(2):
                            c = 400 + e * NL
                            mm = pe.matmul(MX[:, i, c:c + NL], QKst[:, 8 + i, e * S:e * S + 128], QKst[:, 8 + i, 2 * S:2 * S + NL],
                                           start=False, stop=True, skip_group_check=True)
                mm.then_inc(max_full, 1)

            def A4(it):
                ps = enter("A4", it)
                pe.wait_ge(max_read, in_order(MAXIMA, "As1", it))
                pe.transpose(ps[:, 0:S // 2].bitcast(BF16), negmax_s[:], identb[0:S, 0:S]).then_inc(filled["A4"], 1)

            def self_scores(it, u):
                first = pair_of(f"As{u}", it)
                after1 = held(pe, in_order(SCORES, f"As{u}", it, back=2))
                after2 = held(pe, it.of("A").done())
                pe.wait_ge(started, 1)
                pe.wait_ge(st_exp, after1)
                pe.wait_ge(a_shift, after2)
                width = 400 if u < 2 else 200
                for i in range(2):
                    c = 800 * u + width * i
                    pe.matmul(ST[:, first + i, 0:width], eye20[:], mask_s[:, c:c + width], start=True, stop=True)
                for t in range(2 if u < 2 else 1):
                    for i in range(2):
                        flat = QKst.rearrange("p g n -> p (g n)")
                        c = (4 * t + 2 * u + i if u < 2 else 8 + i) * 3 * S
                        mm = pe.matmul(ST[:, first + i, 2 * S * t:2 * S * (t + 1)], flat[:, c + 2 * S:c + 2 * S + 128],
                                       flat[:, c:c + 2 * S], start=False, stop=True, skip_group_check=True)
                mm.then_inc(st_full, 1)

            def weighted(out, ph, pl, vh, vl, first, last):
                pe.matmul(out, ph, vh, start=first, stop=False)
                pe.matmul(out, ph, vl, start=False, stop=False)
                return pe.matmul(out, pl, vh, start=False, stop=last)

            def A6(it):
                ps = enter("A6", it)
                pe.wait_ge(st_low, in_order(SCORES, "As2", it))
                pe.wait_ge(a_vlo, it.of("A").done())
                for h in range(H):
                    t, r, e = h // 8, h % 8 // 2, h % 2
                    c = (4 * r + 2 * t + e) * S
                    weighted(ps[:, h * SP1:(h + 1) * SP1], Psh[:, c:c + 128], Psl[:, c:c + 128], Vsh[:, h], Vsl[:, h], True, True)
                for h in range(LH):
                    c = h * S
                    mm = weighted(ps[:, (H + h) * SP1:(H + h + 1) * SP1], Plh[:, c:c + 128], Pll[:, c:c + 128], Vlh[:, h], Vll[:, h], True, True)
                mm.then_inc(filled["A6"], 1)

            def B1(it):
                ps = MI[bank("B1", it)]
                source, there = left("A6", it.before())
                free, there = held(pe, uses_before("B1", it)), held(pe, there)
                pe.wait_ge(started, 1)
                pe.wait_ge(emptied[bank("B1", it)], free)
                if source is not emptied[bank("B1", it)]:
                    pe.wait_ge(source, there)
                pe.transpose(ps[0:64, 0:S], Os[:, H:H + LH].rearrange("p h d -> p (h d)"), ident[0:S, 0:S]).then_inc(filled["B1"], 1)

            def B2(it):
                ps = enter("B2", it, "B1")
                pe.matmul(ps[0:S, 0:D], latT[:], routw[:], start=True, stop=True).then_inc(filled["B2"], 1)

            def turned(step, it, source):
                ps = MI[bank(step, it)]
                for t in range(2):
                    mm = pe.transpose(ps[:, t * S:(t + 1) * S], source[:, t * 128:(t + 1) * 128], ident[0:S, 0:S])
                mm.then_inc(filled[step], 1)

            def B3(it):
                enter("B3", it)
                pe.wait_ge(b_mixed, it.of("B").done())
                turned("B3", it, mixed)

            def B4(it):
                ps = enter("B4", it, "B3")
                two(ps[0:S, 0:D], lambda k: mixT[:, k], lambda k: outw[:, k]).then_inc(filled["B4"], 1)

            def B5(it):
                enter("B5", it)
                pe.wait_ge(b_ln, it.of("B").done(per=3))
                turned("B5", it, x1)

            def B6(it):
                ps = enter("B6", it, "B5")
                for t in range(2):
                    mm = two(ps[:, t * S:(t + 1) * S], lambda k: WqC[:, k, t * 128:(t + 1) * 128], lambda k: x1T[:, k])
                mm.then_inc(filled["B6"], 1)

            def B7(it):
                ps = enter("B7", it, "B6")
                pe.matmul(ps[:, 0:2 * S], average[:], sqq[:].rearrange("p t q -> p (t q)"), start=True, stop=True).then_inc(filled["B7"], 1)

            def K12(it, t):
                step, b = f"K{t + 1}", it.of("K")
                p, ps = b.parity, enter(step, it)
                pe.wait_ge(loaded_c[p], b.pairs(16))
                two(ps[:, 0:M], lambda k: WkC[:, k, t * 128:(t + 1) * 128], lambda k: cT[p][:, k]).then_inc(filled[step], 1)

            def K34(it, t):
                step, b = f"K{t + 3}", it.of("K")
                ps = enter(step, it, f"K{t + 1}")
                pe.matmul(ps[:, 0:M], average[:], sqk[:, t], start=True, stop=True).then_inc(filled[step], 1)

            def K56(it, tiles):
                step, b = ("K5" if tiles[0] == 0 else "K6"), it.of("K")
                p, ps = b.parity, enter(step, it)
                for n, kt in enumerate(tiles):
                    mm = two(ps[0:KN[kt], n * D:(n + 1) * D], lambda k: cT[p][:, k, KO[kt]:KO[kt] + KN[kt]],
                             lambda k: WvT[:, k])
                mm.then_inc(filled[step], 1)

            def cross_maximum(it, n):
                b = it.of("X")
                p = b.parity
                back = 1 if MAXIMA[MAXIMA.index(f"X{n}") - 1][0] == "A" else 2
                pe.wait_ge(max_read, in_order(MAXIMA, f"X{n}", it, back=back))
                if n == 0:
                    pe.wait_ge(k_stack[p], b.pairs(48))
                    pe.wait_ge(b_stack[p], b.pairs(48))
                pe.matmul(MX[:, n % 2, 0:M], Qst[p][0:96, n * S:n * S + 128], Kst[p][0:96, n // 2 * M:(n // 2 + 1) * M],
                          start=True, stop=True).then_inc(max_full, 1)

            def X1(it):
                ps = enter("X1", it)
                pe.wait_ge(max_read, in_order(MAXIMA, "X15", it))
                pe.transpose(ps[:, 0:S // 2].bitcast(BF16), negmax_x[:], identb[0:S, 0:S]).then_inc(filled["X1"], 1)

            def cross_scores(it, u):
                p, first = it.of("Y").parity, pair_of(f"Y{u}", it)
                pe.wait_ge(st_exp, in_order(SCORES, f"Y{u}", it, back=2))
                if u == 0:
                    pe.wait_ge(*left("X1", it.before()))
                for kt in ([0, 1] if u % 2 == 0 else [2]):
                    for i in range(2):
                        pair = u // 2 * 2 + i
                        k, c = pair * M + KO[kt], kt % 2 * 200
                        mm = pe.matmul(ST[:, first + i, c:c + 2 * S], Kst[p][:, k:k + 128], Qst[p][:, 2 * pair * S:2 * (pair + 1) * S],
                                       start=True, stop=True)
                mm.then_inc(st_full, 1)

            def Y1(it):
                b = it.of("Y")
                p, ps = b.parity, enter("Y1", it)
                pe.wait_ge(st_low, in_order(SCORES, "Y7", it))
                for h in range(H):
                    t, r, e = h // 8, h % 8 // 2, h % 2
                    for kt in range(3):
                        n, c = KN[kt], (12 * (2 * t + r // 2) + 6 * (r % 2) + 2 * kt + e) * S
                        mm = weighted(ps[:, h * SP1:(h + 1) * SP1], Pxh[0:n, c:c + 128], Pxl[0:n, c:c + 128],
                                      Vxh[p][0:n, kt, h], Vxl[p][0:n, kt, h], kt == 0, kt == 2)
                mm.then_inc(filled["Y1"], 1)

            def T2(it):
                enter("T2", it)
                pe.wait_ge(t_pool, it.of("T").done())
                turned("T2", it, Oxb)

            def T3(it):
                ps = enter("T3", it, "T2")
                two(ps[0:S, 0:D], lambda k: OxT[:, k], lambda k: WpT[:, k]).then_inc(filled["T3"], 1)

            def T4(it):
                enter("T4", it)
                pe.wait_ge(t_ln, it.of("T").done(per=3))
                turned("T4", it, x2[it.of("T").parity])

            def T5(it):
                ps = enter("T5", it, "T4")
                two(ps[0:S, 0:E], lambda k: x2T[:, k], lambda k: wsw[:, k]).then_inc(filled["T5"], 1)

            def T6(it):
                ps = enter("T6", it)
                pe.wait_ge(t_top, it.of("T").done(per=5))
                pe.matmul(ps[0:S, 0:E], upto[:], onehot[:], start=True, stop=True)
                pe.matmul(ps[0:S, E:2 * E], ones[:], onehot[:], start=True, stop=True).then_inc(filled["T6"], 1)

            def body(it):
                a, k, b, x, y, t = (it.has(stage) for stage in "AKBXYT")
                if a: A1(it); A2(it)
                if y: cross_scores(it, 0)
                if k: K12(it, 0)
                if x: cross_maximum(it, 0); cross_maximum(it, 1)
                if b: B1(it)
                if t: T2(it)
                if x: cross_maximum(it, 2)
                if k: K12(it, 1)
                if y: cross_scores(it, 1); cross_scores(it, 2)
                if x: cross_maximum(it, 3); cross_maximum(it, 4)
                if b: B2(it)
                if x: cross_maximum(it, 5)
                if t: T3(it)
                if x: cross_maximum(it, 6)
                if y: cross_scores(it, 3)
                if k: K34(it, 0)
                if x: cross_maximum(it, 7); cross_maximum(it, 8)
                if t: T4(it)
                if x: cross_maximum(it, 9)
                if b: B3(it)
                if y: cross_scores(it, 4)
                if x: cross_maximum(it, 10)
                if k: K34(it, 1)
                if x: cross_maximum(it, 11)
                if b: B4(it)
                if x: cross_maximum(it, 12)
                if a: self_maxima(it, 0)
                if y: cross_scores(it, 5)
                if t: T5(it)
                if a: self_maxima(it, 1)
                if x: cross_maximum(it, 13); cross_maximum(it, 14)
                if a: A4(it)
                if y: cross_scores(it, 6)
                if b: B5(it)
                if x: cross_maximum(it, 15)
                if t: T6(it)
                if y: cross_scores(it, 7)
                if x: X1(it)
                if b: B6(it)
                if a: self_scores(it, 0); self_scores(it, 1)
                if b: B7(it)
                if a: self_scores(it, 2)
                if y: Y1(it)
                if k: K56(it, [0, 1])
                if a: A6(it)
                if k: K56(it, [2])

            iterations(pe, body)

            def expert(e):
                p = e.parity
                pe.wait_ge(xe_in[p], e.pairs(16))
                pe.wait_ge(xe_ok, e.done(back=1))
                for s in range(2):
                    for k in range(2):
                        mm = pe.transpose(MI[0][:, k * CAP + s * S:k * CAP + (s + 1) * S], Xe[p][:, s, k * 128:(k + 1) * 128],
                                          ident[0:S, 0:S])
                mm.then_inc(xe_mm, 1)
                pe.wait_ge(xe_ok, e.done())
                pe.wait_ge(w_in[p], e.pairs(64))
                for q in range(4):
                    pe.wait_ge(h_act if q % 2 == 0 else h_dve, e.done(per=2, k=q // 2 + 1, back=1))
                    for m in (2 * q, 2 * q + 1):
                        mm = two(ST[:, q, m % 2 * CAP:(m % 2 + 1) * CAP], lambda k: W1[p][:, k, m * 128:(m + 1) * 128],
                                 lambda k: XeT[:, k])
                    mm.then_inc(h_mm, 1)
                pe.wait_ge(h_act, e.done(per=2))
                pe.wait_ge(h_dve, e.done(per=2))
                pe.wait_ge(y_ok, e.done(per=2, back=1))
                for s in range(2):
                    for m in range(8):
                        mm = pe.matmul(MX[0:S, s, 0:D], hT[:, m, s * S:(s + 1) * S], W2[p][:, m], start=(m == 0), stop=(m == 7))
                    mm.then_inc(y_mm, 1)

            expert(Seq(0))
            expert(Seq(1))
            with pe.Fori(0, (E - 2) // 2) as j:
                expert(Seq(2, j))
                expert(Seq(3, j))

        @block.scalar
        def _(act):
            act.preload_act_table_set("natural_log_exp_and_others")
            act.wait_ge(cast_const, CONSTS_MADE)
            act.wait_ge(weights_ok, 4)

            def leave(ins, step, it):
                ins.then_inc(emptied[bank(step, it)], 1)

            def copy_out(step, it, out, source, free=None):
                act.wait_ge(filled[step], it.of(step[0]).done())
                if free:
                    act.wait_ge(*free)
                leave(act.activation(out, source(MI[bank(step, it)]), ACT.Copy), step, it)

            def K12(it, t):
                step, b = f"K{t + 1}", it.of("K")
                act.wait_ge(filled[step], b.done())
                act.wait_ge(k_n, b.done(per=2, k=t + 1, back=1))
                act.activation(kc[:, t], MI[bank(step, it)][:, 0:M], ACT.Identity, bias=bkC[:, t:t + 1]).then_inc(k_c, 1)
                act.wait_ge(filled[f"K{t + 3}"], b.done(back=1))
                leave(act.activation(sqk[:, t], MI[bank(step, it)][:, 0:M], ACT.Square, bias=bkC[:, t:t + 1]), step, it)

            def K34(it, t):
                step, b = f"K{t + 3}", it.of("K")
                act.wait_ge(filled[step], b.done())
                act.wait_ge(k_rs, b.done(per=2, k=t + 1, back=1))
                leave(act.activation(lnk[:, t], MI[bank(step, it)][:, 0:M], ACT.Ln, bias=eps[:]), step, it)
                act.wait_ge(*left(step, it))
                act.wait_ge(k_n, b.done(per=2, k=t + 1, back=1))
                act.activation(rsk[:, t], lnk[:, t], ACT.Exp, scale=-0.5).then_inc(k_rs, 1)

            def rstd(b, out, log, mv, made, sem_):
                act.wait_ge(made, b.done(per=3, k=2))
                act.wait_ge(made, b.done(per=3, back=1))
                act.activation(log[:], mv[:, 1:2], ACT.Ln, bias=eps[0:S]).then_inc(sem_, 1)
                act.wait_ge(sem_, b.done(per=2, k=1))
                act.activation(out[:], log[:], ACT.Exp, scale=-0.5).then_inc(sem_, 1)

            def self_exp(it, u):
                b, first = it.of("A"), pair_of(f"As{u}", it)
                act.wait_ge(st_full, in_order(SCORES, f"As{u}", it))
                if u == 0:
                    act.wait_ge(filled["A6"], b.done(back=1))
                if it.n > FIRST or u >= 2:
                    act.wait_ge(st_low, in_order(SCORES, f"As{u}", it, back=2))
                n, width = (S, 400) if u < 2 else (NL, 200)
                out, source = self_part(Psh, Plh, u), ST[0:n, first:first + 2, 0:width]
                act.activation(out, source, ACT.Exp, bias=lift[0:n])
                act.activation(Pf[0:n, first // 2, :, 0:width], source, ACT.Exp, bias=lift[0:n]).then_inc(st_exp, 1)

            def cross_exp(it, u):
                b, first = it.of("Y"), pair_of(f"Y{u}", it)
                act.wait_ge(st_full, in_order(SCORES, f"Y{u}", it))
                if u == 0 and b.n == 0:
                    act.wait_ge(zeroed, 48)
                if u == 0:
                    act.wait_ge(filled["Y1"], b.done(back=1))
                act.wait_ge(st_low, in_order(SCORES, f"Y{u}", it, back=2))
                n, width = (KN[0], 400) if u % 2 == 0 else (KN[2], 200)
                source = ST[0:n, first:first + 2, 0:width]
                act.activation(cross_part(Pxh, u), source, ACT.Exp, bias=lift[0:n])
                act.activation(Pf[0:n, first // 2, :, 0:width], source, ACT.Exp, bias=lift[0:n]).then_inc(st_exp, 1)

            def self_hi(it):
                b = it.of("A")
                act.wait_ge(*left("A2", it))
                act.wait_ge(a_out, b.done(per=16, back=1))
                act.activation(QKhl[:, HIGH], QK[:].rearrange("p t n -> p (t n)"), ACT.Copy).then_inc(a_hi, 1)

            def A4(it):
                b = it.of("A")
                act.wait_ge(filled["A4"], b.done())
                act.wait_ge(a_shift, b.done(back=1))
                leave(act.activation(turned_s[:], MI[bank("A4", it)][0:20, 0:S // 2].bitcast(BF16), ACT.Copy), "A4", it)

            def self_vhi(it):
                b = it.of("A")
                act.wait_ge(a_vals, b.done())
                act.wait_ge(filled["A6"], b.done(back=1))
                act.activation(Vsh[:, :, 0:HD], Vs[:], ACT.Copy)
                act.activation(Vlh[:, :, 0:HD], Vl[:], ACT.Copy).then_inc(a_vhi, 1)

            def cross_vhi(it, tiles):
                step, b = ("K5" if tiles[0] == 0 else "K6"), it.of("K")
                act.wait_ge(filled[step], b.done())
                act.wait_ge(filled["Y1"], b.done(back=2))
                for i, kt in enumerate(tiles):
                    ins = act.activation(Vxh[b.parity][0:KN[kt], kt, :, 0:HD],
                                         MI[bank(step, it)][0:KN[kt], i * D:(i + 1) * D].rearrange("p (h d) -> p h d", d=HD), ACT.Copy)
                ins.then_inc(k_vhi, 1)

            def gate_exp(it):
                b = it.of("B")
                act.wait_ge(b_z, b.done(per=4, k=1))
                act.activation(gate_e[:], gate_z[:], ACT.Exp, scale=-1.0).then_inc(b_e, 1)

            def B6(it):
                act.wait_ge(filled["B6"], it.of("B").done())
                act.wait_ge(b_q, it.of("B").done(per=2, k=1, back=1))
                for t in range(2):
                    ins = act.activation(qc[:, t], MI[bank("B6", it)][:, t * S:(t + 1) * S], ACT.Identity, bias=bqC[:, t:t + 1])
                ins.then_inc(b_c, 1)
                act.wait_ge(filled["B7"], it.of("B").done(back=1))
                for t in range(2):
                    ins = act.activation(sqq[:, t], MI[bank("B6", it)][:, t * S:(t + 1) * S], ACT.Square, bias=bqC[:, t:t + 1])
                leave(ins, "B6", it)

            def B7(it):
                b = it.of("B")
                act.wait_ge(filled["B7"], b.done())
                leave(act.activation(lnq[:].rearrange("p t q -> p (t q)"), MI[bank("B7", it)][:, 0:2 * S], ACT.Ln, bias=eps[:]), "B7", it)
                act.wait_ge(*left("B7", it))
                act.activation(rsq[:], lnq[:], ACT.Exp, scale=-0.5).then_inc(b_rsq, 1)

            def high_k(it, t):
                b = it.of("K")
                act.wait_ge(k_n, b.done(per=2, k=t + 1))
                if t == 0:
                    act.wait_ge(k_out, b.done(per=16, back=1))
                act.activation(Khl[:, HIGH, t * M:(t + 1) * M], kn[:, t], ACT.Identity, bias=norm4[:, 3:4]).then_inc(k_hi, 1)

            def high_q(it):
                b = it.of("B")
                act.wait_ge(b_q, b.done(per=2, k=2))
                act.wait_ge(b_out, b.done(per=16, back=1))
                act.activation(Qhl[:, HIGH], Qx[:].rearrange("p t e q -> p (t e q)"), ACT.Copy).then_inc(b_qh, 1)

            def router_exp(it):
                b = it.of("T")
                act.wait_ge(t_top, b.done(per=5, k=2))
                act.wait_ge(t_exp, b.done(back=1))
                act.activation(exps8[:], logits[:], ACT.Exp, bias=negtop[:], accum_out=sum8[:, bass.ds(b.index(), 1)]).then_inc(t_exp, 1)

            halves = lambda ps: ps[:, 0:2 * S].rearrange("p (t q) -> p t q", t=2)

            def body(it):
                a, k, b, x, y, t = (it.has(stage) for stage in "AKBXYT")
                if y: cross_exp(it, 0)
                if k: K12(it, 0)
                if b: copy_out("B1", it, latT[:], lambda ps: ps[0:64, 0:S])
                if t: copy_out("T2", it, OxT[:], halves)
                if a: self_hi(it)
                if k: K12(it, 1)
                if y: cross_exp(it, 1); cross_exp(it, 2)
                if t: rstd(it.of("T"), rs2, ln2, mv2, t_ln, t_rs)
                if k: K34(it, 0)
                if b: gate_exp(it)
                if a: self_vhi(it)
                if t: copy_out("T4", it, x2T[:], halves)
                if y: cross_exp(it, 3)
                if b: copy_out("B3", it, mixT[:], halves)
                if k: high_k(it, 0)
                if y: cross_exp(it, 4)
                if k: K34(it, 1)
                if b: rstd(it.of("B"), rs1, ln1, mv1, b_ln, b_rs)
                if y: cross_exp(it, 5)
                if t: router_exp(it)
                if a: A4(it)
                if k: high_k(it, 1)
                if y: cross_exp(it, 6)
                if b: copy_out("B5", it, x1T[:], halves)
                if y: cross_exp(it, 7)
                if b: B6(it)
                if a: self_exp(it, 0); self_exp(it, 1)
                if b: B7(it)
                if a: self_exp(it, 2)
                if b: high_q(it)
                if k: cross_vhi(it, [0, 1]); cross_vhi(it, [2])

            iterations(act, body)

            def expert(e):
                p = e.parity
                act.wait_ge(xe_mm, e.done())
                act.wait_ge(h_mm, e.done(per=4, back=1))
                act.activation(XeT[:], MI[0][:, 0:2 * CAP].rearrange("p (k c) -> p k c", k=2), ACT.Copy).then_inc(xe_ok, 1)
                for q in (0, 2):
                    act.wait_ge(h_mm, e.done(per=4, k=q + 1))
                    if q == 0:
                        act.wait_ge(y_mm, e.done(per=2, back=1))
                    for m in (2 * q, 2 * q + 1):
                        ins = act.activation(hT[:, m], ST[:, q, m % 2 * CAP:(m % 2 + 1) * CAP], ACT.Relu, bias=b1[p][:, m:m + 1])
                    ins.then_inc(h_act, 1)
                act.wait_ge(y_ok, e.done(per=2))
                act.dma_start(slots[bass.ds(e.index() * CAP, CAP), :].rearrange("(s p) d -> p s d", p=S), Y[p][:]).then_inc(y_out[p], 16)

            expert(Seq(0))
            expert(Seq(1))
            with act.Fori(0, (E - 2) // 2) as j:
                expert(Seq(2, j))
                expert(Seq(3, j))

            def rstd_round(r):
                act.wait_ge(e_mv, r.done(per=4))
                act.wait_ge(e_out, r.done(per=4, back=1))
                act.activation(ln3[:], mv3[:, :, 1], ACT.Ln, bias=eps[0:S]).then_inc(e_rs, 1)
                act.wait_ge(e_rs, r.done(per=2, k=1))
                act.activation(rs3[:], ln3[:], ACT.Exp, scale=-0.5).then_inc(e_rs, 1)

            rounds(act, rstd_round)

        @block.vector
        def _(dve):
            for halves in (Psh, Psl, Plh, Pll):
                dve.memset(halves[:], 0.0).then_inc(cast_const, 1)
            dve.memset(QK[:], 0.0).then_inc(cast_const, 1)
            dve.memset(QKst, 0.0).then_inc(cast_const, 1)
            for p in range(2):
                dve.memset(Qst[p][:], 0.0).then_inc(cast_const, 1)
                dve.memset(Kst[p], WEIGHT).then_inc(cast_const, 1)
            dve.wait_ge(loaded_const, N_CONST)
            dve.tensor_copy(identb[:], ident[:]).then_inc(cast_const, 1)
            heads_of = lambda ap, n: ap.rearrange("p (h q) -> p h q", h=n)
            dve.tensor_copy(heads_of(mask_s[:, 0:H * S], H), mask_s_f[:, 0:1].to_broadcast([120, H, S])).then_inc(cast_const, 1)
            dve.tensor_copy(heads_of(mask_s[:, H * S:], LH), mask_s_f[:, 1:2].to_broadcast([120, LH, S])).then_inc(cast_const, 1)
            dve.tensor_copy(heads_of(mask_q[:, 0:4 * S], 4), mask_q_f[:, 0:S].unsqueeze(1).to_broadcast([S, 4, S])).then_inc(cast_const, 1)
            dve.tensor_copy(heads_of(mask_q[:, 4 * S:], 2), mask_q_f[:, S:].unsqueeze(1).to_broadcast([S, 2, NL])).then_inc(cast_const, 1)
            dve.tensor_copy(eye20[:], eye20_f[:]).then_inc(cast_const, 1)
            dve.tensor_scalar(rkvh[:], rkvw[:], 0.5, None, ALU.mult).then_inc(cast_const, 1)
            dve.tensor_scalar(parity_s[:], parity[:], SCALE, None, ALU.mult).then_inc(cast_const, 1)
            dve.wait_ge(weights_mm, 2)
            for n, w in enumerate((WkC, WqC)):
                dve.tensor_copy(w[:].rearrange("p k o -> p (k o)"), MX[:, n]).then_inc(weights_ok, 1)
            dve.tensor_copy(bkC[:], MI[0][:, 0:2]).then_inc(weights_ok, 1)
            dve.tensor_copy(bqC[:], MI[0][:, 2:4]).then_inc(weights_ok, 1)
            dve.wait_ge(cast_const, CONSTS_MADE - 2)
            dve.tensor_scalar(gq2[:], parity_s[:], norm4[:, 0:1], None, ALU.mult).then_inc(cast_const, 1)
            dve.tensor_scalar(bq2n[:], parity_s[:], norm4[:, 1:2], None, ALU.mult).then_inc(cast_const, 1)
            dve.wait_ge(cast_const, CONSTS_MADE)

            def leave(ins, step, it):
                ins.then_inc(emptied[bank(step, it)], 1)

            def A1(it):
                b, ps = it.of("A"), MI[bank("A1", it)]
                dve.wait_ge(filled["A1"], b.done())
                dve.wait_ge(a_lo, b.done(back=1))
                for t in range(2):
                    for e in range(2):
                        dve.tensor_scalar(QK[:, t, e * S:(e + 1) * S], ps[:, t * S:(t + 1) * S], bqk[:, t:t + 1], parity_s[:, e:e + 1], ALU.add, ALU.mult)
                    ins = dve.tensor_scalar(QK[:, t, 2 * S:], ps[:, (2 + t) * S:(3 + t) * S], bqk[:, 2 + t:3 + t], None, ALU.add)
                leave(ins, "A1", it)

            def A2(it):
                b, ps = it.of("A"), MI[bank("A2", it)]
                dve.wait_ge(filled["A2"], b.done())
                dve.wait_ge(a_vlo, b.done(back=1))
                heads = lambda ap: ap.rearrange("p (h d) -> p h d", d=HD)
                dve.tensor_tensor(Vs[:], heads(ps[0:S, 0:D]), heads(bv_self[:]), ALU.add)
                for e in range(2):
                    dve.tensor_scalar(QK[0:64, 2, e * S:(e + 1) * S], ps[0:64, 256:356], rqb[:], parity_s[0:64, e:e + 1], ALU.add, ALU.mult)
                dve.tensor_tensor(Vl[:], heads(ps[0:NL, 406:470]), heads(rvb[:]), ALU.add).then_inc(a_vals, 1)
                leave(dve.tensor_scalar(QK[0:64, 2, 2 * S:2 * S + NL], ps[0:64, 356:406], rkb[:], None, ALU.add), "A2", it)

            def self_max(it, g):
                dve.wait_ge(max_full, in_order(MAXIMA, f"As{g}", it))
                if g == 0:
                    dve.wait_ge(filled["A4"], it.of("A").done(back=1))
                out = negmax_s[:, 0:16].rearrange("p (r u) -> p r u", u=4)
                if g == 0:
                    dve.tensor_reduce(negmax_s[:, 16:20].rearrange("p (r e) -> p r e", e=2), MX[0:S, :, 400:500].rearrange("p i (e k) -> p i e k", k=NL), X, ALU.max, negate=True)
                dve.tensor_reduce(out[:, 2 * g:2 * g + 2], MX[0:S, :, 0:400].rearrange("p i (u k) -> p i u k", k=S), X, ALU.max,
                                  negate=True).then_inc(max_read, 1)

            def self_low(it, u):
                b, first = it.of("A"), pair_of(f"As{u}", it)
                n, width = (S, 400) if u < 2 else (NL, 200)
                dve.wait_ge(st_exp, in_order(SCORES, f"As{u}", it))
                if u == 0:
                    dve.wait_ge(filled["A6"], b.done(back=1))
                dve.tensor_tensor(self_part(Psl, Pll, u), Pf[0:n, first // 2, :, 0:width], self_part(Psh, Plh, u),
                                  ALU.subtract).then_inc(st_low, 1)

            def cross_low(it, u):
                b, first = it.of("Y"), pair_of(f"Y{u}", it)
                n, width = (KN[0], 400) if u % 2 == 0 else (KN[2], 200)
                dve.wait_ge(st_exp, in_order(SCORES, f"Y{u}", it))
                if u == 0:
                    dve.wait_ge(filled["Y1"], b.done(back=1))
                dve.tensor_tensor(cross_part(Pxl, u), Pf[0:n, first // 2, :, 0:width], cross_part(Pxh, u),
                                  ALU.subtract).then_inc(st_low, 1)

            def cross_max(it, n):
                dve.wait_ge(max_full, in_order(MAXIMA, f"X{n}", it))
                if n == 0:
                    dve.wait_ge(filled["X1"], it.of("X").done(back=1))
                dve.tensor_reduce(negmax_x[:, 96 + n:97 + n], MX[0:S, n % 2, 0:M], X, ALU.max, negate=True).then_inc(max_read, 1)

            def shift_rows(it):
                b = it.of("X")
                dve.wait_ge(filled["X1"], b.done())
                negmax = MI[bank("X1", it)][96:112, 0:S // 2].bitcast(BF16).unsqueeze(1).to_broadcast([H, H, S])
                rows = Qst[b.parity][96:112, 0:H * S].rearrange("p (h q) -> p h q", q=S)
                leave(dve.tensor_tensor(rows, negmax, own_head[96:112].unsqueeze(2).to_broadcast([H, H, S]), ALU.mult), "X1", it)

            def A6(it):
                b = it.of("A")
                dve.wait_ge(filled["A6"], b.done())
                heads = MI[bank("A6", it)][0:S, 0:(H + LH) * SP1].rearrange("p (h d) -> p h d", d=SP1)
                dve.wait_ge(b_pool, b.done(per=5, back=1))
                dve.reciprocal(recip_s[:], heads[:, :, HD]).then_inc(a_dve, 1)
                dve.wait_ge(a_dve, b.done(per=2, k=1))
                dve.tensor_tensor(recip_m[:], recip_s[:], some_key[:], ALU.mult).then_inc(a_dve, 1)
                dve.wait_ge(a_dve, b.done(per=2))
                leave(dve.tensor_tensor(Os[:], heads[:, :, 0:HD], recip_m[:].unsqueeze(2).to_broadcast([S, H + LH, HD]), ALU.mult), "A6", it)

            def B2(it):
                dve.wait_ge(filled["B2"], it.of("B").done())
                dve.wait_ge(b_mixed, it.of("B").done(back=1))
                leave(dve.tensor_tensor(rem[:], MI[bank("B2", it)][0:S, 0:D], routb[:], ALU.add), "B2", it)

            def gate_sum(it):
                b = it.of("B")
                dve.wait_ge(b_pool, b.done(per=5, k=4))
                dve.tensor_reduce(gate_z[:], gate_t[:].rearrange("p (h d) -> p h d", d=HD), X, ALU.add).then_inc(b_z, 1)

            def gating(it):
                b = it.of("B")
                dve.wait_ge(b_e, b.done())
                dve.tensor_scalar(gate_d[:], gate_e[:], 1.0, None, ALU.add).then_inc(b_z, 1)
                dve.wait_ge(b_z, b.done(per=4, k=2))
                dve.reciprocal(gate[:], gate_d[:]).then_inc(b_z, 1)
                dve.wait_ge(b_z, b.done(per=4, k=3))
                dve.wait_ge(b_pool, b.done(per=5))
                heads = lambda x: x[:].rearrange("p (h d) -> p h d", d=HD)
                dve.tensor_tensor(heads(gated), heads(differ), gate[:].unsqueeze(2).to_broadcast([S, H, HD]), ALU.mult).then_inc(b_z, 1)

            def B4(it):
                b = it.of("B")
                dve.wait_ge(filled["B4"], b.done())
                dve.wait_ge(b_pool, b.done(per=5, k=2))
                leave(dve.tensor_tensor(res1[:], MI[bank("B4", it)][0:S, 0:D], xob[:], ALU.add), "B4", it)
                dve.wait_ge(*left("B4", it))
                dve.bn_stats(bn1[:], res1[:]).then_inc(b_ln, 1)
                after = held(dve, b.done(per=3, k=1))
                dve.wait_ge(started, 1)
                dve.wait_ge(b_ln, after)
                dve.bn_aggr(mv1[:], bn1[:]).then_inc(b_ln, 1)

            def norm1(it):
                b = it.of("B")
                dve.wait_ge(b_rs, b.done(per=2))
                dve.wait_ge(filled["B5"], b.done(back=1))
                dve.wait_ge(b_x1bp, b.done(back=1))
                dve.tensor_scalar(x1[:], res1[:], mv1[:, 0:1], rs1[:], ALU.subtract, ALU.mult).then_inc(b_ln, 1)

            def queries(it):
                b = it.of("B")
                p = b.parity
                dve.wait_ge(b_rsq, b.done())
                dve.tensor_tensor(qn[:], qc[:], rsq[:], ALU.mult).then_inc(b_q, 1)
                dve.wait_ge(b_q, b.done(per=2, k=1))
                dve.wait_ge(b_ql, b.done(back=1))
                dve.tensor_scalar(Qx[:, :, 0], qn[:], gq2[:, 0:1], bq2n[:, 0:1], ALU.mult, ALU.add)
                dve.tensor_scalar(Qx[:, :, 1], qn[:], gq2[:, 1:2], bq2n[:, 1:2], ALU.mult, ALU.add).then_inc(b_q, 1)

            def key_norm(it, t):
                b = it.of("K")
                dve.wait_ge(k_rs, b.done(per=2, k=t + 1))
                dve.wait_ge(k_hi, b.done(per=2, k=t + 1, back=1))
                dve.scalar_tensor_tensor(kn[:, t], kc[:, t], norm4[:, 2:3], rsk[:, t], ALU.mult, ALU.mult).then_inc(k_n, 1)

            def key_low(it, t):
                b = it.of("K")
                dve.wait_ge(k_hi, b.done(per=2, k=t + 1))
                if t == 0:
                    dve.wait_ge(k_out, b.done(per=16, back=1))
                tile = slice(t * M, (t + 1) * M)
                dve.scalar_tensor_tensor(Khl[:, LOW, tile], kn[:, t], norm4[:, 3:4], Khl[:, HIGH, tile], ALU.add, ALU.subtract).then_inc(k_lo, 1)

            def values(it, tiles):
                step, b = ("K5" if tiles[0] == 0 else "K6"), it.of("K")
                dve.wait_ge(k_vhi, b.done(per=2, k=1 if tiles[0] == 0 else 2))
                dve.wait_ge(filled["Y1"], b.done(back=2))
                for i, kt in enumerate(tiles):
                    ins = dve.tensor_tensor(Vxl[b.parity][0:KN[kt], kt, :, 0:HD],
                                            MI[bank(step, it)][0:KN[kt], i * D:(i + 1) * D].rearrange("p (h d) -> p h d", d=HD),
                                            Vxh[b.parity][0:KN[kt], kt, :, 0:HD], ALU.subtract)
                leave(ins, step, it)

            def Y1(it):
                b = it.of("Y")
                dve.wait_ge(filled["Y1"], b.done())
                dve.wait_ge(t_pool, b.done(back=1))
                heads = MI[bank("Y1", it)][0:S, 0:H * SP1].rearrange("p (h d) -> p h d", d=SP1)
                dve.reciprocal(recip_x[:], heads[:, :, HD]).then_inc(t_dve, 1)
                dve.wait_ge(t_dve, b.done())
                leave(dve.tensor_tensor(Ox[:], heads[:, :, 0:HD], recip_x[:].unsqueeze(2).to_broadcast([S, H, HD]), ALU.mult), "Y1", it)

            def T3(it):
                b = it.of("T")
                dve.wait_ge(filled["T3"], b.done())
                x1b = x2_all[:, bass.ds(b.index(), 1), :].rearrange("p a d -> p (a d)")
                dve.wait_ge(b_x1bp, b.done())
                leave(dve.tensor_tensor(res2[:], MI[bank("T3", it)][0:S, 0:D], x1b, ALU.add), "T3", it)
                dve.wait_ge(*left("T3", it))
                dve.bn_stats(bn2[:], res2[:]).then_inc(t_ln, 1)
                after = held(dve, b.done(per=3, k=1))
                dve.wait_ge(started, 1)
                dve.wait_ge(t_ln, after)
                dve.bn_aggr(mv2[:], bn2[:]).then_inc(t_ln, 1)

            def norm2(it):
                b = it.of("T")
                dve.wait_ge(t_rs, b.done(per=2))
                dve.wait_ge(scattered, b.done(per=16, back=1))
                dve.tensor_scalar(x2[b.parity][:], res2[:], mv2[:, 0:1], rs2[:], ALU.subtract, ALU.mult).then_inc(t_ln, 1)

            def route_to(it):
                b = it.of("T")
                dve.wait_ge(filled["T5"], b.done())
                dve.wait_ge(t_exp, b.done(back=1))
                leave(dve.tensor_tensor(logits[:], MI[bank("T5", it)][0:S, 0:E], bsw[:], ALU.add), "T5", it)
                after = held(dve, uses("T5", it))
                dve.wait_ge(started, 1)
                dve.wait_ge(emptied[bank("T5", it)], after)
                dve.max(top8[:], logits[:]).then_inc(t_top, 1)
                dve.wait_ge(t_top, b.done(per=5, k=1))
                dve.tensor_scalar(negtop[:], top8[:, 0:1], -1.0, None, ALU.mult).then_inc(t_top, 1)
                dve.max_index(index8[:], top8[:], logits[:]).then_inc(t_top, 1)
                dve.wait_ge(t_top, b.done(per=5, k=3))
                dve.wait_ge(t_pos, b.done(per=7, back=1))
                dve.tensor_copy(route[:], index8[:, 0:1]).then_inc(t_top, 1)
                dve.wait_ge(t_top, b.done(per=5, k=4))
                dve.tensor_scalar(onehot[:], expert_id[:], route[:], None, ALU.is_equal).then_inc(t_top, 1)

            def place_in(it):
                b = it.of("T")
                p, ps = b.parity, MI[bank("T6", it)]
                dve.wait_ge(filled["T6"], b.done())
                dve.tensor_tensor(place[:], ps[0:S, 0:E], carry[1 - p][:], ALU.add).then_inc(t_pos, 1)
                leave(dve.tensor_tensor(carry[p][:], ps[0:S, E:2 * E], carry[1 - p][:], ALU.add), "T6", it)
                dve.wait_ge(t_pos, b.done(per=7, k=1))
                dve.tensor_tensor_reduce(place1[:], place[:], onehot[:], 1.0, 0.0, ALU.mult, ALU.add, pos[:]).then_inc(t_pos, 1)
                dve.wait_ge(t_pos, b.done(per=7, k=2))
                dve.tensor_scalar(keep[:], pos[:], float(CAP), None, ALU.is_lt)
                dve.scalar_tensor_tensor(slot0[:], route[:], float(CAP), pos[:], ALU.mult, ALU.add).then_inc(t_pos, 1)
                dve.wait_ge(t_pos, b.done(per=7, k=3))
                own = own_row[:, bass.ds(b.index(), 1)]
                dve.tensor_tensor(slot1[:], slot0[:], own, ALU.subtract).then_inc(t_pos, 1)
                dve.wait_ge(t_pos, b.done(per=7, k=4))
                dve.scalar_tensor_tensor(slot2[:], slot1[:], keep[:], own, ALU.mult, ALU.add).then_inc(t_pos, 1)
                dve.wait_ge(t_pos, b.done(per=7, k=5))
                dve.wait_ge(*left("T6", it))
                dve.tensor_copy(slot_all[:, bass.ds(b.index(), 1)], slot2[:]).then_inc(t_pos, 1)
                dve.wait_ge(scattered, b.done(per=16, back=1))
                dve.tensor_copy(slot[p][:], slot2[:]).then_inc(t_pos, 1)

            def body(it):
                a, k, b, x, y, t = (it.has(stage) for stage in "AKBXYT")
                if a: A1(it); A2(it)
                if x: cross_max(it, 0); cross_max(it, 1)
                if y: cross_low(it, 0)
                if x: cross_max(it, 2); cross_max(it, 3); cross_max(it, 4); cross_max(it, 5)
                if y: cross_low(it, 1)
                if b: B2(it)
                if t: T3(it)
                if y: cross_low(it, 2)
                if b: gate_sum(it)
                if t: norm2(it)
                if x: cross_max(it, 6); cross_max(it, 7)
                if b: gating(it)
                if y: cross_low(it, 3)
                if k: key_norm(it, 0)
                if x: cross_max(it, 8); cross_max(it, 9); cross_max(it, 10)
                if k: key_low(it, 0)
                if y: cross_low(it, 4)
                if x: cross_max(it, 11); cross_max(it, 12)
                if b: B4(it)
                if a: self_max(it, 0)
                if k: key_norm(it, 1)
                if a: self_max(it, 1)
                if t: route_to(it)
                if y: cross_low(it, 5)
                if b: norm1(it)
                if x: cross_max(it, 13); cross_max(it, 14)
                if k: key_low(it, 1)
                if x: cross_max(it, 15)
                if t: place_in(it)
                if y: cross_low(it, 6)
                if x: shift_rows(it)
                if y: cross_low(it, 7)
                if a: self_low(it, 0); self_low(it, 1)
                if b: queries(it)
                if a: self_low(it, 2)
                if y: Y1(it)
                if k: values(it, [0, 1])
                if a: A6(it)
                if k: values(it, [2])

            iterations(dve, body)

            dve.wait_ge(t_exp, B)
            dve.reciprocal(pmax[:], sum8[:]).then_inc(e_one, 1)
            dve.wait_ge(e_one, 1)
            dve.reciprocal(pinv[:], pmax[:]).then_inc(e_one, 1)
            dve.wait_ge(e_one, 2)
            dve.tensor_tensor(pone[:], pmax[:], pinv[:], ALU.mult).then_inc(e_one, 1)

            def expert(e):
                p = e.parity
                for q in (1, 3):
                    dve.wait_ge(h_mm, e.done(per=4, k=q + 1))
                    if q == 1:
                        dve.wait_ge(y_mm, e.done(per=2, back=1))
                    for m in (2 * q, 2 * q + 1):
                        ins = dve.tensor_scalar(hT[:, m], ST[:, q, m % 2 * CAP:(m % 2 + 1) * CAP], b1[p][:, m:m + 1], 0.0, ALU.add, ALU.max)
                    ins.then_inc(h_dve, 1)
                dve.wait_ge(y_out[p], e.pairs(16, back=1))
                for s in range(2):
                    dve.wait_ge(y_mm, e.done(per=2, k=s + 1))
                    dve.tensor_tensor(Y[p][:, s], MX[0:S, s, 0:D], b2[p][:], ALU.add).then_inc(y_ok, 1)

            expert(Seq(0))
            expert(Seq(1))
            with dve.Fori(0, (E - 2) // 2) as j:
                expert(Seq(2, j))
                expert(Seq(3, j))

            dve.wait_ge(e_one, 3)
            dve.wait_ge(t_keep, B)

            def last_round(r):
                for c in range(4):
                    g, n = 4 * r.parity + c, r.index() * 4 + c
                    dve.wait_ge(g_in[g], r.pairs(16))
                    if c == 0:
                        dve.wait_ge(e_out, r.done(per=4, back=1))
                    x2n = x2_all[:, bass.ds(n, 1), :].rearrange("p a d -> p (a d)")
                    dve.scalar_tensor_tensor(R[c][:], G[g][:], pone[:, bass.ds(n, 1)], x2n, ALU.mult, ALU.add).then_inc(e_sum, 1)
                for c in range(4):
                    dve.wait_ge(e_sum, r.done(per=4, k=c + 1))
                    dve.bn_stats(bn3[:, c], R[c][:]).then_inc(e_bn, 1)
                for c in range(4):
                    after = held(dve, r.done(per=4, k=c + 1))
                    dve.wait_ge(started, 1)
                    dve.wait_ge(e_bn, after)
                    dve.bn_aggr(mv3[:, c], bn3[:, c]).then_inc(e_mv, 1)
                dve.wait_ge(e_rs, r.done(per=2))
                for c in range(4):
                    dve.wait_ge(stored[c], r.done(per=16, back=1))
                    dve.tensor_scalar(O3[c][:], R[c][:], mv3[:, c, 0:1], rs3[:, c:c + 1], ALU.subtract, ALU.mult).then_inc(e_out, 1)

            rounds(dve, last_round)


CONSTS_MADE = 35


def kernel(**inputs):
    import concourse.bacc as bacc
    from concourse.bass_utils import run_bass_kernel_spmd

    w = {k[3:]: np.asarray(v) for k, v in inputs.items() if k.startswith("L0_")}
    x = np.asarray(inputs["x"])
    c = np.asarray(inputs["ctx_1024"])

    def halves(a):
        return a.reshape(2, 128, -1).transpose(1, 0, 2)

    f = np.float32
    rows, cols = np.arange(128)[:, None], np.arange(128)[None, :]
    same_head = (rows // HD == cols // HD).astype(f)
    q = np.arange(S)[:, None]
    self_mask = np.where(np.arange(S)[None, :] >= q, NEG, 0).astype(f)
    latent_mask = np.where(np.arange(NL)[None, :] >= q // 2, NEG, 0).astype(f)
    self_mask[0] = 0
    latent_mask[0:2] = 0
    rows20 = np.zeros((20, S), f)
    mask_s = np.stack([np.concatenate([rows20, self_mask.T]),
                       np.concatenate([rows20, latent_mask.T, np.zeros((S - NL, S), f)])], axis=1)
    eye20 = np.concatenate([np.ones((20, 128), f), np.eye(S, 128, dtype=f)])
    some = np.ones((S, H + LH), f)
    some[0, :H] = 0
    some[0:2, H:] = 0
    arrays = {
        "ident": np.eye(128, dtype=f), "center": np.eye(128, dtype=f) - same_head / HD, "average": same_head / HD,
        "upto": (np.arange(S)[:, None] <= np.arange(S)[None, :]).astype(f), "eye20": eye20, "own20": np.eye(20, dtype=f),
        "mask_q": np.concatenate([self_mask, latent_mask], axis=1),
        "mask_s": mask_s,
        "some_key": some, "expert_id": np.tile(np.arange(E, dtype=f), (S, 1)),
        "own_head": np.concatenate([np.zeros((96, H), f), np.eye(H, dtype=f) / WEIGHT]),
        "own_row": (E * CAP + np.arange(B)[None, :] * S + q).astype(f),
        "parity": np.stack([(np.arange(128) // HD % 2 == e).astype(f) for e in range(2)], axis=1),
        "qkv_w": halves(w["attn_qkv_w"]), "qk_b": w["attn_qkv_b"][:2 * D].reshape(4, 128).T,
        "rq_w": halves(w["attn_rq_w"]), "rq_b": w["attn_rq_b"][:, None], "rkv_w": halves(w["attn_rkv_w"]),
        "rk_b": w["attn_rkv_b"][:64, None], "rout_w": w["attn_rout_w"], "out_w": halves(w["attn_out_w"]),
        "Wq": halves(w["xattn_Wq"]), "Wk": halves(w["xattn_Wk"]), "bq": w["xattn_bq"].reshape(2, 128).T,
        "bk": w["xattn_bk"].reshape(2, 128).T, "WvT": halves(w["xattn_Wv"].T), "WpT": halves(w["xattn_Wp"].T),
        "norm4": np.stack([np.tile(w[f"xattn_{n}"], 8) for n in ("q_gamma", "q_beta", "k_gamma", "k_beta")], axis=1),
        "w_switch": halves(w["ffn_w_switch"]),
        "v_b": w["attn_qkv_b"][2 * D:], "rv_b": w["attn_rkv_b"][64:], "rout_b": w["attn_rout_b"], "out_b": w["attn_out_b"],
        "gl": np.tile(w["attn_gl_w"][:, 0], H), "gr": np.tile(w["attn_gr_w"][:, 0], H), "bv": w["xattn_bv"], "bp": w["xattn_bp"],
        "b_switch": w["ffn_b_switch"],
        "cT": halves(c.reshape(B * M, D).T), "xT": halves(x.reshape(B * S, D).T), "x": x.reshape(B * S, D),
        "w1": w["ffn_w1"], "w2": w["ffn_w2"], "b1": w["ffn_b1"].reshape(E, 8, 128).transpose(0, 2, 1), "b2": w["ffn_b2"],
    }

    def laid_out(specs):
        out = np.zeros((128, columns(specs)), f)
        at = 0
        for name, n, _ in specs:
            a = arrays.pop(name).reshape(n, -1)
            out[:n, at:at + a.shape[1]] = a
            at += a.shape[1]
        return out

    arrays["small"], arrays["weights"] = laid_out(SMALL), laid_out(WEIGHTS)
    arrays["biases"] = np.concatenate([arrays.pop(name) for name, _, _ in ROWS])
    nc = bacc.Bacc("TRN2", target_bir_lowering=False, num_devices=1)
    given, io = {}, {}
    for name, a in arrays.items():
        given[f"in_{name}"] = np.ascontiguousarray(a)
        io[name] = nc.dram_tensor(f"in_{name}", a.shape, F32, kind="ExternalInput").ap()
    io["out"] = nc.dram_tensor("out_x", (B * S, D), F32, kind="ExternalOutput").ap()
    decoder_kernel(nc, io)
    r = run_bass_kernel_spmd(nc, [given], core_ids=[0])
    return r.results[0]["out_x"].reshape(B, S, D)
```
